# Optimizing a Trainium2 kernel written in Bass

```python
import numpy as np
import jax
import jax.numpy as jnp

def _softmax(x, axis=-1):
    return jax.nn.softmax(x, axis=axis)

def _gelu(x):
    return jax.nn.gelu(x, approximate=True)

def _silu(x):
    return jax.nn.silu(x)

def _sigmoid(x):
    return jax.nn.sigmoid(x)

def _layernorm(x, axis=-1, eps=1e-05):
    m = jnp.mean(x, axis=axis, keepdims=True)
    v = jnp.var(x, axis=axis, keepdims=True)
    return (x - m) / jnp.sqrt(v + eps)

def _scatter_add(tgt, idx, src, axis=0):
    return tgt.at[idx].add(src)

def _segment_sum(src, seg, n):
    return jax.ops.segment_sum(src, seg, n)
kernel_name = 'mk_cond_seq_d4_seqx_r8_276ca5'

def setup_inputs(seed: int=0):
    np.random.seed(seed)
    _w = jnp.asarray

    def _rec_inputs():
        import jax
        import jax.numpy as jnp
        _rk = jax.random.key(seed)
        x = -0.0002928 + 1 * jax.random.normal(jax.random.fold_in(_rk, 1), (2, 512, 128), jnp.float32)
        _lenS = 512 - jax.random.randint(jax.random.fold_in(_rk, 7), (2,), 0, max(1, 512 // 4) + 1, jnp.int32)
        _lenS2 = 512 - jax.random.randint(jax.random.fold_in(_rk, 8), (2,), 0, max(1, 512 // 4) + 1, jnp.int32)
        cond_1024 = 0.0061147 + 1.02565 * jax.random.normal(jax.random.fold_in(_rk, 11), (2, 128), jnp.float32)
        return (x, cond_1024)
    x, cond_1024 = _rec_inputs()

    def _L0_cond_setup():
        import jax, jax.numpy as jnp
        import numpy as np
        D = 128
        H = 16
        HD = 4 * D
        B, T = (4, 128)
        EPS = 1e-05

        def _layernorm(x, g, b):
            mu = jnp.mean(x, axis=-1, keepdims=True)
            var = jnp.mean(jnp.square(x - mu), axis=-1, keepdims=True)
            return (x - mu) * jax.lax.rsqrt(var + EPS) * g + b

        def _attention(x, Wqkv, Wproj, bproj):
            b, t, c = x.shape
            hd = c // H
            qkv = (x @ Wqkv).reshape(b, t, 3, H, hd).transpose(2, 0, 3, 1, 4)
            q, k, v = (qkv[0], qkv[1], qkv[2])
            scale = hd ** (-0.5)
            scores = jnp.einsum('bhqd,bhkd->bhqk', q, k) * scale
            causal = jnp.tril(jnp.ones((t, t), bool))
            scores = jnp.where(causal, scores, -jnp.inf)
            attn = jax.nn.softmax(scores, axis=-1)
            out = jnp.einsum('bhqk,bhkd->bhqd', attn, v)
            out = out.transpose(0, 2, 1, 3).reshape(b, t, c)
            return out @ Wproj + bproj
        key = jax.random.key(seed)
        ks = jax.random.split(key, 12)
        s = 0.02
        return {'x': jax.random.normal(ks[0], (B, T, D), jnp.float32), 'condition': jax.random.normal(ks[1], (B, D), jnp.float32), 'Wqkv': jax.random.normal(ks[2], (D, 3 * D), jnp.float32) * s, 'Wproj': jax.random.normal(ks[3], (D, D), jnp.float32) * s, 'bproj': jnp.zeros((D,), jnp.float32), 'W1': jax.random.normal(ks[4], (D, HD), jnp.float32) * s, 'b1': jnp.zeros((HD,), jnp.float32), 'W2': jax.random.normal(ks[5], (HD, D), jnp.float32) * s, 'b2': jnp.zeros((D,), jnp.float32), 'g1': jnp.ones((D,), jnp.float32), 'be1': jnp.zeros((D,), jnp.float32), 'g2': jnp.ones((D,), jnp.float32), 'be2': jnp.zeros((D,), jnp.float32), 'Wada': jax.random.normal(ks[6], (D, 6 * D), jnp.float32) * s, 'bada': jax.random.normal(ks[7], (6 * D,), jnp.float32) * s}
    _L0_cond_all = _L0_cond_setup()
    _L0_cond_in = {k: v for k, v in _L0_cond_all.items() if k in ('Wqkv', 'Wproj', 'bproj', 'W1', 'b1', 'W2', 'b2', 'g1', 'be1', 'g2', 'be2', 'Wada', 'bada')}
    del _L0_cond_all

    def _L1_cond_setup():
        import jax, jax.numpy as jnp
        import numpy as np
        B, S, D = (4, 512, 128)
        H, K = (16, 64)
        DV = 128
        FINAL = H * K
        EPS_ATT = 1e-30
        EPS_LN = 1e-06
        key = jax.random.key(seed)
        ks = jax.random.split(key, 12)
        s = 0.02
        return {'inputs': jax.random.normal(ks[0], (B, S, D), jnp.float32), 'vector': jax.random.normal(ks[1], (B, DV), jnp.float32), 'attention_weights': jax.random.normal(ks[2], (D, H), jnp.float32) * s, 'temperature': jnp.ones((1, 1, H), jnp.float32), 'values': jax.random.normal(ks[3], (D, H, K), jnp.float32) * s, 'operator': jax.random.normal(ks[4], (FINAL, DV), jnp.float32) * s, 'ff1': jax.random.normal(ks[5], (DV + D, D), jnp.float32) * s, 'ff1_bias': jnp.zeros((1, 1, D), jnp.float32), 'ff2': jax.random.normal(ks[6], (D, D), jnp.float32) * s, 'ff2_bias': jnp.zeros((1, 1, D), jnp.float32), 'ln_gamma': jnp.ones((D,), jnp.float32), 'ln_beta': jnp.zeros((D,), jnp.float32)}
    _L1_cond_all = _L1_cond_setup()
    _L1_cond_in = {k: v for k, v in _L1_cond_all.items() if k in ('attention_weights', 'temperature', 'values', 'operator', 'ff1', 'ff1_bias', 'ff2', 'ff2_bias', 'ln_gamma', 'ln_beta')}
    del _L1_cond_all

    def _L2_cond_setup():
        import jax, jax.numpy as jnp
        import numpy as np
        H = 128
        NH = 16
        DH = H // NH
        MLP = 4 * H
        EPS = 1e-05

        def _ln(x):
            m = jnp.mean(x, axis=-1, keepdims=True)
            v = jnp.mean((x - m) ** 2, axis=-1, keepdims=True)
            return (x - m) * jax.lax.rsqrt(v + EPS)

        def _modulate(x, shift, scale):
            return x * (1.0 + scale[:, None, :]) + shift[:, None, :]
        key = jax.random.key(seed)
        ks = jax.random.split(key, 12)
        s = 1.0 / np.sqrt(H)
        inp = {'x': jax.random.normal(ks[0], (8, 128, H), jnp.float32), 'c': jax.random.normal(ks[1], (8, H), jnp.float32), 'Wc': jax.random.normal(ks[2], (H, 6 * H), jnp.float32) * s, 'bc': jnp.zeros((6 * H,), jnp.float32), 'Wq': jax.random.normal(ks[3], (H, H), jnp.float32) * s, 'bq': jnp.zeros((H,), jnp.float32), 'Wk': jax.random.normal(ks[4], (H, H), jnp.float32) * s, 'bk': jnp.zeros((H,), jnp.float32), 'Wv': jax.random.normal(ks[5], (H, H), jnp.float32) * s, 'bv': jnp.zeros((H,), jnp.float32), 'Wo': jax.random.normal(ks[6], (H, H), jnp.float32) * s, 'bo': jnp.zeros((H,), jnp.float32), 'W1': jax.random.normal(ks[7], (H, MLP), jnp.float32) * s, 'b1': jnp.zeros((MLP,), jnp.float32), 'W2': jax.random.normal(ks[8], (MLP, H), jnp.float32) * (1.0 / np.sqrt(MLP)), 'b2': jnp.zeros((H,), jnp.float32)}
        return inp
    _L2_cond_all = _L2_cond_setup()
    _L2_cond_in = {k: v for k, v in _L2_cond_all.items() if k in ('Wc', 'bc', 'Wq', 'bq', 'Wk', 'bk', 'Wv', 'bv', 'Wo', 'bo', 'W1', 'b1', 'W2', 'b2')}
    del _L2_cond_all

    def _L3_cond_setup():
        import jax, jax.numpy as jnp
        import numpy as np
        B, T, DIM = (4, 128, 128)
        COND = 128
        HEADS, DH = (16, 64)
        INNER = HEADS * DH
        MLP = 512
        EPS = 1e-05

        def _layernorm(x):
            mu = jnp.mean(x, axis=-1, keepdims=True)
            var = jnp.mean(jnp.square(x - mu), axis=-1, keepdims=True)
            return (x - mu) * jax.lax.rsqrt(var + EPS)

        def _modulate(x, shift, scale):
            return x * (1.0 + scale) + shift

        def _attention(x, W_qkv, W_out, b_out):
            Bq, Tq, _ = x.shape
            qkv = x @ W_qkv
            q, k, v = jnp.split(qkv, 3, axis=-1)
            q = q.reshape(Bq, Tq, HEADS, DH)
            k = k.reshape(Bq, Tq, HEADS, DH)
            v = v.reshape(Bq, Tq, HEADS, DH)
            scale = DH ** (-0.5)
            attn = jnp.einsum('bqhd,bkhd->bhqk', q, k) * scale
            attn = jax.nn.softmax(attn, axis=-1)
            out = jnp.einsum('bhqk,bkhd->bqhd', attn, v).reshape(Bq, Tq, INNER)
            return out @ W_out + b_out

        def _ff(x, W1, b1, W2, b2):
            return jax.nn.gelu(x @ W1 + b1, approximate=False) @ W2 + b2
        key = jax.random.key(seed)
        ks = jax.random.split(key, 12)
        s = 0.02
        return {'x': jax.random.normal(ks[0], (B, T, DIM), jnp.float32), 'c': jax.random.normal(ks[1], (B, 1, COND), jnp.float32), 'W_mod': jax.random.normal(ks[2], (COND, 6 * DIM), jnp.float32) * s, 'b_mod': jax.random.normal(ks[3], (6 * DIM,), jnp.float32) * s, 'W_qkv': jax.random.normal(ks[4], (DIM, 3 * INNER), jnp.float32) * s, 'W_out': jax.random.normal(ks[5], (INNER, DIM), jnp.float32) * s, 'b_out': jax.random.normal(ks[6], (DIM,), jnp.float32) * s, 'W1': jax.random.normal(ks[7], (DIM, MLP), jnp.float32) * s, 'b1': jax.random.normal(ks[8], (MLP,), jnp.float32) * s, 'W2': jax.random.normal(ks[9], (MLP, DIM), jnp.float32) * s, 'b2': jax.random.normal(ks[10], (DIM,), jnp.float32) * s}
    _L3_cond_all = _L3_cond_setup()
    _L3_cond_in = {k: v for k, v in _L3_cond_all.items() if k in ('W_mod', 'b_mod', 'W_qkv', 'W_out', 'b_out', 'W1', 'b1', 'W2', 'b2')}
    del _L3_cond_all
    return {'x': x, 'cond_1024': cond_1024, 'L0_cond_Wqkv': _L0_cond_in['Wqkv'], 'L0_cond_Wproj': _L0_cond_in['Wproj'], 'L0_cond_bproj': _L0_cond_in['bproj'], 'L0_cond_W1': _L0_cond_in['W1'], 'L0_cond_b1': _L0_cond_in['b1'], 'L0_cond_W2': _L0_cond_in['W2'], 'L0_cond_b2': _L0_cond_in['b2'], 'L0_cond_g1': _L0_cond_in['g1'], 'L0_cond_be1': _L0_cond_in['be1'], 'L0_cond_g2': _L0_cond_in['g2'], 'L0_cond_be2': _L0_cond_in['be2'], 'L0_cond_Wada': _L0_cond_in['Wada'], 'L0_cond_bada': _L0_cond_in['bada'], 'L1_cond_attention_weights': _L1_cond_in['attention_weights'], 'L1_cond_temperature': _L1_cond_in['temperature'], 'L1_cond_values': _L1_cond_in['values'], 'L1_cond_operator': _L1_cond_in['operator'], 'L1_cond_ff1': _L1_cond_in['ff1'], 'L1_cond_ff1_bias': _L1_cond_in['ff1_bias'], 'L1_cond_ff2': _L1_cond_in['ff2'], 'L1_cond_ff2_bias': _L1_cond_in['ff2_bias'], 'L1_cond_ln_gamma': _L1_cond_in['ln_gamma'], 'L1_cond_ln_beta': _L1_cond_in['ln_beta'], 'L2_cond_Wc': _L2_cond_in['Wc'], 'L2_cond_bc': _L2_cond_in['bc'], 'L2_cond_Wq': _L2_cond_in['Wq'], 'L2_cond_bq': _L2_cond_in['bq'], 'L2_cond_Wk': _L2_cond_in['Wk'], 'L2_cond_bk': _L2_cond_in['bk'], 'L2_cond_Wv': _L2_cond_in['Wv'], 'L2_cond_bv': _L2_cond_in['bv'], 'L2_cond_Wo': _L2_cond_in['Wo'], 'L2_cond_bo': _L2_cond_in['bo'], 'L2_cond_W1': _L2_cond_in['W1'], 'L2_cond_b1': _L2_cond_in['b1'], 'L2_cond_W2': _L2_cond_in['W2'], 'L2_cond_b2': _L2_cond_in['b2'], 'L3_cond_W_mod': _L3_cond_in['W_mod'], 'L3_cond_b_mod': _L3_cond_in['b_mod'], 'L3_cond_W_qkv': _L3_cond_in['W_qkv'], 'L3_cond_W_out': _L3_cond_in['W_out'], 'L3_cond_b_out': _L3_cond_in['b_out'], 'L3_cond_W1': _L3_cond_in['W1'], 'L3_cond_b1': _L3_cond_in['b1'], 'L3_cond_W2': _L3_cond_in['W2'], 'L3_cond_b2': _L3_cond_in['b2']}

def reference(x, cond_1024, L0_cond_Wqkv, L0_cond_Wproj, L0_cond_bproj, L0_cond_W1, L0_cond_b1, L0_cond_W2, L0_cond_b2, L0_cond_g1, L0_cond_be1, L0_cond_g2, L0_cond_be2, L0_cond_Wada, L0_cond_bada, L1_cond_attention_weights, L1_cond_temperature, L1_cond_values, L1_cond_operator, L1_cond_ff1, L1_cond_ff1_bias, L1_cond_ff2, L1_cond_ff2_bias, L1_cond_ln_gamma, L1_cond_ln_beta, L2_cond_Wc, L2_cond_bc, L2_cond_Wq, L2_cond_bq, L2_cond_Wk, L2_cond_bk, L2_cond_Wv, L2_cond_bv, L2_cond_Wo, L2_cond_bo, L2_cond_W1, L2_cond_b1, L2_cond_W2, L2_cond_b2, L3_cond_W_mod, L3_cond_b_mod, L3_cond_W_qkv, L3_cond_W_out, L3_cond_b_out, L3_cond_W1, L3_cond_b1, L3_cond_W2, L3_cond_b2):
    import jax
    import jax.numpy as jnp

    def _L0_cond_ref(x, condition, Wqkv, Wproj, bproj, W1, b1, W2, b2, g1, be1, g2, be2, Wada, bada):
        import jax, jax.numpy as jnp
        import numpy as np
        D = 128
        H = 16
        HD = 4 * D
        B, T = (4, 128)
        EPS = 1e-05

        def _layernorm(x, g, b):
            mu = jnp.mean(x, axis=-1, keepdims=True)
            var = jnp.mean(jnp.square(x - mu), axis=-1, keepdims=True)
            return (x - mu) * jax.lax.rsqrt(var + EPS) * g + b

        def _attention(x, Wqkv, Wproj, bproj):
            b, t, c = x.shape
            hd = c // H
            qkv = (x @ Wqkv).reshape(b, t, 3, H, hd).transpose(2, 0, 3, 1, 4)
            q, k, v = (qkv[0], qkv[1], qkv[2])
            scale = hd ** (-0.5)
            scores = jnp.einsum('bhqd,bhkd->bhqk', q, k) * scale
            causal = jnp.tril(jnp.ones((t, t), bool))
            scores = jnp.where(causal, scores, -jnp.inf)
            attn = jax.nn.softmax(scores, axis=-1)
            out = jnp.einsum('bhqk,bhkd->bhqd', attn, v)
            out = out.transpose(0, 2, 1, 3).reshape(b, t, c)
            return out @ Wproj + bproj
        mod = jax.nn.silu(condition) @ Wada + bada
        sh_a, sc_a, gt_a, sh_m, sc_m, gt_m = jnp.split(mod, 6, axis=1)
        xn = _layernorm(x, g1, be1)
        xm = xn * (1.0 + sc_a[:, None, :]) + sh_a[:, None, :]
        x = x + gt_a[:, None, :] * _attention(xm, Wqkv, Wproj, bproj)
        xn = _layernorm(x, g2, be2)
        xm = xn * (1.0 + sc_m[:, None, :]) + sh_m[:, None, :]
        h = jax.nn.gelu(xm @ W1 + b1, approximate=False)
        x = x + gt_m[:, None, :] * (h @ W2 + b2)
        return x

    def _L1_cond_ref(inputs, vector, attention_weights, temperature, values, operator, ff1, ff1_bias, ff2, ff2_bias, ln_gamma, ln_beta):
        import jax, jax.numpy as jnp
        import numpy as np
        B, S, D = (4, 512, 128)
        H, K = (16, 64)
        DV = 128
        FINAL = H * K
        EPS_ATT = 1e-30
        EPS_LN = 1e-06
        att = inputs @ attention_weights
        att = att - jnp.max(att, axis=1, keepdims=True)
        att = jnp.exp(att * temperature)
        v = jnp.einsum('bsi,ihk->bshk', inputs, values)
        cumv = jnp.cumsum(v, axis=1)
        counts = jnp.arange(1, S + 1, dtype=inputs.dtype)[None, :, None]
        denom = att * counts + EPS_ATT
        attn_out = att[..., None] * cumv / denom[..., None]
        attn_out = attn_out.reshape(attn_out.shape[0], S, FINAL)
        op = attn_out @ operator + vector[:, None, :]
        concat = jnp.concatenate([inputs, op], axis=-1)
        res = jax.nn.relu(concat @ ff1 + ff1_bias)
        res = res @ ff2 + ff2_bias + inputs
        mu = jnp.mean(res, axis=-1, keepdims=True)
        var = jnp.mean(jnp.square(res - mu), axis=-1, keepdims=True)
        xhat = (res - mu) * jax.lax.rsqrt(var + EPS_LN)
        return xhat * ln_gamma + ln_beta

    def _L2_cond_ref(x, c, Wc, bc, Wq, bq, Wk, bk, Wv, bv, Wo, bo, W1, b1, W2, b2):
        import jax, jax.numpy as jnp
        import numpy as np
        H = 128
        NH = 16
        DH = H // NH
        MLP = 4 * H
        EPS = 1e-05

        def _ln(x):
            m = jnp.mean(x, axis=-1, keepdims=True)
            v = jnp.mean((x - m) ** 2, axis=-1, keepdims=True)
            return (x - m) * jax.lax.rsqrt(v + EPS)

        def _modulate(x, shift, scale):
            return x * (1.0 + scale[:, None, :]) + shift[:, None, :]
        B, S, _ = x.shape
        c6 = jax.nn.silu(c) @ Wc + bc
        sh_msa, sc_msa, g_msa, sh_mlp, sc_mlp, g_mlp = jnp.split(c6, 6, axis=-1)
        xm = _modulate(_ln(x), sh_msa, sc_msa)
        q = (xm @ Wq + bq).reshape(B, S, NH, DH)
        k = (xm @ Wk + bk).reshape(B, S, NH, DH)
        v = (xm @ Wv + bv).reshape(B, S, NH, DH)
        q = q / DH
        w = jnp.einsum('bqhc,bkhc->bhqk', q, k)
        w = jax.nn.softmax(w, axis=-1)
        y = jnp.einsum('bhqk,bkhc->bqhc', w, v).reshape(B, S, H)
        x = x + g_msa[:, None, :] * (y @ Wo + bo)
        xm2 = _modulate(_ln(x), sh_mlp, sc_mlp)
        h = jax.nn.gelu(xm2 @ W1 + b1, approximate=False)
        x = x + g_mlp[:, None, :] * (h @ W2 + b2)
        return x

    def _L3_cond_ref(x, c, W_mod, b_mod, W_qkv, W_out, b_out, W1, b1, W2, b2):
        import jax, jax.numpy as jnp
        import numpy as np
        B, T, DIM = (4, 128, 128)
        COND = 128
        HEADS, DH = (16, 64)
        INNER = HEADS * DH
        MLP = 512
        EPS = 1e-05

        def _layernorm(x):
            mu = jnp.mean(x, axis=-1, keepdims=True)
            var = jnp.mean(jnp.square(x - mu), axis=-1, keepdims=True)
            return (x - mu) * jax.lax.rsqrt(var + EPS)

        def _modulate(x, shift, scale):
            return x * (1.0 + scale) + shift

        def _attention(x, W_qkv, W_out, b_out):
            Bq, Tq, _ = x.shape
            qkv = x @ W_qkv
            q, k, v = jnp.split(qkv, 3, axis=-1)
            q = q.reshape(Bq, Tq, HEADS, DH)
            k = k.reshape(Bq, Tq, HEADS, DH)
            v = v.reshape(Bq, Tq, HEADS, DH)
            scale = DH ** (-0.5)
            attn = jnp.einsum('bqhd,bkhd->bhqk', q, k) * scale
            attn = jax.nn.softmax(attn, axis=-1)
            out = jnp.einsum('bhqk,bkhd->bqhd', attn, v).reshape(Bq, Tq, INNER)
            return out @ W_out + b_out

        def _ff(x, W1, b1, W2, b2):
            return jax.nn.gelu(x @ W1 + b1, approximate=False) @ W2 + b2
        mod = jax.nn.silu(c) @ W_mod + b_mod
        sh_msa, sc_msa, g_msa, sh_mlp, sc_mlp, g_mlp = jnp.split(mod, 6, axis=-1)
        x = x + g_msa * _attention(_modulate(_layernorm(x), sh_msa, sc_msa), W_qkv, W_out, b_out)
        x = x + g_mlp * _ff(_modulate(_layernorm(x), sh_mlp, sc_mlp), W1, b1, W2, b2)
        return x
    x = _L0_cond_ref(x, cond_1024, L0_cond_Wqkv, L0_cond_Wproj, L0_cond_bproj, L0_cond_W1, L0_cond_b1, L0_cond_W2, L0_cond_b2, L0_cond_g1, L0_cond_be1, L0_cond_g2, L0_cond_be2, L0_cond_Wada, L0_cond_bada)
    x = _L1_cond_ref(x, cond_1024, L1_cond_attention_weights, L1_cond_temperature, L1_cond_values, L1_cond_operator, L1_cond_ff1, L1_cond_ff1_bias, L1_cond_ff2, L1_cond_ff2_bias, L1_cond_ln_gamma, L1_cond_ln_beta)
    x = _L2_cond_ref(x, cond_1024, L2_cond_Wc, L2_cond_bc, L2_cond_Wq, L2_cond_bq, L2_cond_Wk, L2_cond_bk, L2_cond_Wv, L2_cond_bv, L2_cond_Wo, L2_cond_bo, L2_cond_W1, L2_cond_b1, L2_cond_W2, L2_cond_b2)
    x = _L3_cond_ref(x, cond_1024[:, None, :], L3_cond_W_mod, L3_cond_b_mod, L3_cond_W_qkv, L3_cond_W_out, L3_cond_b_out, L3_cond_W1, L3_cond_b1, L3_cond_W2, L3_cond_b2)
    return x

_drawn_inputs = setup_inputs


def setup_inputs(seed=0):
    import zlib

    import numpy as np

    out = dict(_drawn_inputs(seed))
    spreads = {'L0_cond_bproj': (0.0, 0.63),
     'L0_cond_b1': (0.0, 0.8),
     'L0_cond_b2': (0.0, 0.593),
     'L0_cond_g1': (1.0, 0.6),
     'L0_cond_be1': (0.0, 0.8),
     'L0_cond_g2': (1.0, 0.6),
     'L0_cond_be2': (0.0, 0.8),
     'L1_cond_temperature': (1.0, 0.6),
     'L1_cond_ff1_bias': (0.0, 0.453),
     'L1_cond_ff2_bias': (0.0, 0.1),
     'L1_cond_ln_gamma': (1.0, 0.2),
     'L1_cond_ln_beta': (0.0, 0.1),
     'L2_cond_bc': (0.0, 0.1),
     'L2_cond_bq': (0.0, 2.0),
     'L2_cond_bk': (0.0, 2.0),
     'L2_cond_bv': (0.0, 0.1),
     'L2_cond_bo': (0.0, 0.1),
     'L2_cond_b1': (0.0, 0.1),
     'L2_cond_b2': (0.0, 0.1)}
    factors = {'L0_cond_Wqkv': 8.0,
     'L0_cond_Wproj': 8.0,
     'L0_cond_W1': 7.773,
     'L0_cond_W2': 6.957,
     'L0_cond_bada': 8.0,
     'L1_cond_attention_weights': 64.0,
     'L1_cond_values': 8.0,
     'L1_cond_operator': 8.0,
     'L3_cond_W_mod': 5.642,
     'L3_cond_b_mod': 8.0,
     'L3_cond_W_qkv': 7.471,
     'L3_cond_W_out': 6.873,
     'L3_cond_b_out': 34.787,
     'L3_cond_W1': 8.0,
     'L3_cond_b1': 8.0,
     'L3_cond_W2': 8.0,
     'L3_cond_b2': 34.766}
    for name, (base, spread) in spreads.items():
        noise = np.random.default_rng([zlib.crc32(name.encode()), seed]).standard_normal(out[name].shape)
        drawn = base * np.exp(spread * noise) if base else spread * noise
        out[name] = jnp.asarray(drawn.astype(out[name].dtype))
    for name, factor in factors.items():
        out[name] = (out[name] * factor).astype(out[name].dtype)
    return out
```

```python
from contextlib import ExitStack

import concourse.bass as bass
from concourse import mybir

F32 = mybir.dt.float32
F16 = mybir.dt.float16
BF16 = mybir.dt.bfloat16
ALU = mybir.AluOpType
ACT = mybir.ActivationFunctionType
AX_X = mybir.AxisListType.X

P = 128
D = 128
NB = 2
T = 512
KT = T // P
H = 16
DH = D // H
GH = 4
NG = H // GH
NGRP = NB * NG
VW = 32
DW = 64
NC = H * DW // P
MLP = 4 * D // P
NEG = -60000.0
MAXC = 64.0
LN_EPS = (1e-5, 1e-6)

VECTORS = [
    ("cond", NB), ("ada0", 6), ("ada2", 6), ("ada3", 6),
    ("g1", 1), ("g2", 1), ("be1", 1), ("be2", 1), ("bproj", 1), ("L0b1", MLP), ("L0b2", 1),
    ("ff1b", 1), ("ff2b", 1), ("gamma", 1), ("beta", 1),
    ("bq", 1), ("bk", 1), ("bv", 1), ("bo", 1), ("L2b1", MLP), ("L2b2", 1),
    ("bout", 1), ("L3b1", MLP), ("L3b2", 1),
]
COL = {}
for _name, _n in VECTORS:
    COL[_name] = sum(n for _, n in VECTORS[:len(COL)])
NCOL = sum(n for _, n in VECTORS)


def build_program(nc, a, out):
    with ExitStack() as ctx:
        def sb(name, shape, dt=F32):
            return ctx.enter_context(nc.sbuf_tensor(name, shape, dt))

        def sem(name):
            return ctx.enter_context(nc.semaphore(name))

        ident = sb("ident", [P, P])
        ident16 = sb("ident16", [P, P], F16)
        mean_mat = sb("mean_mat", [P, P])
        upper = sb("upper", [P, T])
        mask_q = sb("mask_q", [P, P], F16)
        mask_k = sb("mask_k", [P, P], F16)
        head_of = sb("head_of", [P, GH, VW])
        headmask = sb("headmask", [P, GH])
        num_sel = sb("num_sel", [P, VW])
        den_sel = sb("den_sel", [P, VW])
        pair_sel = sb("pair_sel", [P, NC, 2, DW], BF16)
        counts_i = sb("counts_i", [H, T], mybir.dt.int32)
        counts = sb("counts", [H, T])
        eps = sb("eps", [P, 2])
        zero_col = sb("zero_col", [P, 1])

        w_ada = sb("w_ada", [P, 3, 6 * D])
        w_qkv0 = sb("w_qkv0", [P, 3 * D])
        w_qkv2 = sb("w_qkv2", [P, 3, D])
        w_o0 = sb("w_o0", [P, D])
        w_o2 = sb("w_o2", [P, D])
        w_o3 = sb("w_o3", [P, NC, D])
        w_up = sb("w_up", [P, 3, MLP * P])
        w_down = sb("w_down", [P, 3, MLP, D])
        w_att1 = sb("w_att1", [P, H])
        w_val1 = sb("w_val1", [P, H * DW])
        w_op1 = sb("w_op1", [P, NC, D])
        w_ff1 = sb("w_ff1", [P, 2, D])
        w_ff2 = sb("w_ff2", [P, D])
        w_pair = sb("w_pair", [P, 3, P])

        vec_rows = sb("vec_rows", [NCOL, D])
        cols = sb("cols", [P, NCOL])
        temp = sb("temp", [H, 1])
        silu = sb("silu", [P, 3, NB])
        mods = sb("mods", [P, 18, NB])
        ln_g = sb("ln_g", [P, 3, 2, NB])
        ln_b = sb("ln_b", [P, 3, 2, NB])
        gate_b = sb("gate_b", [P, 3, 2, NB])
        bo2 = sb("bo2", [P, 1])

        xT = sb("xT", [P, NB, T])
        xb = sb("xb", [P, NB, T])
        xm = sb("xm", [P, NB, T])
        xc = sb("xc", [P, NB, T])
        sq = sb("sq", [P, NB, T])
        rs = sb("rs", [P, NB, T])
        hid = sb("hid", [P, NB, MLP, T])
        big = sb("big", [P, 2, GH, KT * T])
        probs = big
        pair_out = big[:, 1, :, :].rearrange("p g (u t) -> p (g u) t", t=T)
        att_out = hid.rearrange("p b m t -> p (b m) t")

        q_hi = sb("q_hi", [P, NB, T], F16)
        q_lo = sb("q_lo", [P, NB, T], F16)
        k_hi = sb("k_hi", [P, NB, T], F16)
        k_lo = sb("k_lo", [P, NB, T], F16)
        k_stack = sb("k_stack", [P, 2, T], F16)
        q_max = sb("q_max", [96, 2, T], F16)
        q_exp = sb("q_exp", [P, 2, T], F16)
        k_head = sb("k_head", [P, 2, GH, T], F16)
        v_all = sb("v_all", [P, NB, NG, KT, GH * DH])
        v_pad = sb("v_pad", [P, 2, KT, GH, VW])
        neg_max = sb("neg_max", [P, 2, KT, VW])
        r_parts = sb("r_parts", [P, NB, T], BF16)
        q_a = sb("q_a", [P, NB, 2, T], F16)
        q_b = sb("q_b", [96, NB, 2, T], F16)
        k_a = sb("k_a", [P, NB, 2, T], F16)
        k_b = sb("k_b", [96, NB, 2, T], F16)
        v_ones = w_ada.rearrange("p l n -> p (l n)")[:, 0:NB * 2 * KT * P].rearrange("p (b h k n) -> p b h k n", b=NB, h=2, k=KT)
        amax = sb("amax", [H, 2 * NB])
        neg_max3 = sb("neg_max3", [P, NB, KT, VW])

        ps = ctx.enter_context(nc.psum_tensor("ps", [P, 8, T], F32))

        scratch = {layer: nc.dram_tensor(f"split{layer}", (2, 3, NB * P, T), F16, kind="Internal").ap()
                   for layer in (0, 2)}

        def col(name, i=0):
            return cols[:, COL[name] + i:COL[name] + i + 1]

        const_pool = sem("const_pool")
        const_made = sem("const_made")
        zeroed = sem("zeroed")
        vec_loaded = sem("vec_loaded")
        w_loaded = sem("w_loaded")
        x_loaded = sem("x_loaded")
        vec_turned = sem("vec_turned")
        cols_ready = sem("cols_ready")
        silu_act = sem("silu_act")
        silu_dve = sem("silu_dve")
        mods_ps = sem("mods_ps")
        mods_done = sem("mods_done")
        x_turned = sem("x_turned")
        xT_ready = sem("xT_ready")
        x_rows = att_out

        row_sources = {
            "cond": a["cond_1024"], "ada0": a["L0_cond_bada"], "ada2": a["L2_cond_bc"], "ada3": a["L3_cond_b_mod"],
            "g1": a["L0_cond_g1"], "g2": a["L0_cond_g2"], "be1": a["L0_cond_be1"], "be2": a["L0_cond_be2"],
            "bproj": a["L0_cond_bproj"], "L0b1": a["L0_cond_b1"], "L0b2": a["L0_cond_b2"],
            "ff1b": a["L1_cond_ff1_bias"], "ff2b": a["L1_cond_ff2_bias"],
            "gamma": a["L1_cond_ln_gamma"], "beta": a["L1_cond_ln_beta"],
            "bq": a["L2_cond_bq"], "bk": a["L2_cond_bk"], "bv": a["L2_cond_bv"], "bo": a["L2_cond_bo"],
            "L2b1": a["L2_cond_b1"], "L2b2": a["L2_cond_b2"],
            "bout": a["L3_cond_b_out"], "L3b1": a["L3_cond_b1"], "L3b2": a["L3_cond_b2"],
        }

        def rows_of(name):
            src = row_sources[name]
            if len(src.shape) == 1:
                return src.rearrange("(n p) -> n p", p=D)
            if len(src.shape) == 3:
                return src.rearrange("a b p -> (a b) p")
            return src

        weights = [
            (w_ada[:, 0, :], a["L0_cond_Wada"]), (w_ada[:, 1, :], a["L2_cond_Wc"]), (w_ada[:, 2, :], a["L3_cond_W_mod"]),
            (w_qkv0[:, :], a["L0_cond_Wqkv"]), (w_o0[:, :], a["L0_cond_Wproj"]),
            (w_up[:, 0, :], a["L0_cond_W1"]), (w_down[:, 0, :, :], a["L0_cond_W2"].rearrange("(m p) n -> p m n", p=P)),
            (w_att1[:, :], a["L1_cond_attention_weights"]),
            (w_val1[:, :], a["L1_cond_values"].rearrange("d h k -> d (h k)")),
            (w_op1[:, :, :], a["L1_cond_operator"].rearrange("(c p) n -> p c n", p=P)),
            (w_ff1[:, :, :], a["L1_cond_ff1"].rearrange("(m p) n -> p m n", p=P)), (w_ff2[:, :], a["L1_cond_ff2"]),
            (w_qkv2[:, 0, :], a["L2_cond_Wq"]), (w_qkv2[:, 1, :], a["L2_cond_Wk"]), (w_qkv2[:, 2, :], a["L2_cond_Wv"]),
            (w_o2[:, :], a["L2_cond_Wo"]),
            (w_up[:, 1, :], a["L2_cond_W1"]), (w_down[:, 1, :, :], a["L2_cond_W2"].rearrange("(m p) n -> p m n", p=P)),
            (w_o3[:, :, :], a["L3_cond_W_out"].rearrange("(c p) n -> p c n", p=P)),
            (w_up[:, 2, :], a["L3_cond_W1"]), (w_down[:, 2, :, :], a["L3_cond_W2"].rearrange("(m p) n -> p m n", p=P)),
        ]
        N_POOL_CONST = 9
        with nc.Block() as block:
            @block.sync
            def _(sp):
                for name, n in VECTORS:
                    sp.dma_start(vec_rows[COL[name]:COL[name] + n, :], rows_of(name)).then_inc(vec_loaded, 16)
                for dst, src in weights[3:]:
                    sp.dma_start(dst, src).then_inc(w_loaded, 16)

            @block.gpsimd
            def _(pool):
                nc.gpsimd.memset(ident[:], 0.0)
                nc.gpsimd.memset(ident16[:], 0.0)
                nc.gpsimd.memset(upper[:], 1.0)
                nc.gpsimd.memset(mask_q[:], 0.0)
                nc.gpsimd.memset(mask_k[:], 0.0)
                nc.gpsimd.memset(head_of[:], 0.0)
                nc.gpsimd.memset(num_sel[:], 0.0)
                nc.gpsimd.memset(den_sel[:], 0.0)
                nc.gpsimd.memset(pair_sel[:], 0.0).then_inc(zeroed, 1)
                pool.wait_ge(zeroed, 1)

                def ones_where(view, pattern, base=0):
                    return nc.gpsimd.affine_select(out=view, in_=view, compare_op=ALU.not_equal, fill=1.0, base=base,
                                                   pattern=pattern, channel_multiplier=1)

                ones_where(ident[:, :], [[-1, P]]).then_inc(const_pool, 1)
                ones_where(ident16[:, :], [[-1, P]]).then_inc(const_pool, 1)
                nc.gpsimd.affine_select(out=upper[:, :], in_=upper[:, :], compare_op=ALU.is_ge, fill=0.0, base=0,
                                        pattern=[[1, T]], channel_multiplier=-1).then_inc(const_pool, 1)
                nc.gpsimd.affine_select(out=mask_q[:, :], in_=mask_q[:, :], compare_op=ALU.is_ge, fill=NEG, base=0,
                                        pattern=[[-1, P]], channel_multiplier=1).then_inc(const_pool, 1)
                nc.gpsimd.affine_select(out=mask_k[:, :], in_=mask_k[:, :], compare_op=ALU.is_ge, fill=NEG, base=0,
                                        pattern=[[1, P]], channel_multiplier=-1).then_inc(const_pool, 1)
                ones_where(head_of[:, :, :].rearrange("p j (q r) -> p j q r", r=DH),
                           [[-DH, GH], [-VW, 4], [-1, DH]]).then_inc(const_pool, 1)
                ones_where(num_sel[:, :].rearrange("p (j r) -> p j r", r=DH), [[-VW, GH], [-1, DH]]).then_inc(const_pool, 1)
                ones_where(den_sel[:, :].rearrange("p (j r) -> p j r", r=DH), [[-VW, GH], [0, DH]],
                           base=-DH).then_inc(const_pool, 1)
                for n in range(3):
                    last = ones_where(pair_sel[:, :, :, :], [[-2, NC], [-1, 2], [0, DW]], base=-32 * n)
                    if n < 2:
                        last.then_inc(zeroed, 1)
                        pool.wait_ge(zeroed, n + 2)
                last.then_inc(const_pool, 1)
                nc.gpsimd.iota(counts_i[:, :], pattern=[[1, T]], base=1, channel_multiplier=0).then_inc(const_pool, 1)

            @block.scalar
            def _(act):
                for b in range(NB):
                    act.dma_start(x_rows[:, 4 * b, :].rearrange("p (k d) -> p k d", d=D),
                                  a["x"][b].rearrange("(k p) d -> p k d", p=P)).then_inc(x_loaded, 16)
                act.dma_start(temp[:, :], a["L1_cond_temperature"].rearrange("a b h -> h (a b)")).then_inc(vec_loaded, 16)
                for dst, src in weights[:3]:
                    act.dma_start(dst, src).then_inc(w_loaded, 16)
                act.wait_ge(cols_ready, 1)
                c = cols[:, COL["cond"]:COL["cond"] + NB]
                nc.scalar.activation(silu[:, 0, :], c, ACT.Exp, scale=-1.0).then_inc(silu_act, 1)

            @block.vector
            def _(dve):
                nc.vector.memset(mean_mat[:], 1.0 / D)
                nc.vector.memset(eps[:, 0:1], LN_EPS[0])
                nc.vector.memset(eps[:, 1:2], LN_EPS[1])
                nc.vector.memset(zero_col[:], 0.0)
                nc.vector.memset(k_stack[96:P, :, :], MAXC)
                nc.vector.memset(v_pad[:, :, :, :, 0:DH], 0.0)
                nc.vector.memset(v_pad[:, :, :, :, DH:DH + 1], 1.0)
                nc.vector.memset(v_pad[:, :, :, :, DH + 1:VW], 0.0)
                nc.vector.memset(neg_max[:], 0.0)
                nc.vector.memset(neg_max3[:], 0.0)
                nc.vector.memset(r_parts[:], 0.0)
                nc.vector.memset(k_b[DW:96, :, :, :], MAXC).then_inc(const_made, 1)
                dve.wait_ge(const_made, 1)
                dve.wait_ge(const_pool, N_POOL_CONST + 1)
                for h in range(2):
                    nc.vector.tensor_scalar(k_b[DW:96, :, h, :], k_b[DW:96, :, h, :], ident[DW:96, DW + h:DW + h + 1], None,
                                            ALU.mult).then_inc(const_made, 1)
                nc.vector.tensor_copy(counts[:, :], counts_i[:, :]).then_inc(const_made, 1)
                nc.vector.reduce_sum(headmask[:, :], head_of[:, :, :], AX_X).then_inc(const_made, 1)
                dve.wait_ge(vec_turned, 1)
                nc.vector.tensor_copy(cols[:, :], ps[:, 0, 0:NCOL]).then_inc(cols_ready, 1)
                dve.wait_ge(silu_act, 1)
                nc.vector.tensor_scalar_add(silu[:, 1, :], silu[:, 0, :], 1.0).then_inc(silu_dve, 1)
                dve.wait_ge(silu_dve, 1)
                nc.vector.reciprocal(silu[:, 2, :], silu[:, 1, :]).then_inc(silu_dve, 1)
                dve.wait_ge(silu_dve, 2)
                dve.wait_ge(cols_ready, 1)
                nc.vector.tensor_tensor(out=silu[:, 0, :], in0=silu[:, 2, :],
                                        in1=cols[:, COL["cond"]:COL["cond"] + NB], op=ALU.mult).then_inc(silu_dve, 1)
                for b in range(NB):
                    dve.wait_ge(x_turned, b + 1)
                    nc.vector.tensor_copy(xT[:, b, :], ps[:, 1 + b, :]).then_inc(xT_ready, 1)
                dve.wait_ge(mods_ps, 1)
                ada = cols[:, COL["ada0"]:COL["ada0"] + 18]
                for b in range(NB):
                    nc.vector.tensor_tensor(out=mods[:, :, b], in0=ps[:, 3, 0:36].rearrange("p (c b) -> p c b", b=NB)[:, :, b],
                                            in1=ada, op=ALU.add).then_inc(mods_done, 1)
                nc.vector.tensor_tensor(out=bo2[:, :], in0=ps[:, 3, 36:37], in1=col("bo"), op=ALU.add).then_inc(mods_done, 1)
                dve.wait_ge(mods_done, 3)
                done = 3
                for layer in range(3):
                    for half in range(2):
                        sh, sc, gt = (mods[:, 6 * layer + 3 * half + i, :] for i in range(3))
                        scale, bias = ln_g[:, layer, half, :], ln_b[:, layer, half, :]
                        nc.vector.tensor_scalar_add(scale, sc, 1.0).then_inc(mods_done, 1)
                        done += 1
                        if layer == 0:
                            dve.wait_ge(mods_done, done)
                            nc.vector.scalar_tensor_tensor(out=bias, in0=scale, scalar=col(f"be{half + 1}"), in1=sh,
                                                           op0=ALU.mult, op1=ALU.add).then_inc(mods_done, 1)
                            done += 1
                            dve.wait_ge(mods_done, done)
                            nc.vector.tensor_scalar(scale, scale, col(f"g{half + 1}"), None, ALU.mult).then_inc(mods_done, 1)
                        else:
                            nc.vector.tensor_copy(bias, sh).then_inc(mods_done, 1)
                        done += 1
                        branch = [["bproj", "L0b2"], [None, "L2b2"], ["bout", "L3b2"]][layer][half]
                        nc.vector.tensor_scalar(gate_b[:, layer, half, :], gt, bo2[:, :] if branch is None else col(branch),
                                                None, ALU.mult).then_inc(mods_done, 1)
                        done += 1

            @block.tensor
            def _(pe):
                pe.wait_ge(const_pool, 1)
                pe.wait_ge(vec_loaded, 16 * (len(VECTORS) + 1))
                nc.tensor.transpose(ps[:, 0, 0:NCOL], vec_rows[:, :], ident[0:NCOL, 0:NCOL]).then_inc(vec_turned, 1)
                pe.wait_ge(x_loaded, 16 * NB)
                for b in range(NB):
                    for k in range(KT):
                        last = nc.tensor.transpose(ps[:, 1 + b, k * P:(k + 1) * P], x_rows[:, 4 * b, k * P:(k + 1) * P],
                                                   ident[:, :])
                    last.then_inc(x_turned, 1)
                pe.wait_ge(w_loaded, 16 * len(weights))
                pe.wait_ge(silu_dve, 3)
                for layer in range(3):
                    for c in range(6):
                        n = 2 * (6 * layer + c)
                        nc.tensor.matmul(ps[:, 3, n:n + 2], w_ada[:, layer, c * D:(c + 1) * D], silu[:, 0, :],
                                         start=True, stop=True)
                nc.tensor.matmul(ps[:, 3, 36:37], w_o2[:, :], col("bv"), start=True, stop=True).then_inc(mods_ps, 1)

        ln_mean, ln_centred, ln_squared = sem("ln_mean"), sem("ln_centred"), sem("ln_squared")
        ln_var, ln_log, ln_rstd = sem("ln_var"), sem("ln_log"), sem("ln_rstd")
        ln_normed, ln_out = sem("ln_normed"), sem("ln_out")

        class LayerNorm:

            def __init__(self, k, eps_i, scale, bias, dst=None):
                self.k, self.eps_i, self.scale, self.bias, self.dst = k, eps_i, scale, bias, xm if dst is None else dst

            def count(self, b):
                return NB * self.k + b + 1

            def pe(self, pe, stream_ready=None):
                for b in range(NB):
                    if stream_ready:
                        pe.wait_ge(stream_ready, b + 1)
                    nc.tensor.matmul(ps[:, 4 * b, :], mean_mat[:, :], xT[:, b, :], start=True, stop=True).then_inc(ln_mean, 1)
                for b in range(NB):
                    pe.wait_ge(ln_squared, self.count(b))
                    nc.tensor.matmul(ps[:, 4 * b + 1, :], mean_mat[:, :], sq[:, b, :], start=True, stop=True).then_inc(ln_var, 1)

            def act(self, act):
                for b in range(NB):
                    act.wait_ge(ln_centred, self.count(b))
                    nc.scalar.activation(sq[:, b, :], xc[:, b, :], ACT.Square).then_inc(ln_squared, 1)
                for b in range(NB):
                    act.wait_ge(ln_var, self.count(b))
                    nc.scalar.activation(rs[:, b, :], ps[:, 4 * b + 1, :], ACT.Ln,
                                         bias=eps[:, self.eps_i:self.eps_i + 1]).then_inc(ln_log, 1)
                    act.wait_ge(ln_log, self.count(b))
                    nc.scalar.activation(rs[:, b, :], rs[:, b, :], ACT.Exp, scale=-0.5).then_inc(ln_rstd, 1)

            def dve(self, dve):
                for b in range(NB):
                    dve.wait_ge(ln_mean, self.count(b))
                    nc.vector.tensor_tensor(out=xc[:, b, :], in0=xT[:, b, :], in1=ps[:, 4 * b, :],
                                            op=ALU.subtract).then_inc(ln_centred, 1)
                for b in range(NB):
                    dve.wait_ge(ln_rstd, self.count(b))
                    nc.vector.tensor_tensor(out=xc[:, b, :], in0=xc[:, b, :], in1=rs[:, b, :],
                                            op=ALU.mult).then_inc(ln_normed, 1)
                    dve.wait_ge(ln_normed, self.count(b))
                    nc.vector.tensor_scalar(self.dst[:, b, :], xc[:, b, :], self.scale(b), self.bias(b), ALU.mult,
                                            ALU.add).then_inc(ln_out, 1)

        def adaptive_norm(k, layer, half):
            return LayerNorm(k, 0, lambda b: ln_g[:, layer, half, b:b + 1], lambda b: ln_b[:, layer, half, b:b + 1])

        class Mlp:

            def __init__(self, layer, norm, b1):
                self.layer, self.norm, self.b1 = layer, norm, b1
                self.up_ps, self.hid_ready = sem(f"up_ps{layer}"), sem(f"hid_ready{layer}")
                self.down_ps, self.biased = sem(f"down_ps{layer}"), sem(f"biased{layer}")
                self.stream = sem(f"stream_mlp{layer}")

            def pe(self, pe):
                for b in range(NB):
                    pe.wait_ge(ln_out, self.norm.count(b))
                    for m in range(MLP):
                        nc.tensor.matmul(ps[:, 4 * b + m, :], w_up[:, self.layer, m * P:(m + 1) * P], xm[:, b, :],
                                         start=True, stop=True).then_inc(self.up_ps, 1)
                for b in range(NB):
                    for m in range(MLP):
                        pe.wait_ge(self.hid_ready, MLP * b + m + 1)
                        last = nc.tensor.matmul(ps[:, 4 * b, :], w_down[:, self.layer, m, :], hid[:, b, m, :],
                                                start=(m == 0), stop=(m == MLP - 1))
                    last.then_inc(self.down_ps, 1)

            def act(self, act):
                for b in range(NB):
                    for m in range(MLP):
                        act.wait_ge(self.up_ps, MLP * b + m + 1)
                        nc.scalar.activation(hid[:, b, m, :], ps[:, 4 * b + m, :], ACT.Gelu,
                                             bias=col(self.b1, m)).then_inc(self.hid_ready, 1)

            def pool(self, pool):
                for b in range(NB):
                    pool.wait_ge(ln_out, self.norm.count(b))
                    nc.gpsimd.tensor_scalar(xb[:, b, :], xT[:, b, :], gate_b[:, self.layer, 1, b:b + 1], None,
                                            ALU.add).then_inc(self.biased, 1)

            def dve(self, dve):
                for b in range(NB):
                    dve.wait_ge(self.down_ps, b + 1)
                    dve.wait_ge(self.biased, b + 1)
                    nc.vector.scalar_tensor_tensor(out=xT[:, b, :], in0=ps[:, 4 * b, :],
                                                   scalar=mods[:, 6 * self.layer + 5, b:b + 1], in1=xb[:, b, :],
                                                   op0=ALU.mult, op1=ALU.add).then_inc(self.stream, 1)

        class Projections:

            def __init__(self, layer, norm, wq, wk, wv, bq, bk):
                self.layer, self.norm, self.w, self.bias = layer, norm, (wq, wk, wv), (bq, bk)
                self.qk_ps, self.hi_ready = sem(f"qk_ps{layer}"), sem(f"hi_ready{layer}")
                self.lo_ready, self.v_ps = sem(f"lo_ready{layer}"), sem(f"v_ps{layer}")
                self.v_ready, self.stored = sem(f"v_ready{layer}"), sem(f"stored{layer}")

            def pe(self, pe):
                for b in range(NB):
                    pe.wait_ge(ln_out, self.norm.count(b))
                    for i in range(2):
                        nc.tensor.matmul(ps[:, 4 * b + i, :], self.w[i], xm[:, b, :], start=True,
                                         stop=True).then_inc(self.qk_ps, 1)
                    for k in range(KT):
                        last = nc.tensor.matmul(ps[:, 4 * b + 2, k * P:(k + 1) * P], xm[:, b, k * P:(k + 1) * P], self.w[2],
                                                start=True, stop=True)
                    last.then_inc(self.v_ps, 1)

            def act(self, act):
                for b in range(NB):
                    for i, hi in enumerate((q_hi, k_hi)):
                        act.wait_ge(self.qk_ps, 2 * b + i + 1)
                        nc.scalar.activation(hi[:, b, :], ps[:, 4 * b + i, :], ACT.Identity,
                                             bias=self.bias[i]).then_inc(self.hi_ready, 1)
                    act.wait_ge(self.v_ps, b + 1)
                    nc.scalar.copy(v_all[:, b, :, :, :].rearrange("p g k n -> p k g n"),
                                   ps[:, 4 * b + 2, :].rearrange("p (k g n) -> p k g n", k=KT, g=NG)).then_inc(self.v_ready, 1)

            def dve(self, dve):
                for b in range(NB):
                    for i, (hi, lo) in enumerate(((q_hi, q_lo), (k_hi, k_lo))):
                        dve.wait_ge(self.hi_ready, 2 * b + i + 1)
                        nc.vector.scalar_tensor_tensor(out=lo[:, b, :], in0=ps[:, 4 * b + i, :], scalar=self.bias[i],
                                                       in1=hi[:, b, :], op0=ALU.add, op1=ALU.subtract).then_inc(self.lo_ready, 1)

            def sp(self, sp):
                for b in range(NB):
                    for i, (parts, sem_) in enumerate((((q_hi, q_lo, q_hi), 0), ((k_hi, k_hi, k_lo), 1))):
                        sp.wait_ge(self.hi_ready, 2 * b + i + 1)
                        sp.wait_ge(self.lo_ready, 2 * b + i + 1)
                        for part, tile in enumerate(parts):
                            sp.dma_start(scratch[self.layer][i, part, b * P:(b + 1) * P, :], tile[:, b, :]).then_inc(self.stored, 16)
                sp.wait_ge(self.stored, 16 * 6 * NB)

        def attention8(layer, causal, scale):
            loaded = [sem(f"km_loaded{layer}_{s}") for s in range(2)]
            q_loaded = [sem(f"qe_loaded{layer}_{s}") for s in range(2)]
            k_made = sem(f"k_made{layer}")
            v_made = sem(f"v_made{layer}")
            max_ps = sem(f"max_ps{layer}")
            max_taken = sem(f"max_taken{layer}")
            max_turned = sem(f"max_turned{layer}")
            max_in = sem(f"max_in{layer}")
            score_ps = sem(f"score_ps{layer}")
            exp_done = sem(f"exp_done{layer}")
            pv_done = sem(f"pv_done{layer}")
            out_free = sem(f"out_free{layer}")

            width = [T - P * k for k in range(KT)] if causal else [T] * KT
            start = [0, T, 2 * T, 2 * T + width[2]]
            seen = [P * (t + 1) for t in range(KT)] if causal else [T] * KT

            def pe_max_head(pe, i, s, j, first=False):
                pe.wait_ge(k_made, i * GH + j + 1)
                for t in range(KT):
                    n = 4 * j + t
                    if not (first and n < 2):
                        pe.wait_ge(max_taken, i * 16 + n - 1)
                    dst = ps[:, n % 2, 0:seen[t]]
                    last = nc.tensor.matmul(dst, q_max[:, s, t * P:(t + 1) * P], k_head[0:96, s, j, 0:seen[t]],
                                            start=True, stop=not causal)
                    if causal:
                        last = nc.tensor.matmul(dst[:, t * P:(t + 1) * P], ident16[:, :], mask_q[:, :], start=False, stop=True)
                    last.then_inc(max_ps, 1)

            def pe_max_turn(pe, i, s, first=False):
                pe.wait_ge(max_taken, i * 16 + 16)
                if not first:
                    pe.wait_ge(max_in, i)
                for t in range(KT):
                    last = nc.tensor.transpose(ps[0:VW, 6, t * P:(t + 1) * P], neg_max[:, s, t, :], ident[:, :])
                last.then_inc(max_turned, 1)

            def pe_scores_head(pe, i, s, uses, j, first=False):
                if j == 0:
                    pe.wait_ge(max_in, i + 1)
                    pe.wait_ge(q_loaded[s], uses * 16)
                for half in range(2):
                    n = 2 * j + half
                    if not (first and n < 2):
                        pe.wait_ge(exp_done, i * 8 + n - 1)
                    for k in (2 * half, 2 * half + 1):
                        off = start[k] - start[2 * half]
                        bank = 2 + 2 * half + off // T
                        dst = ps[:, bank, off % T:off % T + width[k]]
                        last = nc.tensor.matmul(dst, k_head[:, s, j, k * P:(k + 1) * P], q_exp[:, s, T - width[k]:T],
                                                start=True, stop=not causal)
                        if causal:
                            last = nc.tensor.matmul(dst[:, 0:P], ident16[:, :], mask_k[:, :], start=False, stop=True)
                    last.then_inc(score_ps, 1)

            def pe_values(pe, i, s, ks):
                if ks[0] == 0:
                    pe.wait_ge(exp_done, i * 8 + 8)
                    pe.wait_ge(v_made, i + 1)
                    pe.wait_ge(out_free, i + 1)
                for k in ks:
                    for j in range(GH):
                        last = nc.tensor.matmul(ps[VW * j:VW * (j + 1), 7, T - width[k]:T], v_pad[:, s, k, j, :],
                                                probs[:, s, j, start[k]:start[k] + width[k]],
                                                start=(k == 0), stop=(k == KT - 1))
                if ks[-1] == KT - 1:
                    last.then_inc(pv_done, 1)

            def pe_body(pe, i, s, uses, maxima=True, scores=True, values=True, first=False):
                for j in range(GH):
                    if maxima:
                        pe_max_head(pe, i + 1, 1 - s, j)
                    if scores:
                        pe_scores_head(pe, i, s, uses, j, first)
                if values:
                    pe_values(pe, i - 1, 1 - s, (0, 1))
                if maxima:
                    pe_max_turn(pe, i + 1, 1 - s)
                if values:
                    pe_values(pe, i - 1, 1 - s, (2, 3))

            def dve_keys(dve, i, s, uses, j, reuse):
                if j == 0:
                    dve.wait_ge(loaded[s], uses * 32)
                if reuse:
                    dve.wait_ge(score_ps, i * 8 - 16 + 2 * j + 2)
                nc.vector.tensor_scalar(k_head[:, s, j, :], k_stack[:, s, :], headmask[:, j:j + 1], None,
                                        ALU.mult).then_inc(k_made, 1)

            def dve_max_head(dve, i, s, j, reuse):
                if j == 0 and reuse:
                    dve.wait_ge(max_turned, i - 1)
                for t in range(KT):
                    n = 4 * j + t
                    dve.wait_ge(max_ps, i * 16 + n + 1)
                    nc.vector.tensor_reduce(neg_max[:, s, t, DH * j:DH * j + 1], ps[:, n % 2, 0:seen[t]], AX_X, ALU.max,
                                            negate=True).then_inc(max_taken, 1)

            def act_body(act, i, s, scores=True, maxima=True, output=True):
                if output:
                    act.wait_ge(pv_done, i + 1)
                    nc.scalar.copy(att_out[:, i - 2, :], ps[:, 7, :]).then_inc(out_free, 1)
                if scores:
                    if not output:
                        act.wait_ge(pv_done, 2)
                    for j in range(GH):
                        for half in range(2):
                            act.wait_ge(score_ps, i * 8 + 2 * j + half + 1)
                            n = sum(width[2 * half:2 * half + 2])
                            src = ps[:, 2 + 2 * half:4 + 2 * half, :].rearrange("p n t -> p (n t)")[:, 0:n]
                            at = start[2 * half]
                            nc.scalar.activation(probs[:, s, j, at:at + n], src, ACT.Exp, scale=scale).then_inc(exp_done, 1)
                if maxima:
                    act.wait_ge(max_turned, i + 2)
                    nc.scalar.mul(q_exp[96:P, 1 - s, :], ps[0:VW, 6, :], 1.0 / MAXC).then_inc(max_in, 1)

            def sp_load_max(sp, i, s):
                for dst, kind, rows in ((k_stack[0:96, s, :], 1, 96), (q_max[:, s, :], 0, 96)):
                    src = scratch[layer][kind].rearrange("a (i r) t -> i a r t", r=VW)[i]
                    sp.dma_start(dst, src).then_inc(loaded[s], 16)

            def sp_load_exp(sp, i, s):
                src = scratch[layer][0].rearrange("a (i r) t -> i a r t", r=VW)[i]
                sp.dma_start(q_exp[0:96, s, :], src).then_inc(q_loaded[s], 16)

            with nc.Block() as block:
                @block.sync
                def _(sp):
                    def body(i, s, ahead2, ahead1, first=False):
                        if ahead2:
                            sp.wait_ge(k_made, i * GH + GH)
                            sp.wait_ge(max_ps, i * 16 + 16)
                            sp_load_max(sp, i + 2, s)
                        if ahead1:
                            if not first:
                                sp.wait_ge(score_ps, i * 8)
                            sp_load_exp(sp, i + 1, 1 - s)

                    sp_load_max(sp, 0, 0)
                    sp_load_max(sp, 1, 1)
                    sp_load_exp(sp, 0, 0)
                    body(0, 0, True, True, first=True)
                    with sp.Fori(0, 2) as r:
                        for u in range(2):
                            body(r * 2 + (u + 1), (u + 1) % 2, True, True)
                    body(5, 1, True, True)
                    body(6, 0, False, True)

                @block.gpsimd
                def _(pool):
                    def body(i, s, reuse):
                        if reuse:
                            pool.wait_ge(pv_done, i + 1)
                        nc.gpsimd.tensor_copy(
                            v_pad[:, s, :, :, 0:DH],
                            v_all.rearrange("p b g k (j d) -> p (b g) k j d", d=DH)[:, i, :, :, :]).then_inc(v_made, 1)

                    for i in range(2):
                        body(i, i, False)
                    with pool.Fori(0, 3) as r:
                        for u in range(2):
                            body(r * 2 + (u + 2), u, True)

                @block.vector
                def _(dve):
                    def body(i, s, uses_next, reuse_max, reuse_key, keys=True):
                        for j in range(GH):
                            dve_max_head(dve, i, s, j, reuse_max)
                            if keys:
                                dve_keys(dve, i + 1, 1 - s, uses_next, j, reuse_key)

                    for j in range(GH):
                        dve_keys(dve, 0, 0, 1, j, False)
                    body(0, 0, 1, False, False)
                    body(1, 1, 2, False, True)
                    with dve.Fori(0, 2) as r:
                        body(r * 2 + 2, 0, r + 2, True, True)
                        body(r * 2 + 3, 1, r + 3, True, True)
                    body(6, 0, 4, True, True)
                    body(7, 1, None, True, True, keys=False)

                @block.scalar
                def _(act):
                    act_body(act, -1, 1, scores=False, output=False)
                    act_body(act, 0, 0, output=False)
                    act_body(act, 1, 1, output=False)
                    with act.Fori(0, 2) as r:
                        for u in range(2):
                            act_body(act, r * 2 + (u + 2), u)
                    act_body(act, 6, 0)
                    act_body(act, 7, 1, maxima=False)
                    act_body(act, 8, 0, scores=False, maxima=False)
                    act_body(act, 9, 1, scores=False, maxima=False)

                @block.tensor
                def _(pe):
                    pe.sem_inc(pv_done, 2)
                    pe.sem_inc(out_free, 1)
                    for j in range(GH):
                        pe_max_head(pe, 0, 0, j, first=True)
                    pe_max_turn(pe, 0, 0, first=True)
                    pe_body(pe, 0, 0, 1, values=False, first=True)
                    with pe.Fori(0, 3) as r:
                        pe_body(pe, r * 2 + 1, 1, r + 1)
                        pe_body(pe, r * 2 + 2, 0, r + 2)
                    pe_body(pe, 7, 1, 4, maxima=False)
                    pe_body(pe, 8, 0, None, maxima=False, scores=False)

        class Join8:

            def __init__(self, layer, index, wo):
                self.layer, self.index, self.wo = layer, index, wo
                self.picked, self.log, self.inv = sem(f"picked{layer}"), sem(f"den_log{layer}"), sem(f"den_inv{layer}")
                self.normed, self.proj_ps = sem(f"att_normed{layer}"), sem(f"proj_ps{layer}")
                self.biased, self.stream = sem(f"att_biased{layer}"), sem(f"stream_att{layer}")

            def pe(self, pe):
                for b in range(NB):
                    for sel, bank in ((den_sel, 1), (num_sel, 0)):
                        for g in range(NG):
                            last = nc.tensor.matmul(ps[VW * g:VW * (g + 1), 4 * b + bank, :], sel[:, :],
                                                    att_out[:, NG * b + g, :], start=True, stop=True)
                        last.then_inc(self.picked, 1)
                for b in range(NB):
                    pe.wait_ge(self.normed, b + 1)
                    nc.tensor.matmul(ps[:, 4 * b + 2, :], self.wo, xc[:, b, :], start=True, stop=True).then_inc(self.proj_ps, 1)

            def act(self, act):
                for b in range(NB):
                    act.wait_ge(self.picked, 2 * b + 1)
                    nc.scalar.activation(rs[:, b, :], ps[:, 4 * b + 1, :], ACT.Ln).then_inc(self.log, 1)
                    act.wait_ge(self.log, b + 1)
                    nc.scalar.activation(rs[:, b, :], rs[:, b, :], ACT.Exp, scale=-1.0).then_inc(self.inv, 1)

            def pool(self, pool):
                for b in range(NB):
                    nc.gpsimd.tensor_scalar(xb[:, b, :], xT[:, b, :], gate_b[:, self.index, 0, b:b + 1], None,
                                            ALU.add).then_inc(self.biased, 1)

            def dve(self, dve):
                for b in range(NB):
                    dve.wait_ge(self.picked, 2 * b + 2)
                    dve.wait_ge(self.inv, b + 1)
                    nc.vector.tensor_tensor(out=xc[:, b, :], in0=ps[:, 4 * b, :], in1=rs[:, b, :],
                                            op=ALU.mult).then_inc(self.normed, 1)
                for b in range(NB):
                    dve.wait_ge(self.proj_ps, b + 1)
                    dve.wait_ge(self.biased, b + 1)
                    nc.vector.scalar_tensor_tensor(out=xT[:, b, :], in0=ps[:, 4 * b + 2, :],
                                                   scalar=mods[:, 6 * self.index + 2, b:b + 1], in1=xb[:, b, :],
                                                   op0=ALU.mult, op1=ALU.add).then_inc(self.stream, 1)

        norm0a = adaptive_norm(0, 0, 0)
        proj0 = Projections(0, norm0a, w_qkv0[:, 0:D], w_qkv0[:, D:2 * D], w_qkv0[:, 2 * D:3 * D], zero_col[:, :], zero_col[:, :])
        with nc.Block() as block:
            @block.sync
            def _(sp):
                proj0.sp(sp)

            @block.tensor
            def _(pe):
                norm0a.pe(pe)
                proj0.pe(pe)

            @block.scalar
            def _(act):
                norm0a.act(act)
                proj0.act(act)

            @block.vector
            def _(dve):
                norm0a.dve(dve)
                proj0.dve(dve)

        attention8(0, True, DH ** -0.5)

        join0 = Join8(0, 0, w_o0[:, :])
        norm0b = adaptive_norm(1, 0, 1)
        mlp0 = Mlp(0, norm0b, "L0b1")

        x_rows1_ps, x_rows1 = sem("x_rows1_ps"), sem("x_rows1")
        att_ps, att_max, att_bias, att_exp = sem("att_ps"), sem("att_max"), sem("att_bias"), sem("att_exp")
        ratio, cum_ps, cum_ready = sem("ratio"), sem("cum_ps"), sem("cum_ready")
        val_ps, rep_ps, rep_ready, scaled = sem("val_ps"), sem("rep_ps"), sem("rep_ready"), sem("scaled")
        op_ps, op_ready, ff1_ps, ff1_ready = sem("op_ps"), sem("op_ready"), sem("ff1_ps"), sem("ff1_ready")
        ff2_ps, stream1, op_step = sem("ff2_ps"), sem("stream1"), sem("op_step")
        norm1 = LayerNorm(2, 1, lambda b: col("gamma"), lambda b: col("beta"), dst=xT)
        norm2a = adaptive_norm(3, 1, 0)
        proj2 = Projections(2, norm2a, w_qkv2[:, 0, :], w_qkv2[:, 1, :], w_qkv2[:, 2, :], col("bq"), col("bk"))
        RATIO_STEPS = 9

        rows1 = hid[:, :, 0, :]
        cum = hid[:, :, 1, :]
        rep = hid[:, :, 2:4, :]
        att1 = big[0:H, 0, 0, :].rearrange("h (b t) -> h b t", t=T)
        den1 = big[0:H, 0, 1, :].rearrange("h (b t) -> h b t", t=T)
        rat1 = big[0:H, 0, 2, :].rearrange("h (b t) -> h b t", t=T)
        tmp1 = big[0:H, 0, 3, :].rearrange("h (b t) -> h b t", t=T)
        hi1 = q_hi[0:H, :, :].bitcast(BF16)
        scaled1 = big[:, 1, 0:2, :].rearrange("p s (b t) -> p b s t", t=T)
        opT = big[:, 1, 2, :].rearrange("p (b t) -> p b t", t=T)
        resT = big[:, 1, 3, :].rearrange("p (b t) -> p b t", t=T)

        def additive_pe(pe):
            for b in range(NB):
                pe.wait_ge(mlp0.stream, b + 1)
                for k in range(KT):
                    last = nc.tensor.transpose(ps[:, 4 * b + 3, k * P:(k + 1) * P], xT[:, b, k * P:(k + 1) * P], ident[:, :])
                last.then_inc(x_rows1_ps, 1)
                nc.tensor.matmul(ps[0:H, 4 * b + 1, :], w_att1[:, :], xT[:, b, :], start=True, stop=True).then_inc(att_ps, 1)
            for b in range(NB):
                pe.wait_ge(x_rows1, b + 1)
                for k in range(KT):
                    last = nc.tensor.matmul(ps[:, 4 * b + 2, k * P:T], rows1[:, b, k * P:(k + 1) * P], upper[:, 0:T - k * P],
                                            start=(k == 0), stop=(k == KT - 1))
                last.then_inc(cum_ps, 1)
            for c in range(NC):
                for b in range(NB):
                    n = NB * c + b
                    if c == 0:
                        pe.wait_ge(cum_ready, b + 1)
                        pe.wait_ge(ratio, RATIO_STEPS * (b + 1))
                    else:
                        pe.wait_ge(scaled, n - 1)
                        pe.wait_ge(rep_ready, n - 1)
                    nc.tensor.matmul(ps[:, 4 * b, :], w_val1[:, c * P:(c + 1) * P], cum[:, b, :], start=True,
                                     stop=True).then_inc(val_ps, 1)
                    nc.tensor.matmul(ps[:, 4 * b + 1, :], pair_sel[:, c, :, :].rearrange("p a b -> p (a b)"), r_parts[:, b, :],
                                     start=True, stop=True).then_inc(rep_ps, 1)
                if c > 0:
                    for b in range(NB):
                        operator_pe(pe, c - 1, b)
            for b in range(NB):
                operator_pe(pe, NC - 1, b)
            for b in range(NB):
                nc.tensor.matmul(ps[:, 4 * b, :], w_ff1[:, 0, :], xT[:, b, :], start=True, stop=False)
                pe.wait_ge(op_ready, b + 1)
                nc.tensor.matmul(ps[:, 4 * b, :], w_ff1[:, 1, :], opT[:, b, :], start=False, stop=True).then_inc(ff1_ps, 1)
            for b in range(NB):
                pe.wait_ge(ff1_ready, b + 1)
                nc.tensor.matmul(ps[:, 4 * b + 1, :], w_ff2[:, :], resT[:, b, :], start=True, stop=True).then_inc(ff2_ps, 1)

        def operator_pe(pe, c, b):
            pe.wait_ge(scaled, NB * c + b + 1)
            last = nc.tensor.matmul(ps[:, 4 * b + 3, :], w_op1[:, c, :], scaled1[:, b, c % 2, :],
                                    start=(c == 0), stop=(c == NC - 1))
            last.then_inc(op_ps if c == NC - 1 else op_step, 1)

        def additive_act(act):
            for b in range(NB):
                act.wait_ge(x_rows1_ps, b + 1)
                nc.scalar.copy(rows1[:, b, :], ps[:, 4 * b + 3, :]).then_inc(x_rows1, 1)
                act.wait_ge(att_bias, b + 1)
                nc.scalar.activation(att1[:, b, :], ps[0:H, 4 * b + 1, :], ACT.Exp, scale=temp[:, :],
                                     bias=amax[:, 2 + b:3 + b]).then_inc(att_exp, 1)
            for b in range(NB):
                act.wait_ge(cum_ps, b + 1)
                nc.scalar.copy(cum[:, b, :], ps[:, 4 * b + 2, :]).then_inc(cum_ready, 1)
            for c in range(NC):
                for b in range(NB):
                    n = NB * c + b
                    act.wait_ge(rep_ps, n + 1)
                    if c >= 2:
                        act.wait_ge(scaled, n - 3)
                    nc.scalar.copy(rep[:, b, c % 2, :], ps[:, 4 * b + 1, :]).then_inc(rep_ready, 1)
            for b in range(NB):
                act.wait_ge(op_ps, b + 1)
                nc.scalar.activation(opT[:, b, :], ps[:, 4 * b + 3, :], ACT.Identity, bias=col("cond", b)).then_inc(op_ready, 1)
            for b in range(NB):
                act.wait_ge(ff1_ps, b + 1)
                nc.scalar.activation(resT[:, b, :], ps[:, 4 * b, :], ACT.Relu, bias=col("ff1b")).then_inc(ff1_ready, 1)

        def additive_dve(dve):
            for b in range(NB):
                dve.wait_ge(att_ps, b + 1)
                nc.vector.tensor_reduce(amax[:, b:b + 1], ps[0:H, 4 * b + 1, :], AX_X, ALU.max, negate=True).then_inc(att_max, 1)
                dve.wait_ge(att_max, b + 1)
                nc.vector.tensor_tensor(out=amax[:, 2 + b:3 + b], in0=amax[:, b:b + 1], in1=temp[:, :],
                                        op=ALU.mult).then_inc(att_bias, 1)
            for b in range(NB):
                dve.wait_ge(att_exp, b + 1)
                done = RATIO_STEPS * b

                def step(ins, wait=True):
                    nonlocal done
                    done += 1
                    ins.then_inc(ratio, 1)
                    dve.wait_ge(ratio, done)

                step(nc.vector.tensor_tensor(out=den1[:, b, :], in0=att1[:, b, :], in1=counts[:, :], op=ALU.mult))
                step(nc.vector.tensor_scalar_add(den1[:, b, :], den1[:, b, :], 1e-30))
                step(nc.vector.reciprocal(rat1[:, b, :], den1[:, b, :]))
                step(nc.vector.tensor_tensor(out=rat1[:, b, :], in0=rat1[:, b, :], in1=att1[:, b, :], op=ALU.mult))
                step(nc.vector.tensor_copy(r_parts[0:H, b, :], rat1[:, b, :]))
                step(nc.vector.tensor_tensor(out=tmp1[:, b, :], in0=rat1[:, b, :], in1=r_parts[0:H, b, :], op=ALU.subtract))
                step(nc.vector.tensor_copy(hi1[:, b, :], tmp1[:, b, :]))
                step(nc.vector.tensor_copy(r_parts[32:32 + H, b, :], hi1[:, b, :]))
                step(nc.vector.tensor_tensor(out=r_parts[64:64 + H, b, :], in0=tmp1[:, b, :], in1=hi1[:, b, :], op=ALU.subtract))
            for c in range(NC):
                for b in range(NB):
                    n = NB * c + b
                    dve.wait_ge(val_ps, n + 1)
                    dve.wait_ge(rep_ready, n + 1)
                    if c >= 2:
                        dve.wait_ge(op_step, n - 3)
                    nc.vector.tensor_tensor(out=scaled1[:, b, c % 2, :], in0=ps[:, 4 * b, :], in1=rep[:, b, c % 2, :],
                                            op=ALU.mult).then_inc(scaled, 1)
            for b in range(NB):
                dve.wait_ge(ff2_ps, b + 1)
                nc.vector.scalar_tensor_tensor(out=xT[:, b, :], in0=ps[:, 4 * b + 1, :], scalar=col("ff2b"), in1=xT[:, b, :],
                                               op0=ALU.add, op1=ALU.add).then_inc(stream1, 1)

        with nc.Block() as block:
            @block.sync
            def _(sp):
                proj2.sp(sp)

            @block.gpsimd
            def _(pool):
                join0.pool(pool)
                mlp0.pool(pool)

            @block.tensor
            def _(pe):
                join0.pe(pe)
                norm0b.pe(pe, join0.stream)
                mlp0.pe(pe)
                additive_pe(pe)
                norm1.pe(pe, stream1)
                for b in range(NB):
                    pe.wait_ge(ln_out, norm1.count(b))
                norm2a.pe(pe)
                proj2.pe(pe)

            @block.scalar
            def _(act):
                join0.act(act)
                norm0b.act(act)
                mlp0.act(act)
                additive_act(act)
                norm1.act(act)
                norm2a.act(act)
                proj2.act(act)

            @block.vector
            def _(dve):
                join0.dve(dve)
                norm0b.dve(dve)
                mlp0.dve(dve)
                additive_dve(dve)
                norm1.dve(dve)
                norm2a.dve(dve)
                proj2.dve(dve)

        attention8(2, False, 1.0 / DH)

        join2 = Join8(2, 1, w_o2[:, :])
        norm2b = adaptive_norm(4, 1, 1)
        mlp2 = Mlp(1, norm2b, "L2b1")
        norm3a = adaptive_norm(5, 2, 0)
        with nc.Block() as block:
            @block.gpsimd
            def _(pool):
                nc.gpsimd.memset(v_ones[:, :, :, :, DW:P], 1.0)
                join2.pool(pool)
                mlp2.pool(pool)

            @block.tensor
            def _(pe):
                join2.pe(pe)
                norm2b.pe(pe, join2.stream)
                mlp2.pe(pe)
                norm3a.pe(pe, mlp2.stream)

            @block.scalar
            def _(act):
                join2.act(act)
                norm2b.act(act)
                mlp2.act(act)
                norm3a.act(act)

            @block.vector
            def _(dve):
                join2.dve(dve)
                norm2b.dve(dve)
                mlp2.dve(dve)
                norm3a.dve(dve)

        pair_loaded = sem("pair_loaded")
        q3_ps, q3_hi, q3_lo = sem("q3_ps"), sem("q3_hi"), sem("q3_lo")
        k3_ps, k3_hi, k3_lo = sem("k3_ps"), sem("k3_hi"), sem("k3_lo")
        v3_ps, v3_ready = sem("v3_ps"), sem("v3_ready")
        placed = [sem(f"placed{b}") for b in range(NB)]
        max3_ps, max3_taken = sem("max3_ps"), sem("max3_taken")
        max3_turned, max3_in = sem("max3_turned"), sem("max3_in")
        score3_ps, exp3_done = sem("score3_ps"), sem("exp3_done")
        pv3_ps, den3_log, den3_inv, head_out = sem("pv3_ps"), sem("den3_log"), sem("den3_inv"), sem("head_out")
        zero3 = sem("zero3")
        inv3 = sq
        w_qkv3 = a["L3_cond_W_qkv"].rearrange("d (s c n) -> c d s n", s=3, n=P)

        def pe3_project(pe, u, b, c, first=False):
            pe.wait_ge(pair_loaded, c * 16 + 16)
            if not first:
                pe.wait_ge(max3_taken, u * 8)
            nc.tensor.matmul(ps[:, 0, :], w_pair[:, 0, :], xm[:, b, :], start=True, stop=True).then_inc(q3_ps, 1)
            nc.tensor.matmul(ps[:, 1, :], w_pair[:, 1, :], xm[:, b, :], start=True, stop=True).then_inc(k3_ps, 1)

        def pe3_values(pe, u, b):
            pe.wait_ge(q3_lo, u + 1)
            for k in range(KT):
                last = nc.tensor.matmul(ps[:, 0, k * P:(k + 1) * P], xm[:, b, k * P:(k + 1) * P], w_pair[:, 2, :],
                                        start=True, stop=True)
            last.then_inc(v3_ps, 1)

        def pe3_maxima(pe, u, b, uses):
            pe.wait_ge(placed[b], uses * (12 * 16))
            pe.wait_ge(v3_ready, u + 1)
            pe.wait_ge(k3_lo, u + 1)
            for h in range(2):
                for t in range(KT):
                    n = 4 * h + t
                    if n >= 2:
                        pe.wait_ge(max3_taken, u * 8 + n - 1)
                    nc.tensor.matmul(ps[:, n % 2, :], q_a[:, b, h, t * P:(t + 1) * P], k_a[:, b, h, :],
                                     start=True, stop=True).then_inc(max3_ps, 1)

        def pe3_turn(pe, u, b, first=False):
            pe.wait_ge(max3_taken, u * 8 + 8)
            if not first:
                pe.wait_ge(head_out, u * 2 - 1)
            for t in range(KT):
                last = nc.tensor.transpose(ps[0:VW, 2, t * P:(t + 1) * P], neg_max3[:, b, t, :], ident[:, :])
            last.then_inc(max3_turned, 1)

        def pe3_scores(pe, u, b, first=False):
            pe.wait_ge(max3_in, u + 1)
            for h in range(2):
                for half in range(2):
                    n = 2 * h + half
                    if not (first and n < 2):
                        pe.wait_ge(exp3_done, u * 4 + n - 1)
                    for k in (2 * half, 2 * half + 1):
                        dst = ps[:, 4 + k, :]
                        nc.tensor.matmul(dst, k_a[:, b, h, k * P:(k + 1) * P], q_a[:, b, h, :], start=True, stop=False)
                        last = nc.tensor.matmul(dst, k_b[:, b, h, k * P:(k + 1) * P], q_b[:, b, h, :], start=False, stop=True)
                    last.then_inc(score3_ps, 1)

        def pe3_outputs(pe, u, b, h, first=False):
            if not first:
                pe.wait_ge(head_out, u * 2 + h - 1)
            pe.wait_ge(v3_ready, u + 1)
            for k in range(KT):
                if k % 2 == 0:
                    pe.wait_ge(exp3_done, u * 4 + 2 * h + k // 2 + 1)
                last = nc.tensor.matmul(ps[:, 2 + h, :], v_ones[:, b, h, k, :], probs[:, 0, h, k * T:(k + 1) * T],
                                        start=(k == 0), stop=(k == KT - 1))
            last.then_inc(pv3_ps, 1)

        def pe3_body(pe, u, b, c_next, uses_next, first=False, last=False):
            if not last:
                pe3_project(pe, u + 1, 1 - b, c_next)
            pe3_turn(pe, u, b, first)
            if not last:
                pe3_values(pe, u + 1, 1 - b)
            pe.wait_ge(max3_in, u + 1)
            pe3_scores(pe, u, b, first)
            pe3_outputs(pe, u, b, 0, first)
            if not last:
                pe3_maxima(pe, u + 1, 1 - b, uses_next)
            pe3_outputs(pe, u, b, 1, first)

        def act3_split(act, u, b):
            act.wait_ge(q3_ps, u + 1)
            nc.scalar.copy(q_hi[:, b, :], ps[:, 0, :]).then_inc(q3_hi, 1)
            act.wait_ge(k3_ps, u + 1)
            nc.scalar.copy(k_hi[:, b, :], ps[:, 1, :]).then_inc(k3_hi, 1)

        def act3_values(act, u, b, reuse):
            act.wait_ge(v3_ps, u + 1)
            if reuse:
                act.wait_ge(pv3_ps, u * 2 - 2)
            nc.scalar.copy(v_ones[:, b, :, :, 0:DW].rearrange("p h k n -> p k h n"),
                           ps[:, 0, :].rearrange("p (k h n) -> p k h n", k=KT, h=2)).then_inc(v3_ready, 1)

        def act3_max_in(act, u, b):
            act.wait_ge(max3_turned, u + 1)
            act.wait_ge(zero3, 1)
            for h in range(2):
                last = nc.scalar.mul(q_b[DW:96, b, h, :], ps[0:VW, 2, :], 1.0 / MAXC)
            last.then_inc(max3_in, 1)

        def act3_exp(act, u, b, first=False):
            for h in range(2):
                if not first:
                    act.wait_ge(pv3_ps, u * 2 + h - 1)
                for half in range(2):
                    act.wait_ge(score3_ps, u * 4 + 2 * h + half + 1)
                    nc.scalar.activation(probs[:, 0, h, half * 2 * T:(half + 1) * 2 * T],
                                         ps[:, 4 + 2 * half:6 + 2 * half, :].rearrange("p n t -> p (n t)"), ACT.Exp,
                                         scale=DW ** -0.5).then_inc(exp3_done, 1)

        def act3_inverse(act, u, h, first=False):
            act.wait_ge(pv3_ps, u * 2 + h + 1)
            if not first:
                act.wait_ge(head_out, u * 2 + h - 1)
            nc.scalar.activation(inv3[0:DW, h, :], ps[DW:P, 2 + h, :], ACT.Ln).then_inc(den3_log, 1)
            act.wait_ge(den3_log, u * 2 + h + 1)
            nc.scalar.activation(inv3[0:DW, h, :], inv3[0:DW, h, :], ACT.Exp, scale=-1.0).then_inc(den3_inv, 1)

        def act3_body(act, u, b, reuse=True, first=False, last=False):
            if not last:
                act3_split(act, u + 1, 1 - b)
            act3_max_in(act, u, b)
            if not last:
                act3_values(act, u + 1, 1 - b, reuse)
            act3_exp(act, u, b, first)
            for h in range(2):
                act3_inverse(act, u, h, first)

        def dve3_split(dve, u, b):
            dve.wait_ge(q3_hi, u + 1)
            nc.vector.tensor_tensor(out=q_lo[:, b, :], in0=ps[:, 0, :], in1=q_hi[:, b, :], op=ALU.subtract).then_inc(q3_lo, 1)
            dve.wait_ge(k3_hi, u + 1)
            nc.vector.tensor_tensor(out=k_lo[:, b, :], in0=ps[:, 1, :], in1=k_hi[:, b, :], op=ALU.subtract).then_inc(k3_lo, 1)

        def dve3_maxima(dve, u, b, reuse):
            if reuse:
                dve.wait_ge(max3_turned, u - 1)
            for h in range(2):
                for t in range(KT):
                    n = 4 * h + t
                    dve.wait_ge(max3_ps, u * 8 + n + 1)
                    nc.vector.tensor_reduce(neg_max3[:, b, t, h:h + 1], ps[:, n % 2, :], AX_X, ALU.max,
                                            negate=True).then_inc(max3_taken, 1)

        def dve3_divide(dve, u, b, c, h):
            dve.wait_ge(den3_inv, u * 2 + h + 1)
            nc.vector.tensor_tensor(out=pair_out[DW * h:DW * (h + 1), c * NB + b, :], in0=ps[0:DW, 2 + h, :],
                                    in1=inv3[0:DW, h, :], op=ALU.mult).then_inc(head_out, 1)

        def dve3_body(dve, u, b, c, reuse=True, last=False):
            if not last:
                dve3_split(dve, u + 1, 1 - b)
            if not last:
                dve3_divide(dve, u, b, c, 0)
                dve3_maxima(dve, u + 1, 1 - b, reuse)
                dve3_divide(dve, u, b, c, 1)
            else:
                dve3_divide(dve, u, b, c, 0)
                dve3_divide(dve, u, b, c, 1)

        def sp3_place(sp, u, b, reuse):
            sp.wait_ge(q3_lo, u + 1)
            if reuse:
                sp.wait_ge(score3_ps, u * 4 - 4)
            for h in range(2):
                rows = slice(DW * h, DW * (h + 1))
                for dst, src in ((q_a[0:DW, b, h, :], q_hi), (q_a[DW:P, b, h, :], q_lo), (q_b[0:DW, b, h, :], q_hi)):
                    sp.dma_start(dst, src[rows, b, :]).then_inc(placed[b], 16)
            sp.wait_ge(k3_lo, u + 1)
            for h in range(2):
                rows = slice(DW * h, DW * (h + 1))
                for dst, src in ((k_a[0:DW, b, h, :], k_hi), (k_a[DW:P, b, h, :], k_hi), (k_b[0:DW, b, h, :], k_lo)):
                    sp.dma_start(dst, src[rows, b, :]).then_inc(placed[b], 16)

        with nc.Block() as block:
            @block.sync
            def _(sp):
                def load_pair(c, reuse):
                    if reuse:
                        sp.wait_ge(v3_ps, c * 2)
                    sp.dma_start(w_pair[:, :, :], w_qkv3[c]).then_inc(pair_loaded, 16)

                load_pair(0, False)
                sp3_place(sp, 0, 0, False)
                sp3_place(sp, 1, 1, False)
                with sp.Fori(1, NC) as c:
                    load_pair(c, True)
                    sp3_place(sp, c * 2, 0, True)
                    sp3_place(sp, c * 2 + 1, 1, True)

            @block.gpsimd
            def _(pool):
                nc.gpsimd.memset(q_b[DW:96, :, :, :], 0.0).then_inc(zero3, 1)

            @block.tensor
            def _(pe):
                pe3_project(pe, 0, 0, 0, first=True)
                pe3_values(pe, 0, 0)
                pe3_maxima(pe, 0, 0, 1)
                pe3_body(pe, 0, 0, 0, 1, first=True)
                with pe.Fori(1, NC) as c:
                    pe3_body(pe, c * 2 - 1, 1, c, c + 1)
                    pe3_body(pe, c * 2, 0, c, c + 1)
                pe3_body(pe, 2 * NC - 1, 1, None, None, last=True)

            @block.scalar
            def _(act):
                act3_split(act, 0, 0)
                act3_values(act, 0, 0, False)
                act3_body(act, 0, 0, reuse=False, first=True)
                act3_body(act, 1, 1)
                act3_body(act, 2, 0)
                with act.Fori(2, NC) as c:
                    act3_body(act, c * 2 - 1, 1)
                    act3_body(act, c * 2, 0)
                act3_body(act, 2 * NC - 1, 1, last=True)

            @block.vector
            def _(dve):
                dve3_split(dve, 0, 0)
                dve3_maxima(dve, 0, 0, False)
                dve3_body(dve, 0, 0, 0, reuse=False)
                dve3_body(dve, 1, 1, 0)
                dve3_body(dve, 2, 0, 1)
                with dve.Fori(2, NC) as c:
                    dve3_body(dve, c * 2 - 1, 1, c - 1)
                    dve3_body(dve, c * 2, 0, c)
                dve3_body(dve, 2 * NC - 1, 1, NC - 1, last=True)

        out3_ps, biased3, stream3 = sem("out3_ps"), sem("biased3"), sem("stream3")
        norm3b = adaptive_norm(6, 2, 1)
        mlp3 = Mlp(2, norm3b, "L3b1")
        y_ps, y_ready, y_stored = sem("y_ps"), sem("y_ready"), sem("y_stored")
        with nc.Block() as block:
            @block.gpsimd
            def _(pool):
                for b in range(NB):
                    nc.gpsimd.tensor_scalar(xb[:, b, :], xT[:, b, :], gate_b[:, 2, 0, b:b + 1], None, ALU.add).then_inc(biased3, 1)
                mlp3.pool(pool)

            @block.tensor
            def _(pe):
                for b in range(NB):
                    for c in range(NC):
                        last = nc.tensor.matmul(ps[:, 4 * b + 2, :], w_o3[:, c, :], pair_out[:, c * NB + b, :],
                                                start=(c == 0), stop=(c == NC - 1))
                    last.then_inc(out3_ps, 1)
                norm3b.pe(pe, stream3)
                mlp3.pe(pe)
                for b in range(NB):
                    pe.wait_ge(mlp3.stream, b + 1)
                    for k in range(KT):
                        last = nc.tensor.transpose(ps[:, 4 * b + 1, k * P:(k + 1) * P], xT[:, b, k * P:(k + 1) * P], ident[:, :])
                    last.then_inc(y_ps, 1)

            @block.scalar
            def _(act):
                norm3b.act(act)
                mlp3.act(act)
                for b in range(NB):
                    act.wait_ge(y_ps, b + 1)
                    nc.scalar.copy(xc[:, b, :], ps[:, 4 * b + 1, :]).then_inc(y_ready, 1)

            @block.vector
            def _(dve):
                for b in range(NB):
                    dve.wait_ge(out3_ps, b + 1)
                    dve.wait_ge(biased3, b + 1)
                    nc.vector.scalar_tensor_tensor(out=xT[:, b, :], in0=ps[:, 4 * b + 2, :], scalar=mods[:, 14, b:b + 1],
                                                   in1=xb[:, b, :], op0=ALU.mult, op1=ALU.add).then_inc(stream3, 1)
                norm3b.dve(dve)
                mlp3.dve(dve)

            @block.sync
            def _(sp):
                for b in range(NB):
                    sp.wait_ge(y_ready, b + 1)
                    sp.dma_start(out[b].rearrange("(k p) d -> p k d", p=P),
                                 xc[:, b, :].rearrange("p (k d) -> p k d", d=D)).then_inc(y_stored, 16)
                sp.wait_ge(y_stored, 16 * NB)


def kernel(**inputs):
    import numpy as np
    import concourse.bacc as bacc
    from concourse.bass_utils import run_bass_kernel_spmd

    nc = bacc.Bacc("TRN2", target_bir_lowering=False, num_devices=1)
    arrays, aps = {}, {}
    for name, value in inputs.items():
        value = np.ascontiguousarray(value)
        arrays[f"in_{name}"] = value
        aps[name] = nc.dram_tensor(f"in_{name}", value.shape, mybir.dt.from_np(value.dtype), kind="ExternalInput").ap()
    out = nc.dram_tensor("out_0", (NB, T, D), F32, kind="ExternalOutput").ap()
    build_program(nc, aps, out)
    result = run_bass_kernel_spmd(nc, [arrays], core_ids=[0])
    return result.results[0]["out_0"]
```

```python
from contextlib import ExitStack

import concourse.bass as bass
from concourse import mybir

F32 = mybir.dt.float32
F16 = mybir.dt.float16
BF16 = mybir.dt.bfloat16
ALU = mybir.AluOpType
ACT = mybir.ActivationFunctionType
AX_X = mybir.AxisListType.X
LOG_EXP = "natural_log_exp_and_others"

P = 128
D = 128
NB = 2
T = 512
KT = T // P
H = 16
DH = D // H
GH = 4
NG = H // GH
NGRP = NB * NG
VW = 32
DW = 64
NC = H * DW // P
MLP = 4 * D // P
NEG = -60000.0
WSC = 256.0
MAXC = 64.0
LN_EPS = (1e-5, 1e-6)

VECTORS = [
    ("cond", NB), ("ada0", 6), ("ada2", 6), ("ada3", 6),
    ("g1", 1), ("g2", 1), ("be1", 1), ("be2", 1), ("bproj", 1), ("L0b1", MLP), ("L0b2", 1),
    ("ff1b", 1), ("ff2b", 1), ("gamma", 1), ("beta", 1),
    ("bq", 1), ("bk", 1), ("bv", 1), ("bo", 1), ("L2b1", MLP), ("L2b2", 1),
    ("bout", 1), ("L3b1", MLP), ("L3b2", 1),
]
COL = {}
for _name, _n in VECTORS:
    COL[_name] = sum(n for _, n in VECTORS[:len(COL)])
NCOL = sum(n for _, n in VECTORS)


def build_program(nc, a, out):
    with ExitStack() as ctx:
        def sb(name, shape, dt=F32):
            return ctx.enter_context(nc.sbuf_tensor(name, shape, dt))

        def sem(name):
            return ctx.enter_context(nc.semaphore(name))

        ident = sb("ident", [P, P])
        ident16 = sb("ident16", [P, P], F16)
        mean_mat = sb("mean_mat", [P, P])
        upper = sb("upper", [P, T])
        mask_q = sb("mask_q", [P, P], F16)
        mask_k = sb("mask_k", [P, P], F16)
        head_of = sb("head_of", [P, GH, VW])
        headmask = sb("headmask", [P, GH])
        num_sel = sb("num_sel", [P, VW])
        den_sel = sb("den_sel", [P, VW])
        pair_sel = sb("pair_sel", [P, NC, 2, DW], BF16)
        counts_i = sb("counts_i", [H, T], mybir.dt.int32)
        counts = sb("counts", [H, T])
        eps = sb("eps", [P, 2])
        zero_col = sb("zero_col", [P, 1])

        w_ada = sb("w_ada", [P, 3, 6 * D])
        w_qkv0 = sb("w_qkv0", [P, 3 * D])
        w_qkv2 = sb("w_qkv2", [P, 3, D])
        w_o0 = sb("w_o0", [P, D])
        w_o2 = sb("w_o2", [P, D])
        w_o3 = sb("w_o3", [P, NC, D])
        w_up = sb("w_up", [P, 3, MLP * P])
        w_down = sb("w_down", [P, 3, MLP, D])
        w_att1 = sb("w_att1", [P, H])
        w_val1 = sb("w_val1", [P, H * DW])
        w_op1 = sb("w_op1", [P, NC, D])
        w_ff1 = sb("w_ff1", [P, 2, D])
        w_ff2 = sb("w_ff2", [P, D])
        w_pair = sb("w_pair", [P, 3, P])

        vec_rows = sb("vec_rows", [NCOL, D])
        cols = sb("cols", [P, NCOL])
        temp = sb("temp", [H, 1])
        silu = sb("silu", [P, 3, NB])
        mods = sb("mods", [P, 18, NB])
        ln_g = sb("ln_g", [P, 3, 2, NB])
        ln_b = sb("ln_b", [P, 3, 2, NB])
        gate_b = sb("gate_b", [P, 3, 2, NB])
        bo2 = sb("bo2", [P, 1])

        xT = sb("xT", [P, NB, T])
        xb = sb("xb", [P, NB, T])
        xm = sb("xm", [P, NB, T])
        xc = sb("xc", [P, NB, T])
        sq = sb("sq", [P, NB, T])
        rs = sb("rs", [P, NB, T])
        hid = sb("hid", [P, NB, MLP, T])
        big = sb("big", [P, 2, GH, KT * T])
        probs = big
        pair_out = big[:, 1, :, :].rearrange("p g (u t) -> p (g u) t", t=T)
        att_out = hid.rearrange("p b m t -> p (b m) t")

        q_hi = sb("q_hi", [P, NB, T], F16)
        q_lo = sb("q_lo", [P, NB, T], F16)
        k_hi = sb("k_hi", [P, NB, T], F16)
        k_lo = sb("k_lo", [P, NB, T], F16)
        k_stack = sb("k_stack", [P, 2, T], F16)
        q_max = sb("q_max", [96, 2, T], F16)
        q_exp = sb("q_exp", [P, 2, T], F16)
        k_head = sb("k_head", [P, 2, GH, T], F16)
        v_all = sb("v_all", [P, NB, NG, KT, GH * DH])
        v_pad = sb("v_pad", [P, 2, KT, GH, VW])
        neg_max = sb("neg_max", [P, 2, KT, VW])
        r_parts = sb("r_parts", [P, NB, T], BF16)
        q_a = sb("q_a", [P, NB, 2, T], F16)
        q_b = sb("q_b", [96, NB, 2, T], F16)
        k_a = sb("k_a", [P, NB, 2, T], F16)
        k_b = sb("k_b", [96, NB, 2, T], F16)
        late = w_ada.rearrange("p a n -> p (a n)")
        v_pair = late[:, 0:NB * T].rearrange("p (b k n) -> p b k n", b=NB, k=KT)
        ones = sb("ones", [P, DW])
        late16 = late[:, NB * T:].bitcast(F16)
        xm_hi = late16[:, 0:NB * T].rearrange("p (b t) -> p b t", b=NB)
        xm_lo = late16[:, NB * T:2 * NB * T].rearrange("p (b t) -> p b t", b=NB)
        w_hi = late16[:, 2 * NB * T:2 * NB * T + 3 * P].rearrange("p (s n) -> p s n", s=3)
        w_lo = sb("w_lo", [P, 3, P], F16)
        amax = sb("amax", [H, 2 * NB])
        neg_max3 = sb("neg_max3", [P, NB, KT, VW])

        ps = ctx.enter_context(nc.psum_tensor("ps", [P, 8, T], F32))

        scratch = {layer: nc.dram_tensor(f"split{layer}", (2, 3, NB * P, T), F16, kind="Internal").ap()
                   for layer in (0, 2)}

        def col(name, i=0):
            return cols[:, COL[name] + i:COL[name] + i + 1]

        const_pool = sem("const_pool")
        const_made = sem("const_made")
        zeroed = sem("zeroed")
        vec_loaded = sem("vec_loaded")
        w_loaded = sem("w_loaded")
        x_loaded = sem("x_loaded")
        vec_turned = sem("vec_turned")
        cols_ready = sem("cols_ready")
        silu_act = sem("silu_act")
        silu_dve = sem("silu_dve")
        mods_ps = sem("mods_ps")
        mods_done = sem("mods_done")
        x_turned = sem("x_turned")
        xT_ready = sem("xT_ready")
        x_rows = att_out

        row_sources = {
            "cond": a["cond_1024"], "ada0": a["L0_cond_bada"], "ada2": a["L2_cond_bc"], "ada3": a["L3_cond_b_mod"],
            "g1": a["L0_cond_g1"], "g2": a["L0_cond_g2"], "be1": a["L0_cond_be1"], "be2": a["L0_cond_be2"],
            "bproj": a["L0_cond_bproj"], "L0b1": a["L0_cond_b1"], "L0b2": a["L0_cond_b2"],
            "ff1b": a["L1_cond_ff1_bias"], "ff2b": a["L1_cond_ff2_bias"],
            "gamma": a["L1_cond_ln_gamma"], "beta": a["L1_cond_ln_beta"],
            "bq": a["L2_cond_bq"], "bk": a["L2_cond_bk"], "bv": a["L2_cond_bv"], "bo": a["L2_cond_bo"],
            "L2b1": a["L2_cond_b1"], "L2b2": a["L2_cond_b2"],
            "bout": a["L3_cond_b_out"], "L3b1": a["L3_cond_b1"], "L3b2": a["L3_cond_b2"],
        }

        def rows_of(name):
            src = row_sources[name]
            if len(src.shape) == 1:
                return src.rearrange("(n p) -> n p", p=D)
            if len(src.shape) == 3:
                return src.rearrange("a b p -> (a b) p")
            return src

        weights = [
            (w_ada[:, 0, :], a["L0_cond_Wada"]), (w_ada[:, 1, :], a["L2_cond_Wc"]), (w_ada[:, 2, :], a["L3_cond_W_mod"]),
            (w_qkv0[:, :], a["L0_cond_Wqkv"]), (w_o0[:, :], a["L0_cond_Wproj"]),
            (w_up[:, 0, :], a["L0_cond_W1"]), (w_down[:, 0, :, :], a["L0_cond_W2"].rearrange("(m p) n -> p m n", p=P)),
            (w_att1[:, :], a["L1_cond_attention_weights"]),
            (w_val1[:, :], a["L1_cond_values"].rearrange("d h k -> d (h k)")),
            (w_op1[:, :, :], a["L1_cond_operator"].rearrange("(c p) n -> p c n", p=P)),
            (w_ff1[:, :, :], a["L1_cond_ff1"].rearrange("(m p) n -> p m n", p=P)), (w_ff2[:, :], a["L1_cond_ff2"]),
            (w_qkv2[:, 0, :], a["L2_cond_Wq"]), (w_qkv2[:, 1, :], a["L2_cond_Wk"]), (w_qkv2[:, 2, :], a["L2_cond_Wv"]),
            (w_o2[:, :], a["L2_cond_Wo"]),
            (w_up[:, 1, :], a["L2_cond_W1"]), (w_down[:, 1, :, :], a["L2_cond_W2"].rearrange("(m p) n -> p m n", p=P)),
            (w_o3[:, :, :], a["L3_cond_W_out"].rearrange("(c p) n -> p c n", p=P)),
            (w_up[:, 2, :], a["L3_cond_W1"]), (w_down[:, 2, :, :], a["L3_cond_W2"].rearrange("(m p) n -> p m n", p=P)),
        ]
        N_POOL_CONST = 9
        with nc.Block() as block:
            @block.sync
            def _(sp):
                for name, n in VECTORS:
                    sp.dma_start(vec_rows[COL[name]:COL[name] + n, :], rows_of(name)).then_inc(vec_loaded, 16)
                for dst, src in weights[3:]:
                    sp.dma_start(dst, src).then_inc(w_loaded, 16)

            @block.gpsimd
            def _(pool):
                nc.gpsimd.memset(ident[:], 0.0)
                nc.gpsimd.memset(ident16[:], 0.0)
                nc.gpsimd.memset(upper[:], 1.0)
                nc.gpsimd.memset(mask_q[:], 0.0)
                nc.gpsimd.memset(mask_k[:], 0.0)
                nc.gpsimd.memset(head_of[:], 0.0)
                nc.gpsimd.memset(num_sel[:], 0.0)
                nc.gpsimd.memset(den_sel[:], 0.0)
                nc.gpsimd.memset(pair_sel[:], 0.0).then_inc(zeroed, 1)
                pool.wait_ge(zeroed, 1)

                def ones_where(view, pattern, base=0):
                    return nc.gpsimd.affine_select(out=view, in_=view, compare_op=ALU.not_equal, fill=1.0, base=base,
                                                   pattern=pattern, channel_multiplier=1)

                ones_where(ident[:, :], [[-1, P]]).then_inc(const_pool, 1)
                ones_where(ident16[:, :], [[-1, P]]).then_inc(const_pool, 1)
                nc.gpsimd.affine_select(out=upper[:, :], in_=upper[:, :], compare_op=ALU.is_ge, fill=0.0, base=0,
                                        pattern=[[1, T]], channel_multiplier=-1).then_inc(const_pool, 1)
                nc.gpsimd.affine_select(out=mask_q[:, :], in_=mask_q[:, :], compare_op=ALU.is_ge, fill=NEG, base=0,
                                        pattern=[[-1, P]], channel_multiplier=1).then_inc(const_pool, 1)
                nc.gpsimd.affine_select(out=mask_k[:, :], in_=mask_k[:, :], compare_op=ALU.is_ge, fill=NEG, base=0,
                                        pattern=[[1, P]], channel_multiplier=-1).then_inc(const_pool, 1)
                ones_where(head_of[:, :, :].rearrange("p j (q r) -> p j q r", r=DH),
                           [[-DH, GH], [-VW, 4], [-1, DH]]).then_inc(const_pool, 1)
                ones_where(num_sel[:, :].rearrange("p (j r) -> p j r", r=DH), [[-VW, GH], [-1, DH]]).then_inc(const_pool, 1)
                ones_where(den_sel[:, :].rearrange("p (j r) -> p j r", r=DH), [[-VW, GH], [0, DH]],
                           base=-DH).then_inc(const_pool, 1)
                for n in range(3):
                    last = ones_where(pair_sel[:, :, :, :], [[-2, NC], [-1, 2], [0, DW]], base=-32 * n)
                    if n < 2:
                        last.then_inc(zeroed, 1)
                        pool.wait_ge(zeroed, n + 2)
                last.then_inc(const_pool, 1)
                nc.gpsimd.iota(counts_i[:, :], pattern=[[1, T]], base=1, channel_multiplier=0).then_inc(const_pool, 1)

            @block.scalar
            def _(act):
                act.preload_act_table_set(LOG_EXP)
                for b in range(NB):
                    act.dma_start(x_rows[:, 4 * b, :].rearrange("p (k d) -> p k d", d=D),
                                  a["x"][b].rearrange("(k p) d -> p k d", p=P)).then_inc(x_loaded, 16)
                act.dma_start(temp[:, :], a["L1_cond_temperature"].rearrange("a b h -> h (a b)")).then_inc(vec_loaded, 16)
                for dst, src in weights[:3]:
                    act.dma_start(dst, src).then_inc(w_loaded, 16)
                act.wait_ge(cols_ready, 1)
                c = cols[:, COL["cond"]:COL["cond"] + NB]
                nc.scalar.activation(silu[:, 0, :], c, ACT.Exp, scale=-1.0).then_inc(silu_act, 1)

            @block.vector
            def _(dve):
                nc.vector.memset(mean_mat[:], 1.0 / D)
                nc.vector.memset(ones[:], 1.0)
                nc.vector.memset(eps[:, 0:1], LN_EPS[0])
                nc.vector.memset(eps[:, 1:2], LN_EPS[1])
                nc.vector.memset(zero_col[:], 0.0)
                nc.vector.memset(k_stack[96:P, :, :], MAXC)
                nc.vector.memset(v_pad[:, :, :, :, 0:DH], 0.0)
                nc.vector.memset(v_pad[:, :, :, :, DH:DH + 1], 1.0)
                nc.vector.memset(v_pad[:, :, :, :, DH + 1:VW], 0.0)
                nc.vector.memset(neg_max[:], 0.0)
                nc.vector.memset(neg_max3[:], 0.0)
                nc.vector.memset(r_parts[:], 0.0)
                nc.vector.memset(k_b[DW:96, :, :, :], MAXC).then_inc(const_made, 1)
                dve.wait_ge(const_made, 1)
                dve.wait_ge(const_pool, N_POOL_CONST + 1)
                for h in range(2):
                    nc.vector.tensor_scalar(k_b[DW:96, :, h, :], k_b[DW:96, :, h, :], ident[DW:96, DW + h:DW + h + 1], None,
                                            ALU.mult).then_inc(const_made, 1)
                nc.vector.tensor_copy(counts[:, :], counts_i[:, :]).then_inc(const_made, 1)
                nc.vector.reduce_sum(headmask[:, :], head_of[:, :, :], AX_X).then_inc(const_made, 1)
                dve.wait_ge(vec_turned, 1)
                nc.vector.tensor_copy(cols[:, :], ps[:, 0, 0:NCOL]).then_inc(cols_ready, 1)
                dve.wait_ge(silu_act, 1)
                nc.vector.tensor_scalar_add(silu[:, 1, :], silu[:, 0, :], 1.0).then_inc(silu_dve, 1)
                dve.wait_ge(silu_dve, 1)
                nc.vector.reciprocal(silu[:, 2, :], silu[:, 1, :]).then_inc(silu_dve, 1)
                dve.wait_ge(silu_dve, 2)
                dve.wait_ge(cols_ready, 1)
                nc.vector.tensor_tensor(out=silu[:, 0, :], in0=silu[:, 2, :],
                                        in1=cols[:, COL["cond"]:COL["cond"] + NB], op=ALU.mult).then_inc(silu_dve, 1)
                for b in range(NB):
                    dve.wait_ge(x_turned, b + 1)
                    nc.vector.tensor_copy(xT[:, b, :], ps[:, 1 + b, :]).then_inc(xT_ready, 1)
                dve.wait_ge(mods_ps, 1)
                ada = cols[:, COL["ada0"]:COL["ada0"] + 18]
                for b in range(NB):
                    nc.vector.tensor_tensor(out=mods[:, :, b], in0=ps[:, 3, 0:36].rearrange("p (c b) -> p c b", b=NB)[:, :, b],
                                            in1=ada, op=ALU.add).then_inc(mods_done, 1)
                nc.vector.tensor_tensor(out=bo2[:, :], in0=ps[:, 3, 36:37], in1=col("bo"), op=ALU.add).then_inc(mods_done, 1)
                dve.wait_ge(mods_done, 3)
                done = 3
                for layer in range(3):
                    for half in range(2):
                        sh, sc, gt = (mods[:, 6 * layer + 3 * half + i, :] for i in range(3))
                        scale, bias = ln_g[:, layer, half, :], ln_b[:, layer, half, :]
                        nc.vector.tensor_scalar_add(scale, sc, 1.0).then_inc(mods_done, 1)
                        done += 1
                        if layer == 0:
                            dve.wait_ge(mods_done, done)
                            nc.vector.scalar_tensor_tensor(out=bias, in0=scale, scalar=col(f"be{half + 1}"), in1=sh,
                                                           op0=ALU.mult, op1=ALU.add).then_inc(mods_done, 1)
                            done += 1
                            dve.wait_ge(mods_done, done)
                            nc.vector.tensor_scalar(scale, scale, col(f"g{half + 1}"), None, ALU.mult).then_inc(mods_done, 1)
                        else:
                            nc.vector.tensor_copy(bias, sh).then_inc(mods_done, 1)
                        done += 1
                        branch = [["bproj", "L0b2"], [None, "L2b2"], ["bout", "L3b2"]][layer][half]
                        nc.vector.tensor_scalar(gate_b[:, layer, half, :], gt, bo2[:, :] if branch is None else col(branch),
                                                None, ALU.mult).then_inc(mods_done, 1)
                        done += 1

            @block.tensor
            def _(pe):
                pe.wait_ge(const_pool, 1)
                pe.wait_ge(vec_loaded, 16 * (len(VECTORS) + 1))
                nc.tensor.transpose(ps[:, 0, 0:NCOL], vec_rows[:, :], ident[0:NCOL, 0:NCOL]).then_inc(vec_turned, 1)
                pe.wait_ge(x_loaded, 16 * NB)
                for b in range(NB):
                    for k in range(KT):
                        last = nc.tensor.transpose(ps[:, 1 + b, k * P:(k + 1) * P], x_rows[:, 4 * b, k * P:(k + 1) * P],
                                                   ident[:, :])
                    last.then_inc(x_turned, 1)
                pe.wait_ge(w_loaded, 16 * len(weights))
                pe.wait_ge(silu_dve, 3)
                for layer in range(3):
                    for c in range(6):
                        n = 2 * (6 * layer + c)
                        nc.tensor.matmul(ps[:, 3, n:n + 2], w_ada[:, layer, c * D:(c + 1) * D], silu[:, 0, :],
                                         start=True, stop=True)
                nc.tensor.matmul(ps[:, 3, 36:37], w_o2[:, :], col("bv"), start=True, stop=True).then_inc(mods_ps, 1)

        ln_mean, ln_centred, ln_squared = sem("ln_mean"), sem("ln_centred"), sem("ln_squared")
        ln_var, ln_log, ln_rstd = sem("ln_var"), sem("ln_log"), sem("ln_rstd")
        ln_normed, ln_out = sem("ln_normed"), sem("ln_out")

        class LayerNorm:

            def __init__(self, k, eps_i, scale, bias, dst=None):
                self.k, self.eps_i, self.scale, self.bias, self.dst = k, eps_i, scale, bias, xm if dst is None else dst

            def count(self, b):
                return NB * self.k + b + 1

            def pe(self, pe, stream_ready=None):
                for b in range(NB):
                    if stream_ready:
                        pe.wait_ge(stream_ready, b + 1)
                    nc.tensor.matmul(ps[:, 4 * b, :], mean_mat[:, :], xT[:, b, :], start=True, stop=True).then_inc(ln_mean, 1)
                for b in range(NB):
                    pe.wait_ge(ln_squared, self.count(b))
                    nc.tensor.matmul(ps[:, 4 * b + 1, :], mean_mat[:, :], sq[:, b, :], start=True, stop=True).then_inc(ln_var, 1)

            def act(self, act):
                for b in range(NB):
                    act.wait_ge(ln_centred, self.count(b))
                    nc.scalar.activation(sq[:, b, :], xc[:, b, :], ACT.Square).then_inc(ln_squared, 1)
                for b in range(NB):
                    act.wait_ge(ln_var, self.count(b))
                    nc.scalar.activation(rs[:, b, :], ps[:, 4 * b + 1, :], ACT.Ln,
                                         bias=eps[:, self.eps_i:self.eps_i + 1]).then_inc(ln_log, 1)
                    act.wait_ge(ln_log, self.count(b))
                    nc.scalar.activation(rs[:, b, :], rs[:, b, :], ACT.Exp, scale=-0.5).then_inc(ln_rstd, 1)

            def dve(self, dve):
                for b in range(NB):
                    dve.wait_ge(ln_mean, self.count(b))
                    nc.vector.tensor_tensor(out=xc[:, b, :], in0=xT[:, b, :], in1=ps[:, 4 * b, :],
                                            op=ALU.subtract).then_inc(ln_centred, 1)
                for b in range(NB):
                    dve.wait_ge(ln_rstd, self.count(b))
                    nc.vector.tensor_tensor(out=xc[:, b, :], in0=xc[:, b, :], in1=rs[:, b, :],
                                            op=ALU.mult).then_inc(ln_normed, 1)
                    dve.wait_ge(ln_normed, self.count(b))
                    nc.vector.tensor_scalar(self.dst[:, b, :], xc[:, b, :], self.scale(b), self.bias(b), ALU.mult,
                                            ALU.add).then_inc(ln_out, 1)

        def adaptive_norm(k, layer, half):
            return LayerNorm(k, 0, lambda b: ln_g[:, layer, half, b:b + 1], lambda b: ln_b[:, layer, half, b:b + 1])

        class Mlp:

            def __init__(self, layer, norm, b1):
                self.layer, self.norm, self.b1 = layer, norm, b1
                self.up_ps, self.hid_ready = sem(f"up_ps{layer}"), sem(f"hid_ready{layer}")
                self.down_ps, self.biased = sem(f"down_ps{layer}"), sem(f"biased{layer}")
                self.stream = sem(f"stream_mlp{layer}")

            def pe(self, pe):
                for b in range(NB):
                    pe.wait_ge(ln_out, self.norm.count(b))
                    for m in range(MLP):
                        nc.tensor.matmul(ps[:, 4 * b + m, :], w_up[:, self.layer, m * P:(m + 1) * P], xm[:, b, :],
                                         start=True, stop=True).then_inc(self.up_ps, 1)
                for b in range(NB):
                    for m in range(MLP):
                        pe.wait_ge(self.hid_ready, MLP * b + m + 1)
                        last = nc.tensor.matmul(ps[:, 4 * b, :], w_down[:, self.layer, m, :], hid[:, b, m, :],
                                                start=(m == 0), stop=(m == MLP - 1))
                    last.then_inc(self.down_ps, 1)

            def act(self, act):
                for b in range(NB):
                    for m in range(MLP):
                        act.wait_ge(self.up_ps, MLP * b + m + 1)
                        nc.scalar.activation(hid[:, b, m, :], ps[:, 4 * b + m, :], ACT.Gelu,
                                             bias=col(self.b1, m)).then_inc(self.hid_ready, 1)
                act.preload_act_table_set(LOG_EXP)

            def pool(self, pool):
                for b in range(NB):
                    pool.wait_ge(ln_out, self.norm.count(b))
                    nc.gpsimd.tensor_scalar(xb[:, b, :], xT[:, b, :], gate_b[:, self.layer, 1, b:b + 1], None,
                                            ALU.add).then_inc(self.biased, 1)

            def dve(self, dve):
                for b in range(NB):
                    dve.wait_ge(self.down_ps, b + 1)
                    dve.wait_ge(self.biased, b + 1)
                    nc.vector.scalar_tensor_tensor(out=xT[:, b, :], in0=ps[:, 4 * b, :],
                                                   scalar=mods[:, 6 * self.layer + 5, b:b + 1], in1=xb[:, b, :],
                                                   op0=ALU.mult, op1=ALU.add).then_inc(self.stream, 1)

        class Projections:

            def __init__(self, layer, norm, wq, wk, wv, bq, bk):
                self.layer, self.norm, self.w, self.bias = layer, norm, (wq, wk, wv), (bq, bk)
                self.qk_ps, self.hi_ready = sem(f"qk_ps{layer}"), sem(f"hi_ready{layer}")
                self.lo_ready, self.v_ps = sem(f"lo_ready{layer}"), sem(f"v_ps{layer}")
                self.v_ready, self.stored = sem(f"v_ready{layer}"), sem(f"stored{layer}")

            def pe(self, pe):
                for b in range(NB):
                    pe.wait_ge(ln_out, self.norm.count(b))
                    for i in range(2):
                        nc.tensor.matmul(ps[:, 4 * b + i, :], self.w[i], xm[:, b, :], start=True,
                                         stop=True).then_inc(self.qk_ps, 1)
                    for k in range(KT):
                        last = nc.tensor.matmul(ps[:, 4 * b + 2, k * P:(k + 1) * P], xm[:, b, k * P:(k + 1) * P], self.w[2],
                                                start=True, stop=True)
                    last.then_inc(self.v_ps, 1)

            def act(self, act):
                for b in range(NB):
                    for i, hi in enumerate((q_hi, k_hi)):
                        act.wait_ge(self.qk_ps, 2 * b + i + 1)
                        nc.scalar.activation(hi[:, b, :], ps[:, 4 * b + i, :], ACT.Identity,
                                             bias=self.bias[i]).then_inc(self.hi_ready, 1)
                    act.wait_ge(self.v_ps, b + 1)
                    nc.scalar.copy(v_all[:, b, :, :, :].rearrange("p g k n -> p k g n"),
                                   ps[:, 4 * b + 2, :].rearrange("p (k g n) -> p k g n", k=KT, g=NG)).then_inc(self.v_ready, 1)

            def dve(self, dve):
                for b in range(NB):
                    for i, (hi, lo) in enumerate(((q_hi, q_lo), (k_hi, k_lo))):
                        dve.wait_ge(self.hi_ready, 2 * b + i + 1)
                        nc.vector.scalar_tensor_tensor(out=lo[:, b, :], in0=ps[:, 4 * b + i, :], scalar=self.bias[i],
                                                       in1=hi[:, b, :], op0=ALU.add, op1=ALU.subtract).then_inc(self.lo_ready, 1)

            def sp(self, sp):
                for b in range(NB):
                    for i, (parts, sem_) in enumerate((((q_hi, q_lo, q_hi), 0), ((k_hi, k_hi, k_lo), 1))):
                        sp.wait_ge(self.hi_ready, 2 * b + i + 1)
                        sp.wait_ge(self.lo_ready, 2 * b + i + 1)
                        for part, tile in enumerate(parts):
                            sp.dma_start(scratch[self.layer][i, part, b * P:(b + 1) * P, :], tile[:, b, :]).then_inc(self.stored, 16)
                sp.wait_ge(self.stored, 16 * 6 * NB)

        def attention8(layer, causal, scale):
            loaded = [sem(f"km_loaded{layer}_{s}") for s in range(2)]
            q_loaded = [sem(f"qe_loaded{layer}_{s}") for s in range(2)]
            k_made = sem(f"k_made{layer}")
            v_made = sem(f"v_made{layer}")
            max_ps = sem(f"max_ps{layer}")
            max_taken = sem(f"max_taken{layer}")
            max_turned = sem(f"max_turned{layer}")
            max_in = sem(f"max_in{layer}")
            score_ps = sem(f"score_ps{layer}")
            exp_done = sem(f"exp_done{layer}")
            pv_done = sem(f"pv_done{layer}")
            out_free = sem(f"out_free{layer}")

            width = [T - P * k for k in range(KT)] if causal else [T] * KT
            start = [0, T, 2 * T, 2 * T + width[2]]
            seen = [P * (t + 1) for t in range(KT)] if causal else [T] * KT

            def pe_maxima(pe, i, s, j, t, first=False):
                if t == 0:
                    pe.wait_ge(k_made, i * GH + j + 1)
                n = 4 * j + t
                if not (first and n < 2):
                    pe.wait_ge(max_taken, i * 16 + n - 1)
                dst = ps[:, n % 2, 0:seen[t]]
                last = nc.tensor.matmul(dst, q_max[:, s, t * P:(t + 1) * P], k_head[0:96, s, j, 0:seen[t]],
                                        start=True, stop=not causal)
                if causal:
                    last = nc.tensor.matmul(dst[:, t * P:(t + 1) * P], ident16[:, :], mask_q[:, :], start=False, stop=True)
                last.then_inc(max_ps, 1)

            def pe_turn(pe, i, s, first=False):
                pe.wait_ge(max_taken, i * 16 + 16)
                if not first:
                    pe.wait_ge(max_in, i)
                for t in range(KT):
                    last = nc.tensor.transpose(ps[0:VW, 6, t * P:(t + 1) * P], neg_max[:, s, t, :], ident[:, :])
                last.then_inc(max_turned, 1)

            def pe_scores(pe, i, s, uses, j, half, first=False):
                if j == 0 and half == 0:
                    pe.wait_ge(max_in, i + 1)
                    pe.wait_ge(q_loaded[s], uses * 16)
                n = 2 * j + half
                if not (first and n < 2):
                    pe.wait_ge(exp_done, i * 8 + n - 1)
                for k in (2 * half, 2 * half + 1):
                    off = start[k] - start[2 * half]
                    bank = 2 + 2 * half + off // T
                    dst = ps[:, bank, off % T:off % T + width[k]]
                    last = nc.tensor.matmul(dst, k_head[:, s, j, k * P:(k + 1) * P], q_exp[:, s, T - width[k]:T],
                                            start=True, stop=not causal)
                    if causal:
                        last = nc.tensor.matmul(dst[:, 0:P], ident16[:, :], mask_k[:, :], start=False, stop=True)
                last.then_inc(score_ps, 1)

            def pe_values(pe, i, s, k):
                if k == 0:
                    pe.wait_ge(exp_done, i * 8 + 8)
                    pe.wait_ge(v_made, i + 1)
                    pe.wait_ge(out_free, i + 1)
                for j in range(GH):
                    last = nc.tensor.matmul(ps[VW * j:VW * (j + 1), 7, T - width[k]:T], v_pad[:, s, k, j, :],
                                            probs[:, s, j, start[k]:start[k] + width[k]],
                                            start=(k == 0), stop=(k == KT - 1))
                if k == KT - 1:
                    last.then_inc(pv_done, 1)

            def pe_body(pe, i, s, uses, maxima=True, scores=True, values=True, first=False):
                for j in range(GH):
                    if maxima:
                        pe_maxima(pe, i + 1, 1 - s, j, 0)
                    if j == 0 and scores:
                        pe_turn(pe, i, s, first)
                    if j > 0 and scores:
                        pe_scores(pe, i, s, uses, j, 0, first)
                    if maxima:
                        pe_maxima(pe, i + 1, 1 - s, j, 1)
                    if values:
                        pe_values(pe, i - 1, 1 - s, j)
                    if j == 0 and scores:
                        pe_scores(pe, i, s, uses, j, 0, first)
                    if maxima:
                        pe_maxima(pe, i + 1, 1 - s, j, 2)
                    if scores:
                        pe_scores(pe, i, s, uses, j, 1, first)
                    if maxima:
                        pe_maxima(pe, i + 1, 1 - s, j, 3)

            def dve_keys(dve, i, s, uses, j, reuse):
                if j == 0:
                    dve.wait_ge(loaded[s], uses * 32)
                if reuse:
                    dve.wait_ge(score_ps, i * 8 - 16 + 2 * j + 2)
                nc.vector.tensor_scalar(k_head[:, s, j, :], k_stack[:, s, :], headmask[:, j:j + 1], None,
                                        ALU.mult).then_inc(k_made, 1)

            def dve_max_head(dve, i, s, j, reuse):
                if j == 0 and reuse:
                    dve.wait_ge(max_turned, i - 1)
                for t in range(KT):
                    n = 4 * j + t
                    dve.wait_ge(max_ps, i * 16 + n + 1)
                    nc.vector.tensor_reduce(neg_max[:, s, t, DH * j:DH * j + 1], ps[:, n % 2, 0:seen[t]], AX_X, ALU.max,
                                            negate=True).then_inc(max_taken, 1)

            def act_body(act, i, s, output=True):
                act.wait_ge(max_turned, i + 1)
                nc.scalar.mul(q_exp[96:P, s, :], ps[0:VW, 6, :], 1.0 / MAXC).then_inc(max_in, 1)
                act.wait_ge(pv_done, i + 1)
                for j in range(GH):
                    for half in range(2):
                        if output and j == GH - 1 and half == 1:
                            act_output(act, i - 1)
                        act.wait_ge(score_ps, i * 8 + 2 * j + half + 1)
                        n = sum(width[2 * half:2 * half + 2])
                        src = ps[:, 2 + 2 * half:4 + 2 * half, :].rearrange("p n t -> p (n t)")[:, 0:n]
                        at = start[2 * half]
                        nc.scalar.activation(probs[:, s, j, at:at + n], src, ACT.Exp, scale=scale).then_inc(exp_done, 1)

            def act_output(act, i):
                act.wait_ge(pv_done, i + 3)
                nc.scalar.copy(att_out[:, i, :], ps[:, 7, :]).then_inc(out_free, 1)

            def sp_load_max(sp, i, s):
                for dst, kind, rows in ((k_stack[0:96, s, :], 1, 96), (q_max[:, s, :], 0, 96)):
                    src = scratch[layer][kind].rearrange("a (i r) t -> i a r t", r=VW)[i]
                    sp.dma_start(dst, src).then_inc(loaded[s], 16)

            def sp_load_exp(sp, i, s):
                src = scratch[layer][0].rearrange("a (i r) t -> i a r t", r=VW)[i]
                sp.dma_start(q_exp[0:96, s, :], src).then_inc(q_loaded[s], 16)

            with nc.Block() as block:
                @block.sync
                def _(sp):
                    def body(i, s, ahead2, ahead1, first=False):
                        if ahead2:
                            sp.wait_ge(k_made, i * GH + GH)
                            sp.wait_ge(max_ps, i * 16 + 16)
                            sp_load_max(sp, i + 2, s)
                        if ahead1:
                            if not first:
                                sp.wait_ge(score_ps, i * 8)
                            sp_load_exp(sp, i + 1, 1 - s)

                    sp_load_max(sp, 0, 0)
                    sp_load_max(sp, 1, 1)
                    sp_load_exp(sp, 0, 0)
                    body(0, 0, True, True, first=True)
                    with sp.Fori(0, 2) as r:
                        for u in range(2):
                            body(r * 2 + (u + 1), (u + 1) % 2, True, True)
                    body(5, 1, True, True)
                    body(6, 0, False, True)

                @block.gpsimd
                def _(pool):
                    def body(i, s, reuse):
                        if reuse:
                            pool.wait_ge(pv_done, i + 1)
                        nc.gpsimd.tensor_copy(
                            v_pad[:, s, :, :, 0:DH],
                            v_all.rearrange("p b g k (j d) -> p (b g) k j d", d=DH)[:, i, :, :, :]).then_inc(v_made, 1)

                    for i in range(2):
                        body(i, i, False)
                    with pool.Fori(0, 3) as r:
                        for u in range(2):
                            body(r * 2 + (u + 2), u, True)

                @block.vector
                def _(dve):
                    def body(i, s, uses_next, reuse_max, reuse_key, keys=True):
                        for j in range(GH):
                            dve_max_head(dve, i, s, j, reuse_max)
                            if keys:
                                dve_keys(dve, i + 1, 1 - s, uses_next, j, reuse_key)

                    for j in range(GH):
                        dve_keys(dve, 0, 0, 1, j, False)
                    body(0, 0, 1, False, False)
                    body(1, 1, 2, False, True)
                    with dve.Fori(0, 2) as r:
                        body(r * 2 + 2, 0, r + 2, True, True)
                        body(r * 2 + 3, 1, r + 3, True, True)
                    body(6, 0, 4, True, True)
                    body(7, 1, None, True, True, keys=False)

                @block.scalar
                def _(act):
                    act.preload_act_table_set(LOG_EXP)
                    act_body(act, 0, 0, output=False)
                    with act.Fori(0, 3) as r:
                        act_body(act, r * 2 + 1, 1)
                        act_body(act, r * 2 + 2, 0)
                    act_body(act, 7, 1)
                    act_output(act, 7)

                @block.tensor
                def _(pe):
                    pe.sem_inc(pv_done, 2)
                    pe.sem_inc(out_free, 1)
                    for j in range(GH):
                        for t in range(KT):
                            pe_maxima(pe, 0, 0, j, t, first=True)
                    pe_body(pe, 0, 0, 1, values=False, first=True)
                    with pe.Fori(0, 3) as r:
                        pe_body(pe, r * 2 + 1, 1, r + 1)
                        pe_body(pe, r * 2 + 2, 0, r + 2)
                    pe_body(pe, 7, 1, 4, maxima=False)
                    pe_body(pe, 8, 0, None, maxima=False, scores=False)

        class Join8:

            def __init__(self, layer, index, wo):
                self.layer, self.index, self.wo = layer, index, wo
                self.picked, self.log, self.inv = sem(f"picked{layer}"), sem(f"den_log{layer}"), sem(f"den_inv{layer}")
                self.normed, self.proj_ps = sem(f"att_normed{layer}"), sem(f"proj_ps{layer}")
                self.biased, self.stream = sem(f"att_biased{layer}"), sem(f"stream_att{layer}")

            def pe(self, pe):
                for b in range(NB):
                    for sel, bank in ((den_sel, 1), (num_sel, 0)):
                        for g in range(NG):
                            last = nc.tensor.matmul(ps[VW * g:VW * (g + 1), 4 * b + bank, :], sel[:, :],
                                                    att_out[:, NG * b + g, :], start=True, stop=True)
                        last.then_inc(self.picked, 1)
                for b in range(NB):
                    pe.wait_ge(self.normed, b + 1)
                    nc.tensor.matmul(ps[:, 4 * b + 2, :], self.wo, xc[:, b, :], start=True, stop=True).then_inc(self.proj_ps, 1)

            def act(self, act):
                for b in range(NB):
                    act.wait_ge(self.picked, 2 * b + 1)
                    nc.scalar.activation(rs[:, b, :], ps[:, 4 * b + 1, :], ACT.Ln).then_inc(self.log, 1)
                    act.wait_ge(self.log, b + 1)
                    nc.scalar.activation(rs[:, b, :], rs[:, b, :], ACT.Exp, scale=-1.0).then_inc(self.inv, 1)

            def pool(self, pool):
                for b in range(NB):
                    nc.gpsimd.tensor_scalar(xb[:, b, :], xT[:, b, :], gate_b[:, self.index, 0, b:b + 1], None,
                                            ALU.add).then_inc(self.biased, 1)

            def dve(self, dve):
                for b in range(NB):
                    dve.wait_ge(self.picked, 2 * b + 2)
                    dve.wait_ge(self.inv, b + 1)
                    nc.vector.tensor_tensor(out=xc[:, b, :], in0=ps[:, 4 * b, :], in1=rs[:, b, :],
                                            op=ALU.mult).then_inc(self.normed, 1)
                for b in range(NB):
                    dve.wait_ge(self.proj_ps, b + 1)
                    dve.wait_ge(self.biased, b + 1)
                    nc.vector.scalar_tensor_tensor(out=xT[:, b, :], in0=ps[:, 4 * b + 2, :],
                                                   scalar=mods[:, 6 * self.index + 2, b:b + 1], in1=xb[:, b, :],
                                                   op0=ALU.mult, op1=ALU.add).then_inc(self.stream, 1)

        norm0a = adaptive_norm(0, 0, 0)
        proj0 = Projections(0, norm0a, w_qkv0[:, 0:D], w_qkv0[:, D:2 * D], w_qkv0[:, 2 * D:3 * D], zero_col[:, :], zero_col[:, :])
        with nc.Block() as block:
            @block.sync
            def _(sp):
                proj0.sp(sp)

            @block.tensor
            def _(pe):
                norm0a.pe(pe)
                proj0.pe(pe)

            @block.scalar
            def _(act):
                act.preload_act_table_set(LOG_EXP)
                norm0a.act(act)
                proj0.act(act)

            @block.vector
            def _(dve):
                norm0a.dve(dve)
                proj0.dve(dve)

        attention8(0, True, DH ** -0.5)

        join0 = Join8(0, 0, w_o0[:, :])
        norm0b = adaptive_norm(1, 0, 1)
        mlp0 = Mlp(0, norm0b, "L0b1")

        x_rows1_ps, x_rows1 = sem("x_rows1_ps"), sem("x_rows1")
        att_ps, att_max, att_bias, att_exp = sem("att_ps"), sem("att_max"), sem("att_bias"), sem("att_exp")
        ratio, cum_ps, cum_ready = sem("ratio"), sem("cum_ps"), sem("cum_ready")
        val_ps, rep_ps, rep_ready, scaled = sem("val_ps"), sem("rep_ps"), sem("rep_ready"), sem("scaled")
        op_ps, op_ready, ff1_ps, ff1_ready = sem("op_ps"), sem("op_ready"), sem("ff1_ps"), sem("ff1_ready")
        ff2_ps, stream1, op_step = sem("ff2_ps"), sem("stream1"), sem("op_step")
        norm1 = LayerNorm(2, 1, lambda b: col("gamma"), lambda b: col("beta"), dst=xT)
        norm2a = adaptive_norm(3, 1, 0)
        proj2 = Projections(2, norm2a, w_qkv2[:, 0, :], w_qkv2[:, 1, :], w_qkv2[:, 2, :], col("bq"), col("bk"))
        RATIO_STEPS = 9

        rows1 = hid[:, :, 0, :]
        cum = hid[:, :, 1, :]
        rep = hid[:, :, 2:4, :]
        att1 = big[0:H, 0, 0, :].rearrange("h (b t) -> h b t", t=T)
        den1 = big[0:H, 0, 1, :].rearrange("h (b t) -> h b t", t=T)
        rat1 = big[0:H, 0, 2, :].rearrange("h (b t) -> h b t", t=T)
        tmp1 = big[0:H, 0, 3, :].rearrange("h (b t) -> h b t", t=T)
        hi1 = q_hi[0:H, :, :].bitcast(BF16)
        scaled1 = big[:, 1, 0:2, :].rearrange("p s (b t) -> p b s t", t=T)
        opT = big[:, 1, 2, :].rearrange("p (b t) -> p b t", t=T)
        resT = big[:, 1, 3, :].rearrange("p (b t) -> p b t", t=T)

        def additive_pe(pe):
            for b in range(NB):
                pe.wait_ge(mlp0.stream, b + 1)
                for k in range(KT):
                    last = nc.tensor.transpose(ps[:, 4 * b + 3, k * P:(k + 1) * P], xT[:, b, k * P:(k + 1) * P], ident[:, :])
                last.then_inc(x_rows1_ps, 1)
                nc.tensor.matmul(ps[0:H, 4 * b + 1, :], w_att1[:, :], xT[:, b, :], start=True, stop=True).then_inc(att_ps, 1)
            for b in range(NB):
                pe.wait_ge(x_rows1, b + 1)
                for k in range(KT):
                    last = nc.tensor.matmul(ps[:, 4 * b + 2, k * P:T], rows1[:, b, k * P:(k + 1) * P], upper[:, 0:T - k * P],
                                            start=(k == 0), stop=(k == KT - 1))
                last.then_inc(cum_ps, 1)
            for c in range(NC):
                for b in range(NB):
                    n = NB * c + b
                    if c == 0:
                        pe.wait_ge(cum_ready, b + 1)
                        pe.wait_ge(ratio, RATIO_STEPS * (b + 1))
                    else:
                        pe.wait_ge(scaled, n - 1)
                        pe.wait_ge(rep_ready, n - 1)
                    nc.tensor.matmul(ps[:, 4 * b, :], w_val1[:, c * P:(c + 1) * P], cum[:, b, :], start=True,
                                     stop=True).then_inc(val_ps, 1)
                    nc.tensor.matmul(ps[:, 4 * b + 1, :], pair_sel[:, c, :, :].rearrange("p a b -> p (a b)"), r_parts[:, b, :],
                                     start=True, stop=True).then_inc(rep_ps, 1)
                if c > 0:
                    for b in range(NB):
                        operator_pe(pe, c - 1, b)
            for b in range(NB):
                operator_pe(pe, NC - 1, b)
            for b in range(NB):
                nc.tensor.matmul(ps[:, 4 * b, :], w_ff1[:, 0, :], xT[:, b, :], start=True, stop=False)
                pe.wait_ge(op_ready, b + 1)
                nc.tensor.matmul(ps[:, 4 * b, :], w_ff1[:, 1, :], opT[:, b, :], start=False, stop=True).then_inc(ff1_ps, 1)
            for b in range(NB):
                pe.wait_ge(ff1_ready, b + 1)
                nc.tensor.matmul(ps[:, 4 * b + 1, :], w_ff2[:, :], resT[:, b, :], start=True, stop=True).then_inc(ff2_ps, 1)

        def operator_pe(pe, c, b):
            pe.wait_ge(scaled, NB * c + b + 1)
            last = nc.tensor.matmul(ps[:, 4 * b + 3, :], w_op1[:, c, :], scaled1[:, b, c % 2, :],
                                    start=(c == 0), stop=(c == NC - 1))
            last.then_inc(op_ps if c == NC - 1 else op_step, 1)

        def additive_act(act):
            for b in range(NB):
                act.wait_ge(x_rows1_ps, b + 1)
                nc.scalar.copy(rows1[:, b, :], ps[:, 4 * b + 3, :]).then_inc(x_rows1, 1)
                act.wait_ge(att_bias, b + 1)
                nc.scalar.activation(att1[:, b, :], ps[0:H, 4 * b + 1, :], ACT.Exp, scale=temp[:, :],
                                     bias=amax[:, 2 + b:3 + b]).then_inc(att_exp, 1)
            for b in range(NB):
                act.wait_ge(cum_ps, b + 1)
                nc.scalar.copy(cum[:, b, :], ps[:, 4 * b + 2, :]).then_inc(cum_ready, 1)
            for c in range(NC):
                for b in range(NB):
                    n = NB * c + b
                    act.wait_ge(rep_ps, n + 1)
                    if c >= 2:
                        act.wait_ge(scaled, n - 3)
                    nc.scalar.copy(rep[:, b, c % 2, :], ps[:, 4 * b + 1, :]).then_inc(rep_ready, 1)
            for b in range(NB):
                act.wait_ge(op_ps, b + 1)
                nc.scalar.activation(opT[:, b, :], ps[:, 4 * b + 3, :], ACT.Identity, bias=col("cond", b)).then_inc(op_ready, 1)
            for b in range(NB):
                act.wait_ge(ff1_ps, b + 1)
                nc.scalar.activation(resT[:, b, :], ps[:, 4 * b, :], ACT.Relu, bias=col("ff1b")).then_inc(ff1_ready, 1)

        def additive_dve(dve):
            for b in range(NB):
                dve.wait_ge(att_ps, b + 1)
                nc.vector.tensor_reduce(amax[:, b:b + 1], ps[0:H, 4 * b + 1, :], AX_X, ALU.max, negate=True).then_inc(att_max, 1)
                dve.wait_ge(att_max, b + 1)
                nc.vector.tensor_tensor(out=amax[:, 2 + b:3 + b], in0=amax[:, b:b + 1], in1=temp[:, :],
                                        op=ALU.mult).then_inc(att_bias, 1)
            for b in range(NB):
                dve.wait_ge(att_exp, b + 1)
                done = RATIO_STEPS * b

                def step(ins, wait=True):
                    nonlocal done
                    done += 1
                    ins.then_inc(ratio, 1)
                    dve.wait_ge(ratio, done)

                step(nc.vector.tensor_tensor(out=den1[:, b, :], in0=att1[:, b, :], in1=counts[:, :], op=ALU.mult))
                step(nc.vector.tensor_scalar_add(den1[:, b, :], den1[:, b, :], 1e-30))
                step(nc.vector.reciprocal(rat1[:, b, :], den1[:, b, :]))
                step(nc.vector.tensor_tensor(out=rat1[:, b, :], in0=rat1[:, b, :], in1=att1[:, b, :], op=ALU.mult))
                step(nc.vector.tensor_copy(r_parts[0:H, b, :], rat1[:, b, :]))
                step(nc.vector.tensor_tensor(out=tmp1[:, b, :], in0=rat1[:, b, :], in1=r_parts[0:H, b, :], op=ALU.subtract))
                step(nc.vector.tensor_copy(hi1[:, b, :], tmp1[:, b, :]))
                step(nc.vector.tensor_copy(r_parts[32:32 + H, b, :], hi1[:, b, :]))
                step(nc.vector.tensor_tensor(out=r_parts[64:64 + H, b, :], in0=tmp1[:, b, :], in1=hi1[:, b, :], op=ALU.subtract))
            for c in range(NC):
                for b in range(NB):
                    n = NB * c + b
                    dve.wait_ge(val_ps, n + 1)
                    dve.wait_ge(rep_ready, n + 1)
                    if c >= 2:
                        dve.wait_ge(op_step, n - 3)
                    nc.vector.tensor_tensor(out=scaled1[:, b, c % 2, :], in0=ps[:, 4 * b, :], in1=rep[:, b, c % 2, :],
                                            op=ALU.mult).then_inc(scaled, 1)
            for b in range(NB):
                dve.wait_ge(ff2_ps, b + 1)
                nc.vector.scalar_tensor_tensor(out=xT[:, b, :], in0=ps[:, 4 * b + 1, :], scalar=col("ff2b"), in1=xT[:, b, :],
                                               op0=ALU.add, op1=ALU.add).then_inc(stream1, 1)

        with nc.Block() as block:
            @block.sync
            def _(sp):
                proj2.sp(sp)

            @block.gpsimd
            def _(pool):
                join0.pool(pool)
                mlp0.pool(pool)

            @block.tensor
            def _(pe):
                join0.pe(pe)
                norm0b.pe(pe, join0.stream)
                mlp0.pe(pe)
                additive_pe(pe)
                norm1.pe(pe, stream1)
                for b in range(NB):
                    pe.wait_ge(ln_out, norm1.count(b))
                norm2a.pe(pe)
                proj2.pe(pe)

            @block.scalar
            def _(act):
                act.preload_act_table_set(LOG_EXP)
                join0.act(act)
                norm0b.act(act)
                mlp0.act(act)
                additive_act(act)
                norm1.act(act)
                norm2a.act(act)
                proj2.act(act)

            @block.vector
            def _(dve):
                join0.dve(dve)
                norm0b.dve(dve)
                mlp0.dve(dve)
                additive_dve(dve)
                norm1.dve(dve)
                norm2a.dve(dve)
                proj2.dve(dve)

        attention8(2, False, 1.0 / DH)

        join2 = Join8(2, 1, w_o2[:, :])
        norm2b = adaptive_norm(4, 1, 1)
        mlp2 = Mlp(1, norm2b, "L2b1")
        norm3a = adaptive_norm(5, 2, 0)
        xm_hi_ready, xm_lo_ready = sem("xm_hi_ready"), sem("xm_lo_ready")
        with nc.Block() as block:
            @block.gpsimd
            def _(pool):
                join2.pool(pool)
                mlp2.pool(pool)

            @block.tensor
            def _(pe):
                join2.pe(pe)
                norm2b.pe(pe, join2.stream)
                mlp2.pe(pe)
                norm3a.pe(pe, mlp2.stream)

            @block.scalar
            def _(act):
                act.preload_act_table_set(LOG_EXP)
                join2.act(act)
                norm2b.act(act)
                mlp2.act(act)
                norm3a.act(act)
                for b in range(NB):
                    act.wait_ge(ln_out, norm3a.count(b))
                    nc.scalar.copy(xm_hi[:, b, :], xm[:, b, :]).then_inc(xm_hi_ready, 1)

            @block.vector
            def _(dve):
                join2.dve(dve)
                norm2b.dve(dve)
                mlp2.dve(dve)
                norm3a.dve(dve)
                for b in range(NB):
                    dve.wait_ge(xm_hi_ready, b + 1)
                    dve.wait_ge(ln_out, norm3a.count(b))
                    nc.vector.tensor_tensor(out=xm_lo[:, b, :], in0=xm[:, b, :], in1=xm_hi[:, b, :],
                                            op=ALU.subtract).then_inc(xm_lo_ready, 1)

        pair_loaded = sem("pair_loaded")
        w_hi_ready, w_lo_ready = sem("w_hi_ready"), sem("w_lo_ready")
        q3_ps, q3_hi, q3_lo = sem("q3_ps"), sem("q3_hi"), sem("q3_lo")
        k3_ps, k3_hi, k3_lo = sem("k3_ps"), sem("k3_hi"), sem("k3_lo")
        v3_ps, v3_ready = sem("v3_ps"), sem("v3_ready")
        placed = [sem(f"placed{b}") for b in range(NB)]
        max3_ps, max3_taken = sem("max3_ps"), sem("max3_taken")
        max3_turned, max3_in = sem("max3_turned"), sem("max3_in")
        score3_ps, exp3_done = sem("score3_ps"), sem("exp3_done")
        pair3_sum, key3_sum = sem("pair3_sum"), sem("key3_sum")
        pv3_ps, den3_ps = sem("pv3_ps"), sem("den3_ps")
        den3_log, den3_inv, pair3_out = sem("den3_log"), sem("den3_inv"), sem("pair3_out")
        inv3 = sq[:, 0, :]
        half_sum = big[:, 0, 2, :].rearrange("p (h n) -> p h n", h=2)
        key_sum = big[:, 0, 3, 0:2 * T].rearrange("p (h n) -> p h n", h=2)
        w_qkv3 = a["L3_cond_W_qkv"].rearrange("d (s c n) -> c d s n", s=3, n=P)

        def pe3_project(pe, v, b, c):
            pe.wait_ge(w_lo_ready, c + 1)
            for i in range(2):
                for n, (w, x) in enumerate(((w_hi, xm_hi), (w_lo, xm_hi), (w_hi, xm_lo))):
                    last = nc.tensor.matmul(ps[:, i, :], w[:, i, :], x[:, b, :], start=(n == 0), stop=(n == 2))
                last.then_inc((q3_ps, k3_ps)[i], 1)

        def pe3_values(pe, b):
            for k in range(KT):
                for n, (w, x) in enumerate(((w_hi, xm_hi), (w_lo, xm_hi), (w_hi, xm_lo))):
                    last = nc.tensor.matmul(ps[:, 6, k * P:(k + 1) * P], x[:, b, k * P:(k + 1) * P], w[:, 2, :],
                                            start=(n == 0), stop=(n == 2))
            last.then_inc(v3_ps, 1)

        def pe3_maxima(pe, v, b, uses, n, projected=True):
            h, t = n // KT, n % KT
            if n == 0:
                pe.wait_ge(placed[b], uses * (12 * 16))
            if n < 2 and projected:
                pe.wait_ge((q3_lo, k3_lo)[n], v + 2)
            if n >= 2:
                pe.wait_ge(max3_taken, v * 8 + n - 1)
            nc.tensor.matmul(ps[:, n % 2, :], q_a[:, b, h, t * P:(t + 1) * P], k_a[:, b, h, :],
                             start=True, stop=True).then_inc(max3_ps, 1)

        def pe3_turn(pe, u, b):
            pe.wait_ge(max3_taken, u * 8 + 8)
            for t in range(KT):
                last = nc.tensor.transpose(ps[0:VW, 7, t * P:(t + 1) * P], neg_max3[:, b, t, :], ident[:, :])
            last.then_inc(max3_turned, 1)

        def pe3_scores(pe, u, b, n, values=True, first=False):
            h, half = n // 2, n % 2
            if n < 2:
                pe.wait_ge(max3_in, u * 2 + n + 1)
            if n == 1 and values:
                pe.wait_ge(v3_ready, u + 2)
            if not (first and n < 2):
                pe.wait_ge(exp3_done, u * 4 + n - 1)
            for k in (2 * half, 2 * half + 1):
                dst = ps[:, 4 + k, :]
                nc.tensor.matmul(dst, k_a[:, b, h, k * P:(k + 1) * P], q_a[:, b, h, :], start=True, stop=False)
                last = nc.tensor.matmul(dst, k_b[:, b, h, k * P:(k + 1) * P], q_b[:, b, h, :], start=False, stop=True)
            last.then_inc(score3_ps, 1)

        def pe3_outputs(pe, u, b, k, first=False):
            if k == 0 and not first:
                pe.wait_ge(pair3_out, u)
            for h in range(2):
                if k % 2 == 0:
                    pe.wait_ge(exp3_done, u * 4 + 2 * h + k // 2 + 1)
                last = nc.tensor.matmul(ps[DW * h:DW * (h + 1), 2, :], v_pair[:, b, k, DW * h:DW * (h + 1)],
                                        probs[:, 0, h, k * T:(k + 1) * T], start=(k == 0), stop=(k == KT - 1))
            if k == KT - 1:
                last.then_inc(pv3_ps, 1)

        def pe3_denominators(pe, u, first=False):
            if not first:
                pe.wait_ge(den3_log, u)
            for h in range(2):
                pe.wait_ge(key3_sum, u * 2 + h + 1)
                last = nc.tensor.matmul(ps[DW * h:DW * (h + 1), 3, :], ones[:, :], key_sum[:, h, :], start=True, stop=True)
            last.then_inc(den3_ps, 1)

        def pe3_body(pe, u, b, c_next, uses_next, index=2, last=False):
            pe3_turn(pe, u, b)
            if index == 0:
                pe.wait_ge(v3_ready, 1)
            if not last:
                pe3_values(pe, 1 - b)
            pe3_scores(pe, u, b, 0, first=(index == 0))
            pe3_scores(pe, u, b, 1, values=not last, first=(index == 0))
            if index > 0:
                pe3_denominators(pe, u - 1, first=(index == 1))
            if c_next is not None:
                pe3_project(pe, u + 2, b, c_next)
            pe3_scores(pe, u, b, 2)
            pe3_scores(pe, u, b, 3)
            for n in range(2 * KT):
                if n % 2 == 0:
                    pe3_outputs(pe, u, b, n // 2, first=(index == 0))
                if not last:
                    pe3_maxima(pe, u + 1, 1 - b, uses_next, n, projected=c_next is not None)

        def act3_weights(act, c, reuse=True):
            act.wait_ge(pair_loaded, c * 16 + 16)
            if reuse:
                act.wait_ge(v3_ps, c * 2)
            nc.scalar.mul(w_hi[:, :, :], w_pair[:, :, :], WSC).then_inc(w_hi_ready, 1)

        def act3_split(act, v, b):
            act.wait_ge(q3_ps, v + 1)
            nc.scalar.mul(q_hi[:, b, :], ps[:, 0, :], 1.0 / WSC).then_inc(q3_hi, 1)
            act.wait_ge(k3_ps, v + 1)
            nc.scalar.mul(k_hi[:, b, :], ps[:, 1, :], 1.0 / WSC).then_inc(k3_hi, 1)

        def act3_max_in(act, u, b):
            act.wait_ge(max3_turned, u + 1)
            for h in range(2):
                nc.scalar.mul(q_b[DW:96, b, h, :], ps[0:VW, 7, :], 1.0 / MAXC).then_inc(max3_in, 1)

        def act3_exp(act, u, b, n, first=False):
            h, half = n // 2, n % 2
            if n == 0 and not first:
                act.wait_ge(pv3_ps, u)
            if half == 0 and not first:
                act.wait_ge(pair3_sum, u * 2 + h - 1)
            act.wait_ge(score3_ps, u * 4 + n + 1)
            nc.scalar.activation(probs[:, 0, h, half * 2 * T:(half + 1) * 2 * T],
                                 ps[:, 4 + 2 * half:6 + 2 * half, :].rearrange("p n t -> p (n t)"), ACT.Exp,
                                 scale=DW ** -0.5).then_inc(exp3_done, 1)

        def act3_inverse(act, u, first=False):
            act.wait_ge(den3_ps, u + 1)
            if not first:
                act.wait_ge(pair3_out, u)
            nc.scalar.activation(inv3, ps[:, 3, :], ACT.Ln).then_inc(den3_log, 1)
            act.wait_ge(den3_log, u + 1)
            nc.scalar.activation(inv3, inv3, ACT.Exp, scale=-1.0).then_inc(den3_inv, 1)

        def act3_body(act, u, b, c_new=None, project=True, index=2):
            act3_max_in(act, u, b)
            if c_new is not None:
                act3_weights(act, c_new)
            act3_exp(act, u, b, 0, index == 0)
            act3_exp(act, u, b, 1)
            if project:
                act3_split(act, u + 2, b)
            if index > 0:
                act3_inverse(act, u - 1, index == 1)
            act3_exp(act, u, b, 2, index == 0)
            act3_exp(act, u, b, 3)

        def dve3_weights(dve, c):
            dve.wait_ge(w_hi_ready, c + 1)
            nc.vector.scalar_tensor_tensor(out=w_lo[:, :, :], in0=w_pair[:, :, :], scalar=WSC, in1=w_hi[:, :, :],
                                           op0=ALU.mult, op1=ALU.subtract).then_inc(w_lo_ready, 1)

        def dve3_split(dve, v, b):
            for i, (hi, lo, hi_ready, lo_ready) in enumerate(((q_hi, q_lo, q3_hi, q3_lo), (k_hi, k_lo, k3_hi, k3_lo))):
                dve.wait_ge(hi_ready, v + 1)
                nc.vector.scalar_tensor_tensor(out=lo[:, b, :], in0=ps[:, i, :], scalar=1.0 / WSC, in1=hi[:, b, :],
                                               op0=ALU.mult, op1=ALU.subtract).then_inc(lo_ready, 1)

        def dve3_values(dve, v, b, reuse):
            dve.wait_ge(v3_ps, v + 1)
            if reuse:
                dve.wait_ge(pv3_ps, v - 1)
            nc.vector.tensor_scalar(v_pair[:, b, :, :].rearrange("p k n -> p (k n)"), ps[:, 6, :], 1.0 / WSC, None,
                                    ALU.mult).then_inc(v3_ready, 1)

        def dve3_maxima(dve, v, b, n, reuse):
            if n == 0 and reuse:
                dve.wait_ge(max3_turned, v - 1)
            h, t = n // KT, n % KT
            dve.wait_ge(max3_ps, v * 8 + n + 1)
            nc.vector.tensor_reduce(neg_max3[:, b, t, h:h + 1], ps[:, n % 2, :], AX_X, ALU.max,
                                    negate=True).then_inc(max3_taken, 1)

        def dve3_sum(dve, u, h, first=False):
            dve.wait_ge(pair3_sum, u * 2 + h + 1)
            if h == 0 and not first:
                dve.wait_ge(den3_ps, u)
            nc.vector.tensor_tensor(out=key_sum[:, h, :], in0=half_sum[:, h, 0:T], in1=half_sum[:, h, T:2 * T],
                                    op=ALU.add).then_inc(key3_sum, 1)

        def dve3_divide(dve, u):
            dve.wait_ge(den3_inv, u + 1)
            nc.vector.tensor_tensor(out=pair_out[:, u, :], in0=ps[:, 2, :], in1=inv3, op=ALU.mult).then_inc(pair3_out, 1)

        def dve3_body(dve, u, b, c_new=None, project=True, index=2, last=False):
            if not last:
                dve3_values(dve, u + 1, 1 - b, index > 0)
            if c_new is not None:
                dve3_weights(dve, c_new)
            if project:
                dve3_split(dve, u + 2, b)
            if index > 0:
                dve3_divide(dve, u - 1)
            for n in range(2 * KT):
                if not last:
                    dve3_maxima(dve, u + 1, 1 - b, n, index > 0)
                if n == KT:
                    dve3_sum(dve, u, 0, index == 0)
            dve3_sum(dve, u, 1)

        def pool3_body(pool, u, first=False):
            for h in range(2):
                pool.wait_ge(exp3_done, u * 4 + 2 * h + 2)
                if not first:
                    pool.wait_ge(key3_sum, u * 2 + h - 1)
                nc.gpsimd.tensor_tensor(out=half_sum[:, h, :], in0=probs[:, 0, h, 0:2 * T], in1=probs[:, 0, h, 2 * T:4 * T],
                                        op=ALU.add).then_inc(pair3_sum, 1)

        def sp3_place(sp, v, b, reuse):
            sp.wait_ge(q3_lo, v + 1)
            if reuse:
                sp.wait_ge(score3_ps, v * 4 - 4)
            for h in range(2):
                rows = slice(DW * h, DW * (h + 1))
                for dst, src in ((q_a[0:DW, b, h, :], q_hi), (q_a[DW:P, b, h, :], q_lo), (q_b[0:DW, b, h, :], q_hi)):
                    sp.dma_start(dst, src[rows, b, :]).then_inc(placed[b], 16)
            sp.wait_ge(k3_lo, v + 1)
            for h in range(2):
                rows = slice(DW * h, DW * (h + 1))
                for dst, src in ((k_a[0:DW, b, h, :], k_hi), (k_a[DW:P, b, h, :], k_hi), (k_b[0:DW, b, h, :], k_lo)):
                    sp.dma_start(dst, src[rows, b, :]).then_inc(placed[b], 16)

        with nc.Block() as block:
            @block.sync
            def _(sp):
                def load_pair(c):
                    sp.dma_start(w_pair[:, :, :], w_qkv3[c]).then_inc(pair_loaded, 16)

                load_pair(0)
                sp.wait_ge(w_lo_ready, 1)
                load_pair(1)
                sp3_place(sp, 0, 0, False)
                sp3_place(sp, 1, 1, False)
                with sp.Fori(1, NC - 1) as c:
                    sp.wait_ge(w_lo_ready, c + 1)
                    load_pair(c + 1)
                    sp3_place(sp, c * 2, 0, True)
                    sp3_place(sp, c * 2 + 1, 1, True)
                sp3_place(sp, 2 * NC - 2, 0, True)
                sp3_place(sp, 2 * NC - 1, 1, True)

            @block.gpsimd
            def _(pool):
                pool3_body(pool, 0, first=True)
                with pool.Fori(1, 2 * NC) as u:
                    pool3_body(pool, u)

            @block.tensor
            def _(pe):
                pe3_project(pe, 0, 0, 0)
                pe3_values(pe, 0)
                pe.wait_ge(q3_lo, 1)
                pe.wait_ge(k3_lo, 1)
                pe3_project(pe, 1, 1, 0)
                for n in range(2 * KT):
                    pe3_maxima(pe, 0, 0, 1, n)
                pe3_body(pe, 0, 0, 1, 1, index=0)
                pe3_body(pe, 1, 1, 1, 2, index=1)
                with pe.Fori(1, NC - 1) as c:
                    pe3_body(pe, c * 2, 0, c + 1, c + 1)
                    pe3_body(pe, c * 2 + 1, 1, c + 1, c + 2)
                pe3_body(pe, 2 * NC - 2, 0, None, NC)
                pe3_body(pe, 2 * NC - 1, 1, None, None, last=True)
                pe3_denominators(pe, 2 * NC - 1)

            @block.scalar
            def _(act):
                act.preload_act_table_set(LOG_EXP)
                act3_weights(act, 0, reuse=False)
                act3_split(act, 0, 0)
                act3_split(act, 1, 1)
                act3_body(act, 0, 0, c_new=1, index=0)
                act3_body(act, 1, 1, index=1)
                with act.Fori(1, NC - 1) as c:
                    act3_body(act, c * 2, 0, c_new=c + 1)
                    act3_body(act, c * 2 + 1, 1)
                act3_body(act, 2 * NC - 2, 0, project=False)
                act3_body(act, 2 * NC - 1, 1, project=False)
                act3_inverse(act, 2 * NC - 1)

            @block.vector
            def _(dve):
                dve3_weights(dve, 0)
                dve3_split(dve, 0, 0)
                dve3_values(dve, 0, 0, False)
                dve3_split(dve, 1, 1)
                for n in range(2 * KT):
                    dve3_maxima(dve, 0, 0, n, False)
                dve3_body(dve, 0, 0, c_new=1, index=0)
                dve3_body(dve, 1, 1, index=1)
                with dve.Fori(1, NC - 1) as c:
                    dve3_body(dve, c * 2, 0, c_new=c + 1)
                    dve3_body(dve, c * 2 + 1, 1)
                dve3_body(dve, 2 * NC - 2, 0, project=False)
                dve3_body(dve, 2 * NC - 1, 1, project=False, last=True)
                dve3_divide(dve, 2 * NC - 1)

        out3_ps, biased3, stream3 = sem("out3_ps"), sem("biased3"), sem("stream3")
        norm3b = adaptive_norm(6, 2, 1)
        mlp3 = Mlp(2, norm3b, "L3b1")
        y_ps, y_ready, y_stored = sem("y_ps"), sem("y_ready"), sem("y_stored")
        with nc.Block() as block:
            @block.gpsimd
            def _(pool):
                for b in range(NB):
                    nc.gpsimd.tensor_scalar(xb[:, b, :], xT[:, b, :], gate_b[:, 2, 0, b:b + 1], None, ALU.add).then_inc(biased3, 1)
                mlp3.pool(pool)

            @block.tensor
            def _(pe):
                for b in range(NB):
                    for c in range(NC):
                        last = nc.tensor.matmul(ps[:, 4 * b + 2, :], w_o3[:, c, :], pair_out[:, c * NB + b, :],
                                                start=(c == 0), stop=(c == NC - 1))
                    last.then_inc(out3_ps, 1)
                norm3b.pe(pe, stream3)
                mlp3.pe(pe)
                for b in range(NB):
                    pe.wait_ge(mlp3.stream, b + 1)
                    for k in range(KT):
                        last = nc.tensor.transpose(ps[:, 4 * b + 1, k * P:(k + 1) * P], xT[:, b, k * P:(k + 1) * P], ident[:, :])
                    last.then_inc(y_ps, 1)

            @block.scalar
            def _(act):
                act.preload_act_table_set(LOG_EXP)
                norm3b.act(act)
                mlp3.act(act)
                for b in range(NB):
                    act.wait_ge(y_ps, b + 1)
                    nc.scalar.copy(xc[:, b, :], ps[:, 4 * b + 1, :]).then_inc(y_ready, 1)

            @block.vector
            def _(dve):
                for b in range(NB):
                    dve.wait_ge(out3_ps, b + 1)
                    dve.wait_ge(biased3, b + 1)
                    nc.vector.scalar_tensor_tensor(out=xT[:, b, :], in0=ps[:, 4 * b + 2, :], scalar=mods[:, 14, b:b + 1],
                                                   in1=xb[:, b, :], op0=ALU.mult, op1=ALU.add).then_inc(stream3, 1)
                norm3b.dve(dve)
                mlp3.dve(dve)

            @block.sync
            def _(sp):
                for b in range(NB):
                    sp.wait_ge(y_ready, b + 1)
                    sp.dma_start(out[b].rearrange("(k p) d -> p k d", p=P),
                                 xc[:, b, :].rearrange("p (k d) -> p k d", d=D)).then_inc(y_stored, 16)
                sp.wait_ge(y_stored, 16 * NB)


def kernel(**inputs):
    import numpy as np
    import concourse.bacc as bacc
    from concourse.bass_utils import run_bass_kernel_spmd

    nc = bacc.Bacc("TRN2", target_bir_lowering=False, num_devices=1)
    arrays, aps = {}, {}
    for name, value in inputs.items():
        value = np.ascontiguousarray(value)
        arrays[f"in_{name}"] = value
        aps[name] = nc.dram_tensor(f"in_{name}", value.shape, mybir.dt.from_np(value.dtype), kind="ExternalInput").ap()
    out = nc.dram_tensor("out_0", (NB, T, D), F32, kind="ExternalOutput").ap()
    build_program(nc, aps, out)
    result = run_bass_kernel_spmd(nc, [arrays], core_ids=[0])
    return result.results[0]["out_0"]
```

```python
from contextlib import ExitStack

import concourse.bass as bass
from concourse import mybir

F32 = mybir.dt.float32
F16 = mybir.dt.float16
BF16 = mybir.dt.bfloat16
ALU = mybir.AluOpType
ACT = mybir.ActivationFunctionType
AX_X = mybir.AxisListType.X
LOG_EXP = "natural_log_exp_and_others"

P = 128
D = 128
NB = 2
T = 512
KT = T // P
H = 16
DH = D // H
GH = 4
NG = H // GH
NGRP = NB * NG
VW = 32
DW = 64
NC = H * DW // P
MLP = 4 * D // P
NEG = -60000.0
WSC = 256.0
SUMC = 1024.0
MAXC = 64.0
LN_EPS = (1e-5, 1e-6)

VECTORS = [
    ("cond", NB), ("ada0", 6), ("g1", 1), ("be1", 1),
    ("ada2", 6), ("ada3", 6), ("g2", 1), ("be2", 1), ("bproj", 1), ("L0b1", MLP), ("L0b2", 1),
    ("ff1b", 1), ("ff2b", 1), ("gamma", 1), ("beta", 1),
    ("bq", 1), ("bk", 1), ("bv", 1), ("bo", 1), ("L2b1", MLP), ("L2b2", 1),
    ("bout", 1), ("L3b1", MLP), ("L3b2", 1),
]
COL = {}
for _name, _n in VECTORS:
    COL[_name] = sum(n for _, n in VECTORS[:len(COL)])
NCOL = sum(n for _, n in VECTORS)
FIRST = 4
NFIRST = sum(n for _, n in VECTORS[:FIRST])


def build_program(nc, a, out):
    with ExitStack() as ctx:
        def sb(name, shape, dt=F32):
            return ctx.enter_context(nc.sbuf_tensor(name, shape, dt))

        def sem(name):
            return ctx.enter_context(nc.semaphore(name))

        ident = sb("ident", [P, P])
        ident16 = sb("ident16", [P, P], F16)
        mean_mat = sb("mean_mat", [P, P])
        centre_mat = sb("centre_mat", [P, P])
        ones_row = sb("ones_row", [P, T])
        mask_q = sb("mask_q", [P, P], F16)
        mask_k = sb("mask_k", [P, P], F16)
        head_of = sb("head_of", [P, GH, VW])
        headmask = sb("headmask", [P, GH])
        num_sel = sb("num_sel", [P, VW])
        den_sel = sb("den_sel", [P, VW])
        pair_sel = sb("pair_sel", [P, NC, 2, DW], BF16)
        counts_i = sb("counts_i", [NB * VW, T], mybir.dt.int32)
        counts = sb("counts", [NB * VW, T])
        eps = sb("eps", [P, 2])
        zero_col = sb("zero_col", [P, 1])

        w_ada = sb("w_ada", [P, 3, 6 * D])
        w_qkv0 = sb("w_qkv0", [P, 3 * D])
        w_qkv2 = sb("w_qkv2", [P, 3, D])
        w_o0 = sb("w_o0", [P, D])
        w_o2 = sb("w_o2", [P, D])
        w_o3 = sb("w_o3", [P, NC, D])
        w_up = sb("w_up", [P, 3, MLP * P])
        w_down = sb("w_down", [P, 3, MLP, D])
        w_att1 = sb("w_att1", [P, VW])
        w_val1 = sb("w_val1", [P, H * DW])
        w_op1 = sb("w_op1", [P, NC, D])
        w_ff1 = sb("w_ff1", [P, 2, D])
        w_ff2 = sb("w_ff2", [P, D])
        w_pair = sb("w_pair", [P, 3, P])

        vec_rows = sb("vec_rows", [NCOL, D])
        cols = sb("cols", [P, NCOL])
        temp = sb("temp", [NB * VW, 1])
        silu = sb("silu", [P, 3, NB])
        mods = sb("mods", [P, 18, NB])
        ln_g = sb("ln_g", [P, 3, 2, NB])
        ln_b = sb("ln_b", [P, 3, 2, NB])
        gate_b = sb("gate_b", [P, 3, 2, NB])
        bo2 = sb("bo2", [P, 1])

        xT = sb("xT", [P, NB, T])
        xb = sb("xb", [P, NB, T])
        xm = sb("xm", [P, NB, T])
        xc = sb("xc", [P, NB, T])
        sq = sb("sq", [P, NB, T])
        rs = sb("rs", [P, NB, T])
        hid = sb("hid", [P, NB, MLP, T])
        big = sb("big", [P, 2, GH, KT * T])
        probs = big
        pair_out = big[:, 1, :, :].rearrange("p g (u t) -> p (g u) t", t=T)
        att_out = hid.rearrange("p b m t -> p (b m) t")

        q_hi = sb("q_hi", [P, NB, T], F16)
        q_lo = sb("q_lo", [P, NB, T], F16)
        k_hi = sb("k_hi", [P, NB, T], F16)
        k_lo = sb("k_lo", [P, NB, T], F16)
        k_stack = sb("k_stack", [P, 2, T], F16)
        q_max = sb("q_max", [96, 2, T], F16)
        q_exp = sb("q_exp", [P, 2, T], F16)
        k_head = sb("k_head", [P, 2, GH, T], F16)
        v_all = sb("v_all", [P, NB, NG, KT, GH * DH])
        v_pad = sb("v_pad", [P, 2, KT, GH, VW])
        neg_max = sb("neg_max", [P, 2, KT, VW])
        r_parts = sb("r_parts", [P, NB, T], BF16)
        q_a = sb("q_a", [P, NB, 2, T], F16)
        q_b = sb("q_b", [96, NB, 2, T], F16)
        k_a = sb("k_a", [P, NB, 2, T], F16)
        k_b = sb("k_b", [96, NB, 2, T], F16)
        late = w_ada.rearrange("p a n -> p (a n)")
        v_pair = late[:, 0:NB * T].rearrange("p (b k n) -> p b k n", b=NB, k=KT)
        den_ones = sb("den_ones", [P, DW], F16)
        late16 = late[:, NB * T:].bitcast(F16)
        xm_hi = late16[:, 0:NB * T].rearrange("p (b t) -> p b t", b=NB)
        xm_lo = late16[:, NB * T:2 * NB * T].rearrange("p (b t) -> p b t", b=NB)
        w_hi = late16[:, 2 * NB * T:2 * NB * T + 3 * P].rearrange("p (s n) -> p s n", s=3)
        w_lo = k_stack[:, 0, 0:3 * P].rearrange("p (s n) -> p s n", s=3)
        amax = sb("amax", [NB * VW, 2])
        neg_max3 = sb("neg_max3", [P, NB, 2, KT, VW])

        ps = ctx.enter_context(nc.psum_tensor("ps", [P, 8, T], F32))

        scratch = {layer: nc.dram_tensor(f"split{layer}", (2, 3, NB * P, T), F16, kind="Internal").ap()
                   for layer in (0, 2)}

        def col(name, i=0):
            return cols[:, COL[name] + i:COL[name] + i + 1]

        zeroed = sem("zeroed")
        ident_made = sem("ident_made")
        const_pool = sem("const_pool")
        const_first, const_made = sem("const_first"), sem("const_made")
        x_loaded = [sem(f"x_loaded{b}") for b in range(NB)]
        x_turned, xT_ready = sem("x_turned"), sem("xT_ready")
        rows_first, rows_rest = sem("rows_first"), sem("rows_rest")
        w_first = sem("w_first")
        w_rest = sem("w_rest")
        w_bulk = sem("w_bulk")
        vec_turned, cols_ready = sem("vec_turned"), sem("cols_ready")
        silu_act, silu_dve = sem("silu_act"), sem("silu_dve")
        mods_ps0, mods_ps = sem("mods_ps0"), sem("mods_ps")
        mods_done0, mods_done = sem("mods_done0"), sem("mods_done")
        x_rows = att_out

        row_sources = {
            "cond": a["cond_1024"], "ada0": a["L0_cond_bada"], "ada2": a["L2_cond_bc"], "ada3": a["L3_cond_b_mod"],
            "g1": a["L0_cond_g1"], "g2": a["L0_cond_g2"], "be1": a["L0_cond_be1"], "be2": a["L0_cond_be2"],
            "bproj": a["L0_cond_bproj"], "L0b1": a["L0_cond_b1"], "L0b2": a["L0_cond_b2"],
            "ff1b": a["L1_cond_ff1_bias"], "ff2b": a["L1_cond_ff2_bias"],
            "gamma": a["L1_cond_ln_gamma"], "beta": a["L1_cond_ln_beta"],
            "bq": a["L2_cond_bq"], "bk": a["L2_cond_bk"], "bv": a["L2_cond_bv"], "bo": a["L2_cond_bo"],
            "L2b1": a["L2_cond_b1"], "L2b2": a["L2_cond_b2"],
            "bout": a["L3_cond_b_out"], "L3b1": a["L3_cond_b1"], "L3b2": a["L3_cond_b2"],
        }

        def rows_of(name):
            src = row_sources[name]
            if len(src.shape) == 1:
                return src.rearrange("(n p) -> n p", p=D)
            if len(src.shape) == 3:
                return src.rearrange("a b p -> (a b) p")
            return src

        weights = [
            (w_o0[:, :], a["L0_cond_Wproj"]),
            (w_up[:, 0, :], a["L0_cond_W1"]), (w_down[:, 0, :, :], a["L0_cond_W2"].rearrange("(m p) n -> p m n", p=P)),
            (w_val1[:, :], a["L1_cond_values"].rearrange("d h k -> d (h k)")),
            (w_op1[:, :, :], a["L1_cond_operator"].rearrange("(c p) n -> p c n", p=P)),
            (w_ff1[:, :, :], a["L1_cond_ff1"].rearrange("(m p) n -> p m n", p=P)), (w_ff2[:, :], a["L1_cond_ff2"]),
            (w_qkv2[:, 0, :], a["L2_cond_Wq"]), (w_qkv2[:, 1, :], a["L2_cond_Wk"]), (w_qkv2[:, 2, :], a["L2_cond_Wv"]),
            (w_up[:, 1, :], a["L2_cond_W1"]), (w_down[:, 1, :, :], a["L2_cond_W2"].rearrange("(m p) n -> p m n", p=P)),
            (w_o3[:, :, :], a["L3_cond_W_out"].rearrange("(c p) n -> p c n", p=P)),
            (w_up[:, 2, :], a["L3_cond_W1"]), (w_down[:, 2, :, :], a["L3_cond_W2"].rearrange("(m p) n -> p m n", p=P)),
        ]
        N_POOL_CONST, N_CONST_MADE = 8, 7
        N_MODS_DONE0, N_MODS_DONE = 5, 20

        def setup_sp(sp):
            for i, (name, n) in enumerate(VECTORS):
                sp.dma_start(vec_rows[COL[name]:COL[name] + n, :], rows_of(name)).then_inc(rows_first if i < FIRST else rows_rest, 16)
                if i == FIRST - 1:
                    sp.dma_start(w_qkv0[:, :], a["L0_cond_Wqkv"]).then_inc(w_first, 16)
            sp.dma_start(w_o2[:, :], a["L2_cond_Wo"]).then_inc(w_rest, 16)
            sp.wait_ge(const_first, 1)
            sp.dma_start(w_att1[:, 0:H], a["L1_cond_attention_weights"]).then_inc(rows_rest, 16)
            for b in range(NB):
                sp.dma_start(temp[VW * b:VW * b + H, :], a["L1_cond_temperature"].rearrange("a b h -> h (a b)")).then_inc(rows_rest, 16)

        def setup_pool(pool):
            nc.gpsimd.memset(ident[:], 0.0).then_inc(zeroed, 1)
            pool.wait_ge(zeroed, 1)

            def ones_where(view, pattern, base=0):
                return nc.gpsimd.affine_select(out=view, in_=view, compare_op=ALU.not_equal, fill=1.0, base=base,
                                               pattern=pattern, channel_multiplier=1)

            ones_where(ident[:, :], [[-1, P]]).then_inc(ident_made, 1)
            nc.gpsimd.memset(ident16[:], 0.0)
            nc.gpsimd.memset(ones_row[:], 1.0)
            nc.gpsimd.memset(mask_q[:], 0.0)
            nc.gpsimd.memset(mask_k[:], 0.0)
            nc.gpsimd.memset(head_of[:], 0.0)
            nc.gpsimd.memset(num_sel[:], 0.0)
            nc.gpsimd.memset(den_sel[:], 0.0)
            nc.gpsimd.memset(pair_sel[:], 0.0).then_inc(zeroed, 1)
            pool.wait_ge(zeroed, 2)
            ones_where(head_of[:, :, :].rearrange("p j (q r) -> p j q r", r=DH),
                       [[-DH, GH], [-VW, 4], [-1, DH]]).then_inc(const_pool, 1)
            ones_where(ident16[:, :], [[-1, P]]).then_inc(const_pool, 1)
            nc.gpsimd.affine_select(out=mask_q[:, :], in_=mask_q[:, :], compare_op=ALU.is_ge, fill=NEG, base=0,
                                    pattern=[[-1, P]], channel_multiplier=1).then_inc(const_pool, 1)
            nc.gpsimd.affine_select(out=mask_k[:, :], in_=mask_k[:, :], compare_op=ALU.is_ge, fill=NEG, base=0,
                                    pattern=[[1, P]], channel_multiplier=-1).then_inc(const_pool, 1)
            ones_where(num_sel[:, :].rearrange("p (j r) -> p j r", r=DH), [[-VW, GH], [-1, DH]]).then_inc(const_pool, 1)
            ones_where(den_sel[:, :].rearrange("p (j r) -> p j r", r=DH), [[-VW, GH], [0, DH]],
                       base=-DH).then_inc(const_pool, 1)
            for n in range(3):
                last = ones_where(pair_sel[:, :, :, :], [[-2, NC], [-1, 2], [0, DW]], base=-32 * n)
                if n < 2:
                    last.then_inc(zeroed, 1)
                    pool.wait_ge(zeroed, n + 3)
            last.then_inc(const_pool, 1)
            nc.gpsimd.iota(counts_i[:, :], pattern=[[1, T]], base=1, channel_multiplier=0).then_inc(const_pool, 1)
            for dst, src in weights:
                pool.dma_start(dst, src).then_inc(w_bulk, 16)

        def setup_act(act):
            for b in range(NB):
                act.dma_start(x_rows[:, 4 * b, :].rearrange("p (k d) -> p k d", d=D),
                              a["x"][b].rearrange("(k p) d -> p k d", p=P)).then_inc(x_loaded[b], 16)
            act.dma_start(w_ada[:, 0, :], a["L0_cond_Wada"]).then_inc(w_first, 16)
            act.dma_start(w_ada[:, 1, :], a["L2_cond_Wc"]).then_inc(w_rest, 16)
            act.dma_start(w_ada[:, 2, :], a["L3_cond_W_mod"]).then_inc(w_rest, 16)
            act.preload_act_table_set(LOG_EXP)
            act.wait_ge(cols_ready, 1)
            act.wait_ge(const_first, 1)
            c = cols[:, COL["cond"]:COL["cond"] + NB]
            nc.scalar.activation(silu[:, 0, :], c, ACT.Exp, scale=-1.0).then_inc(silu_act, 1)

        def adaptive_scales(dve, layer, half, signal, done):
            sh, sc, gt = (mods[:, 6 * layer + 3 * half + i, :] for i in range(3))
            scale, bias = ln_g[:, layer, half, :], ln_b[:, layer, half, :]
            nc.vector.tensor_scalar_add(scale, sc, 1.0).then_inc(signal, 1)
            if layer == 0:
                dve.wait_ge(signal, done + 1)
                nc.vector.scalar_tensor_tensor(out=bias, in0=scale, scalar=col(f"be{half + 1}"), in1=sh,
                                               op0=ALU.mult, op1=ALU.add).then_inc(signal, 1)
                dve.wait_ge(signal, done + 2)
                nc.vector.tensor_scalar(scale, scale, col(f"g{half + 1}"), None, ALU.mult).then_inc(signal, 1)
                return done + 3
            nc.vector.tensor_copy(bias, sh).then_inc(signal, 1)
            return done + 2

        def setup_dve(dve):
            nc.vector.memset(mean_mat[:], 1.0 / D)
            nc.vector.memset(eps[:, 0:1], LN_EPS[0])
            nc.vector.memset(eps[:, 1:2], LN_EPS[1])
            nc.vector.memset(zero_col[:], 0.0)
            nc.vector.memset(temp[:], 1.0)
            nc.vector.memset(w_att1[:], 0.0).then_inc(const_first, 1)
            nc.vector.memset(k_stack[96:P, :, :], MAXC)
            nc.vector.memset(v_pad[:, :, :, :, 0:DH], 0.0)
            nc.vector.memset(v_pad[:, :, :, :, DH:DH + 1], 1.0)
            nc.vector.memset(v_pad[:, :, :, :, DH + 1:VW], 0.0)
            nc.vector.memset(neg_max[:], 0.0).then_inc(const_made, 1)
            nc.vector.memset(den_ones[:], 1.0 / SUMC)
            nc.vector.memset(neg_max3[:], 0.0)
            nc.vector.memset(r_parts[:], 0.0)
            nc.vector.memset(k_b[DW:96, :, :, :], MAXC).then_inc(const_made, 1)
            dve.wait_ge(ident_made, 1)
            dve.wait_ge(const_first, 1)
            nc.vector.tensor_tensor(out=centre_mat[:, :], in0=ident[:, :], in1=mean_mat[:, :], op=ALU.subtract).then_inc(const_made, 1)
            dve.wait_ge(vec_turned, 1)
            nc.vector.tensor_copy(cols[:, 0:NFIRST], ps[:, 7, 0:NFIRST]).then_inc(cols_ready, 1)
            for b in range(NB):
                dve.wait_ge(x_turned, b + 1)
                nc.vector.tensor_copy(xT[:, b, :], ps[:, 1 + b, :]).then_inc(xT_ready, 1)
            dve.wait_ge(silu_act, 1)
            nc.vector.tensor_scalar_add(silu[:, 1, :], silu[:, 0, :], 1.0).then_inc(silu_dve, 1)
            dve.wait_ge(silu_dve, 1)
            nc.vector.reciprocal(silu[:, 2, :], silu[:, 1, :]).then_inc(silu_dve, 1)
            dve.wait_ge(silu_dve, 2)
            dve.wait_ge(cols_ready, 1)
            nc.vector.tensor_tensor(out=silu[:, 0, :], in0=silu[:, 2, :],
                                    in1=cols[:, COL["cond"]:COL["cond"] + NB], op=ALU.mult).then_inc(silu_dve, 1)

        def mods0_dve(dve):
            dve.wait_ge(mods_ps0, 1)
            for b in range(NB):
                nc.vector.tensor_tensor(out=mods[:, 0:6, b], in0=ps[:, 3, 0:12].rearrange("p (c b) -> p c b", b=NB)[:, :, b],
                                        in1=cols[:, COL["ada0"]:COL["ada0"] + 6], op=ALU.add).then_inc(mods_done0, 1)
            dve.wait_ge(mods_done0, 2)
            adaptive_scales(dve, 0, 0, mods_done0, 2)
            dve.wait_ge(mods_done0, N_MODS_DONE0)

        def mods_dve(dve):
            dve.wait_ge(const_pool, N_POOL_CONST)
            nc.vector.reduce_sum(headmask[:, :], head_of[:, :, :], AX_X).then_inc(const_made, 1)
            dve.wait_ge(vec_turned, 2)
            nc.vector.tensor_copy(cols[:, NFIRST:NCOL], ps[:, 7, P + NFIRST:P + NCOL]).then_inc(cols_ready, 1)
            dve.wait_ge(mods_ps, 1)
            dve.wait_ge(cols_ready, 2)
            ada = cols[:, COL["ada2"]:COL["ada2"] + 12]
            for b in range(NB):
                nc.vector.tensor_tensor(out=mods[:, 6:18, b], in0=ps[:, 3, 12:36].rearrange("p (c b) -> p c b", b=NB)[:, :, b],
                                        in1=ada, op=ALU.add).then_inc(mods_done, 1)
            nc.vector.tensor_tensor(out=bo2[:, :], in0=ps[:, 3, 36:37], in1=col("bo"), op=ALU.add).then_inc(mods_done, 1)
            dve.wait_ge(mods_done, 3)

        def vectors_dve(dve):
            for h in range(2):
                nc.vector.tensor_scalar(k_b[DW:96, :, h, :], k_b[DW:96, :, h, :], ident[DW:96, DW + h:DW + h + 1], None,
                                        ALU.mult).then_inc(const_made, 1)
            nc.vector.tensor_copy(counts[:, :], counts_i[:, :]).then_inc(const_made, 1)
            done = 3
            for layer in range(3):
                for half in range(2):
                    if layer or half:
                        done = adaptive_scales(dve, layer, half, mods_done, done)
                    branch = [["bproj", "L0b2"], [None, "L2b2"], ["bout", "L3b2"]][layer][half]
                    nc.vector.tensor_scalar(gate_b[:, layer, half, :], mods[:, 6 * layer + 3 * half + 2, :],
                                            bo2[:, :] if branch is None else col(branch), None, ALU.mult).then_inc(mods_done, 1)
                    done += 1
            dve.wait_ge(mods_done, done)
            assert done == N_MODS_DONE

        def mods_matmuls(layer, n0):
            for c in range(6):
                n = n0 + 2 * c
                last = nc.tensor.matmul(ps[:, 3, n:n + 2], w_ada[:, layer, c * D:(c + 1) * D], silu[:, 0, :],
                                        start=True, stop=True)
            return last

        def setup_pe(pe):
            pe.wait_ge(ident_made, 1)
            pe.wait_ge(rows_first, 16 * FIRST)
            nc.tensor.transpose(ps[:, 7, 0:NFIRST], vec_rows[0:NFIRST, :], ident[0:NFIRST, 0:NFIRST]).then_inc(vec_turned, 1)
            for b in range(NB):
                pe.wait_ge(x_loaded[b], 16)
                for k in range(KT):
                    last = nc.tensor.transpose(ps[:, 1 + b, k * P:(k + 1) * P], x_rows[:, 4 * b, k * P:(k + 1) * P],
                                               ident[:, :])
                last.then_inc(x_turned, 1)
            pe.wait_ge(const_made, 3)

        def mods0_pe(pe):
            pe.wait_ge(w_first, 32)
            pe.wait_ge(silu_dve, 3)
            mods_matmuls(0, 0).then_inc(mods_ps0, 1)

        def mods_pe(pe):
            pe.wait_ge(rows_rest, 16 * (len(VECTORS) - FIRST + 3))
            nc.tensor.transpose(ps[:, 7, P:P + NCOL], vec_rows[:, :], ident[0:NCOL, 0:NCOL]).then_inc(vec_turned, 1)
            pe.wait_ge(w_rest, 48)
            mods_matmuls(1, 12)
            mods_matmuls(2, 24)
            pe.wait_ge(cols_ready, 2)
            nc.tensor.matmul(ps[:, 3, 36:37], w_o2[:, :], col("bv"), start=True, stop=True).then_inc(mods_ps, 1)

        ln_centred, ln_squared = sem("ln_centred"), sem("ln_squared")
        ln_var, ln_log, ln_rstd = sem("ln_var"), sem("ln_log"), sem("ln_rstd")
        ln_normed, ln_out = sem("ln_normed"), sem("ln_out")

        class LayerNorm:

            def __init__(self, k, eps_i, scale, bias, dst=None):
                self.k, self.eps_i, self.scale, self.bias, self.dst = k, eps_i, scale, bias, xm if dst is None else dst

            def count(self, b):
                return NB * self.k + b + 1

            def centre(self, pe, b, stream_ready=None):
                if stream_ready:
                    pe.wait_ge(stream_ready, b + 1)
                nc.tensor.matmul(ps[:, 4 * b, :], centre_mat[:, :], xT[:, b, :], start=True, stop=True).then_inc(ln_centred, 1)

            def variance(self, pe, b):
                pe.wait_ge(ln_squared, self.count(b))
                nc.tensor.matmul(ps[:, 4 * b + 1, :], mean_mat[:, :], sq[:, b, :], start=True, stop=True).then_inc(ln_var, 1)

            def pe(self, pe, stream_ready=None):
                for b in range(NB):
                    self.centre(pe, b, stream_ready)
                for b in range(NB):
                    self.variance(pe, b)

            def square(self, act, b):
                act.wait_ge(ln_centred, self.count(b))
                nc.scalar.activation(sq[:, b, :], ps[:, 4 * b, :], ACT.Square).then_inc(ln_squared, 1)

            def rstd(self, act, b):
                act.wait_ge(ln_var, self.count(b))
                nc.scalar.activation(rs[:, b, :], ps[:, 4 * b + 1, :], ACT.Ln,
                                     bias=eps[:, self.eps_i:self.eps_i + 1]).then_inc(ln_log, 1)
                act.wait_ge(ln_log, self.count(b))
                nc.scalar.activation(rs[:, b, :], rs[:, b, :], ACT.Exp, scale=-0.5).then_inc(ln_rstd, 1)

            def act(self, act):
                for b in range(NB):
                    self.square(act, b)
                for b in range(NB):
                    self.rstd(act, b)

            def act_skewed(self, act):
                for b in range(NB):
                    self.square(act, b)
                    self.rstd(act, b)

            def apply(self, dve, b):
                dve.wait_ge(ln_rstd, self.count(b))
                nc.vector.tensor_tensor(out=xc[:, b, :], in0=ps[:, 4 * b, :], in1=rs[:, b, :],
                                        op=ALU.mult).then_inc(ln_normed, 1)
                dve.wait_ge(ln_normed, self.count(b))
                nc.vector.tensor_scalar(self.dst[:, b, :], xc[:, b, :], self.scale(b), self.bias(b), ALU.mult,
                                        ALU.add).then_inc(ln_out, 1)

            def dve(self, dve, beside=None):
                if beside:
                    beside(dve)
                for b in range(NB):
                    self.apply(dve, b)

        def adaptive_norm(k, layer, half):
            return LayerNorm(k, 0, lambda b: ln_g[:, layer, half, b:b + 1], lambda b: ln_b[:, layer, half, b:b + 1])

        class Mlp:

            def __init__(self, layer, norm, b1):
                self.layer, self.norm, self.b1 = layer, norm, b1
                self.up_ps, self.hid_ready = sem(f"up_ps{layer}"), sem(f"hid_ready{layer}")
                self.down_ps, self.biased = sem(f"down_ps{layer}"), sem(f"biased{layer}")
                self.stream = sem(f"stream_mlp{layer}")

            def up(self, pe, b, m):
                if m == 0:
                    pe.wait_ge(ln_out, self.norm.count(b))
                nc.tensor.matmul(ps[:, 4 * b + m, :], w_up[:, self.layer, m * P:(m + 1) * P], xm[:, b, :],
                                 start=True, stop=True).then_inc(self.up_ps, 1)

            def down(self, pe, b, m):
                pe.wait_ge(self.hid_ready, MLP * b + m + 1)
                last = nc.tensor.matmul(ps[:, 4 * b, :], w_down[:, self.layer, m, :], hid[:, b, m, :],
                                        start=(m == 0), stop=(m == MLP - 1))
                if m == MLP - 1:
                    last.then_inc(self.down_ps, 1)

            def norm_up(self, pe, stream):
                self.norm.centre(pe, 1, stream)
                self.up(pe, 0, 0)
                self.norm.variance(pe, 1)
                for b, m in [(0, m) for m in range(1, MLP)] + [(1, m) for m in range(MLP)]:
                    self.up(pe, b, m)

            def downs(self, pe):
                for b in range(NB):
                    for m in range(MLP):
                        self.down(pe, b, m)

            def act(self, act):
                for b in range(NB):
                    for m in range(MLP):
                        act.wait_ge(self.up_ps, MLP * b + m + 1)
                        nc.scalar.activation(hid[:, b, m, :], ps[:, 4 * b + m, :], ACT.Gelu,
                                             bias=col(self.b1, m)).then_inc(self.hid_ready, 1)
                act.preload_act_table_set(LOG_EXP)

            def pool(self, pool):
                for b in range(NB):
                    pool.wait_ge(ln_out, self.norm.count(b))
                    nc.gpsimd.tensor_scalar(xb[:, b, :], xT[:, b, :], gate_b[:, self.layer, 1, b:b + 1], None,
                                            ALU.add).then_inc(self.biased, 1)

            def dve(self, dve, behind=None):
                for b in range(NB):
                    dve.wait_ge(self.down_ps, b + 1)
                    dve.wait_ge(self.biased, b + 1)
                    nc.vector.scalar_tensor_tensor(out=xT[:, b, :], in0=ps[:, 4 * b, :],
                                                   scalar=mods[:, 6 * self.layer + 5, b:b + 1], in1=xb[:, b, :],
                                                   op0=ALU.mult, op1=ALU.add).then_inc(self.stream, 1)
                    if behind:
                        behind(dve, b)

        class Projections:

            def __init__(self, layer, norm, wq, wk, wv, bq, bk):
                self.layer, self.norm, self.w, self.bias = layer, norm, (wq, wk, wv), (bq, bk)
                self.qk_ps, self.hi_ready = sem(f"qk_ps{layer}"), sem(f"hi_ready{layer}")
                self.lo_ready, self.v_ps = sem(f"lo_ready{layer}"), sem(f"v_ps{layer}")
                self.v_ready = sem(f"v_ready{layer}")
                self.stored = [sem(f"stored{layer}_{b}") for b in range(NB)]

            def pe(self, pe):
                for b in range(NB):
                    pe.wait_ge(ln_out, self.norm.count(b))
                    for i in range(2):
                        nc.tensor.matmul(ps[:, 4 * b + i, :], self.w[i], xm[:, b, :], start=True,
                                         stop=True).then_inc(self.qk_ps, 1)
                    for k in range(KT):
                        last = nc.tensor.matmul(ps[:, 4 * b + 2, k * P:(k + 1) * P], xm[:, b, k * P:(k + 1) * P], self.w[2],
                                                start=True, stop=True)
                    last.then_inc(self.v_ps, 1)

            def act(self, act):
                for b in range(NB):
                    for i, hi in enumerate((q_hi, k_hi)):
                        act.wait_ge(self.qk_ps, 2 * b + i + 1)
                        nc.scalar.activation(hi[:, b, :], ps[:, 4 * b + i, :], ACT.Identity,
                                             bias=self.bias[i]).then_inc(self.hi_ready, 1)
                    act.wait_ge(self.v_ps, b + 1)
                    nc.scalar.copy(v_all[:, b, :, :, :].rearrange("p g k n -> p k g n"),
                                   ps[:, 4 * b + 2, :].rearrange("p (k g n) -> p k g n", k=KT, g=NG)).then_inc(self.v_ready, 1)

            def dve(self, dve):
                for b in range(NB):
                    for i, (hi, lo) in enumerate(((q_hi, q_lo), (k_hi, k_lo))):
                        dve.wait_ge(self.hi_ready, 2 * b + i + 1)
                        nc.vector.scalar_tensor_tensor(out=lo[:, b, :], in0=ps[:, 4 * b + i, :], scalar=self.bias[i],
                                                       in1=hi[:, b, :], op0=ALU.add, op1=ALU.subtract).then_inc(self.lo_ready, 1)

            def sp(self, sp):
                for b in range(NB):
                    for i, (parts, sem_) in enumerate((((q_hi, q_lo, q_hi), 0), ((k_hi, k_hi, k_lo), 1))):
                        self.wait_parts(sp, 2 * b + i + 1)
                        for part, tile in enumerate(parts):
                            sp.dma_start(scratch[self.layer][i, part, b * P:(b + 1) * P, :], tile[:, b, :]).then_inc(self.stored[b], 16)

            def wait_parts(self, sp, count):
                sp.wait_ge(self.hi_ready, count)
                sp.wait_ge(self.lo_ready, count)

            def wait_stored(self, sp, b):
                sp.wait_ge(self.stored[b], 16 * 6)

        def attention8(layer, causal, scale, proj):
            loaded = [sem(f"km_loaded{layer}_{s}") for s in range(2)]
            q_loaded = [sem(f"qe_loaded{layer}_{s}") for s in range(2)]
            k_made = sem(f"k_made{layer}")
            v_made = sem(f"v_made{layer}")
            max_ps = sem(f"max_ps{layer}")
            max_taken = sem(f"max_taken{layer}")
            max_turned = sem(f"max_turned{layer}")
            max_in = sem(f"max_in{layer}")
            score_ps = sem(f"score_ps{layer}")
            exp_done = sem(f"exp_done{layer}")
            pv_done = sem(f"pv_done{layer}")
            out_free = sem(f"out_free{layer}")

            width = [T - P * k for k in range(KT)] if causal else [T] * KT
            start = [0, T, 2 * T, 2 * T + width[2]]
            seen = [P * (t + 1) for t in range(KT)] if causal else [T] * KT

            def max_bank(n, first):
                return n % 4 if first else (0, 1, 6)[(n if n < 2 else n + 1) % 3]

            def pe_maxima(pe, i, s, j, t, first=False):
                if t == 0:
                    pe.wait_ge(k_made, i * GH + j + 1)
                n = 4 * j + t
                if first and n >= 4:
                    pe.wait_ge(max_taken, n - 3)
                elif not first and n == 4:
                    pe.wait_ge(max_in, i)
                elif not first:
                    pe.wait_ge(max_taken, i * 16 + {0: -1, 1: 0, 2: 1, 3: 2}.get(n, n - 2))
                dst = ps[:, max_bank(n, first), 0:seen[t]]
                last = nc.tensor.matmul(dst, q_max[:, s, t * P:(t + 1) * P], k_head[0:96, s, j, 0:seen[t]],
                                        start=True, stop=not causal)
                if causal:
                    last = nc.tensor.matmul(dst[:, t * P:(t + 1) * P], ident16[:, :], mask_q[:, :], start=False, stop=True)
                last.then_inc(max_ps, 1)

            def pe_turn(pe, i, s, first=False):
                pe.wait_ge(max_taken, i * 16 + 16)
                if not first:
                    pe.wait_ge(max_in, i)
                for t in range(KT):
                    last = nc.tensor.transpose(ps[0:VW, 6, t * P:(t + 1) * P], neg_max[:, s, t, :], ident[:, :])
                last.then_inc(max_turned, 1)

            def pe_scores(pe, i, s, uses, j, half, first=False):
                if j == 0 and half == 0:
                    pe.wait_ge(max_in, i + 1)
                    pe.wait_ge(q_loaded[s], uses * 16 + (0 if s else 32))
                n = 2 * j + half
                if not (first and n < 2):
                    pe.wait_ge(exp_done, i * 8 + n - 1)
                for k in (2 * half, 2 * half + 1):
                    off = start[k] - start[2 * half]
                    bank = 2 + 2 * half + off // T
                    dst = ps[:, bank, off % T:off % T + width[k]]
                    last = nc.tensor.matmul(dst, k_head[:, s, j, k * P:(k + 1) * P], q_exp[:, s, T - width[k]:T],
                                            start=True, stop=not causal)
                    if causal:
                        last = nc.tensor.matmul(dst[:, 0:P], ident16[:, :], mask_k[:, :], start=False, stop=True)
                last.then_inc(score_ps, 1)

            def pe_values(pe, i, s, k):
                if k == 0:
                    pe.wait_ge(exp_done, i * 8 + 8)
                    pe.wait_ge(v_made, i + 1)
                    pe.wait_ge(out_free, i + 1)
                for j in range(GH):
                    last = nc.tensor.matmul(ps[VW * j:VW * (j + 1), 7, T - width[k]:T], v_pad[:, s, k, j, :],
                                            probs[:, s, j, start[k]:start[k] + width[k]],
                                            start=(k == 0), stop=(k == KT - 1))
                if k == KT - 1:
                    last.then_inc(pv_done, 1)

            def pe_body(pe, i, s, uses, maxima=True, scores=True, values=True, first=False):
                def next_maxima(j, t):
                    if maxima:
                        pe_maxima(pe, i + 1, 1 - s, j, t)

                next_maxima(0, 0)
                next_maxima(0, 1)
                if scores:
                    pe_turn(pe, i, s, first)
                next_maxima(0, 2)
                if values:
                    pe_values(pe, i - 1, 1 - s, 0)
                next_maxima(0, 3)
                if scores:
                    pe_scores(pe, i, s, uses, 0, 0, first)
                    pe_scores(pe, i, s, uses, 0, 1, first)
                for j in range(1, GH):
                    next_maxima(j, 0)
                    next_maxima(j, 1)
                    if values:
                        pe_values(pe, i - 1, 1 - s, j)
                    if scores:
                        pe_scores(pe, i, s, uses, j, 0, first)
                    next_maxima(j, 2)
                    next_maxima(j, 3)
                    if scores:
                        pe_scores(pe, i, s, uses, j, 1, first)

            def dve_keys(dve, i, s, uses, j, reuse):
                if j == 0:
                    dve.wait_ge(loaded[s], uses * 32 + 64)
                if reuse:
                    dve.wait_ge(score_ps, i * 8 - 16 + 2 * j + 2)
                nc.vector.tensor_scalar(k_head[:, s, j, :], k_stack[:, s, :], headmask[:, j:j + 1], None,
                                        ALU.mult).then_inc(k_made, 1)

            def dve_max_head(dve, i, s, j, reuse, first=False):
                if j == 0 and reuse:
                    dve.wait_ge(max_turned, i - 1)
                for t in range(KT):
                    n = 4 * j + t
                    dve.wait_ge(max_ps, i * 16 + n + 1)
                    nc.vector.tensor_reduce(neg_max[:, s, t, DH * j:DH * j + 1], ps[:, max_bank(n, first), 0:seen[t]], AX_X, ALU.max,
                                            negate=True).then_inc(max_taken, 1)

            def act_body(act, i, s, output=True):
                act.wait_ge(max_turned, i + 1)
                nc.scalar.mul(q_exp[96:P, s, :], ps[0:VW, 6, :], 1.0 / MAXC).then_inc(max_in, 1)
                act.wait_ge(pv_done, i + 1)
                for j in range(GH):
                    for half in range(2):
                        if output and j == GH - 1 and half == 1:
                            act_output(act, i - 1)
                        act.wait_ge(score_ps, i * 8 + 2 * j + half + 1)
                        n = sum(width[2 * half:2 * half + 2])
                        src = ps[:, 2 + 2 * half:4 + 2 * half, :].rearrange("p n t -> p (n t)")[:, 0:n]
                        at = start[2 * half]
                        nc.scalar.activation(probs[:, s, j, at:at + n], src, ACT.Exp, scale=scale).then_inc(exp_done, 1)

            def act_output(act, i):
                act.wait_ge(pv_done, i + 3)
                nc.scalar.copy(att_out[:, i, :], ps[:, 7, :]).then_inc(out_free, 1)

            def sp_load_max(sp, i, s):
                for dst, kind, rows in ((k_stack[0:96, s, :], 1, 96), (q_max[:, s, :], 0, 96)):
                    src = scratch[layer][kind].rearrange("a (i r) t -> i a r t", r=VW)[i]
                    sp.dma_start(dst, src).then_inc(loaded[s], 16)

            def sp_load_exp(sp, i, s):
                src = scratch[layer][0].rearrange("a (i r) t -> i a r t", r=VW)[i]
                sp.dma_start(q_exp[0:96, s, :], src).then_inc(q_loaded[s], 16)

            def sp_program(sp):
                def body(i, s, ahead2, ahead1, first=False):
                    if ahead2:
                        sp.wait_ge(k_made, i * GH + GH)
                        sp.wait_ge(max_ps, i * 16 + 16)
                        sp_load_max(sp, i + 2, s)
                    if ahead1:
                        if not first:
                            sp.wait_ge(score_ps, i * 8)
                        sp_load_exp(sp, i + 1, 1 - s)

                q_parts, k_parts = (q_hi, q_lo, q_hi), (k_hi, k_hi, k_lo)
                for i in range(2):
                    for dst, parts, count in ((q_max, q_parts, 1), (k_stack, k_parts, 2)):
                        proj.wait_parts(sp, count)
                        for n, part in enumerate(parts):
                            sp.dma_start(dst[VW * n:VW * (n + 1), i, :], part[VW * i:VW * (i + 1), 0, :]).then_inc(loaded[i], 16)
                for n, part in enumerate(q_parts):
                    sp.dma_start(q_exp[VW * n:VW * (n + 1), 0, :], part[0:VW, 0, :]).then_inc(q_loaded[0], 16)
                proj.sp(sp)
                proj.wait_stored(sp, 0)
                body(0, 0, True, True, first=True)
                proj.wait_stored(sp, 1)
                with sp.Fori(0, 2) as r:
                    for u in range(2):
                        body(r * 2 + (u + 1), (u + 1) % 2, True, True)
                body(5, 1, True, True)
                body(6, 0, False, True)

            def pool_program(pool):
                def body(i, s, reuse):
                    if reuse:
                        pool.wait_ge(pv_done, i + 1)
                    nc.gpsimd.tensor_copy(
                        v_pad[:, s, :, :, 0:DH],
                        v_all.rearrange("p b g k (j d) -> p (b g) k j d", d=DH)[:, i, :, :, :]).then_inc(v_made, 1)

                pool.wait_ge(const_made, 1)
                pool.wait_ge(proj.v_ready, NB)
                for i in range(2):
                    body(i, i, False)
                with pool.Fori(0, 3) as r:
                    for u in range(2):
                        body(r * 2 + (u + 2), u, True)

            def dve_program(dve):
                def body(i, s, uses_next, reuse_max, reuse_key, keys=True):
                    for j in range(GH):
                        dve_max_head(dve, i, s, j, reuse_max)
                        if keys:
                            dve_keys(dve, i + 1, 1 - s, uses_next, j, reuse_key)

                for j in range(GH):
                    dve_keys(dve, 0, 0, 1, j, False)
                for j in range(GH):
                    dve_max_head(dve, 0, 0, j, False, first=True)
                for j in range(GH):
                    dve_keys(dve, 1, 1, 1, j, False)
                body(1, 1, 2, False, True)
                with dve.Fori(0, 2) as r:
                    body(r * 2 + 2, 0, r + 2, True, True)
                    body(r * 2 + 3, 1, r + 3, True, True)
                body(6, 0, 4, True, True)
                body(7, 1, None, True, True, keys=False)

            def act_program(act, before_last):
                act_body(act, 0, 0, output=False)
                with act.Fori(0, 3) as r:
                    act_body(act, r * 2 + 1, 1)
                    act_body(act, r * 2 + 2, 0)
                act_body(act, 7, 1)
                before_last(act)
                act_output(act, 7)

            def pe_program(pe, before_last):
                pe.sem_inc(pv_done, 2)
                pe.sem_inc(out_free, 1)
                pe.wait_ge(const_pool, 4)
                pe.wait_ge(proj.lo_ready, 2 * NB)
                pe.wait_ge(proj.v_ready, NB)
                for j in range(GH):
                    for t in range(KT):
                        pe_maxima(pe, 0, 0, j, t, first=True)
                pe_body(pe, 0, 0, 1, values=False, first=True)
                with pe.Fori(0, 3) as r:
                    pe_body(pe, r * 2 + 1, 1, r + 1)
                    pe_body(pe, r * 2 + 2, 0, r + 2)
                pe_body(pe, 7, 1, 4, maxima=False)
                pe.wait_ge(out_free, NG + 1)
                before_last(pe)
                pe_body(pe, 8, 0, None, maxima=False, scores=False)
                pe.wait_ge(out_free, NGRP + 1)

            return sp_program, pool_program, dve_program, act_program, pe_program

        class Join8:

            def __init__(self, layer, index, wo):
                self.layer, self.index, self.wo = layer, index, wo
                self.picked, self.log, self.inv = sem(f"picked{layer}"), sem(f"den_log{layer}"), sem(f"den_inv{layer}")
                self.normed, self.proj_ps = sem(f"att_normed{layer}"), sem(f"proj_ps{layer}")
                self.biased, self.stream = sem(f"att_biased{layer}"), sem(f"stream_att{layer}")

            def pick(self, pe, b):
                for sel, bank in ((den_sel, 1), (num_sel, 0)):
                    for g in range(NG):
                        last = nc.tensor.matmul(ps[VW * g:VW * (g + 1), 4 * b + bank, :], sel[:, :],
                                                att_out[:, NG * b + g, :], start=True, stop=True)
                    last.then_inc(self.picked, 1)

            def project(self, pe, b):
                pe.wait_ge(self.normed, b + 1)
                nc.tensor.matmul(ps[:, 4 * b + 2, :], self.wo, xc[:, b, :], start=True, stop=True).then_inc(self.proj_ps, 1)

            def pe(self, pe, mlp):
                self.project(pe, 0)
                self.pick(pe, 1)
                mlp.norm.centre(pe, 0, self.stream)
                self.project(pe, 1)
                mlp.norm.variance(pe, 0)
                mlp.norm_up(pe, self.stream)
                mlp.downs(pe)

            def act(self, act, b):
                act.wait_ge(self.picked, 2 * b + 1)
                nc.scalar.activation(rs[:, b, :], ps[:, 4 * b + 1, :], ACT.Ln).then_inc(self.log, 1)
                act.wait_ge(self.log, b + 1)
                nc.scalar.activation(rs[:, b, :], rs[:, b, :], ACT.Exp, scale=-1.0).then_inc(self.inv, 1)

            def pool(self, pool):
                for b in range(NB):
                    nc.gpsimd.tensor_scalar(xb[:, b, :], xT[:, b, :], gate_b[:, self.index, 0, b:b + 1], None,
                                            ALU.add).then_inc(self.biased, 1)

            def dve(self, dve):
                for b in range(NB):
                    dve.wait_ge(self.picked, 2 * b + 2)
                    dve.wait_ge(self.inv, b + 1)
                    nc.vector.tensor_tensor(out=xc[:, b, :], in0=ps[:, 4 * b, :], in1=rs[:, b, :],
                                            op=ALU.mult).then_inc(self.normed, 1)
                    dve.wait_ge(self.proj_ps, b + 1)
                    dve.wait_ge(self.biased, b + 1)
                    nc.vector.scalar_tensor_tensor(out=xT[:, b, :], in0=ps[:, 4 * b + 2, :],
                                                   scalar=mods[:, 6 * self.index + 2, b:b + 1], in1=xb[:, b, :],
                                                   op0=ALU.mult, op1=ALU.add).then_inc(self.stream, 1)

        norm0a = adaptive_norm(0, 0, 0)
        proj0 = Projections(0, norm0a, w_qkv0[:, 0:D], w_qkv0[:, D:2 * D], w_qkv0[:, 2 * D:3 * D], zero_col[:, :], zero_col[:, :])
        sp_att0, pool_att0, dve_att0, act_att0, pe_att0 = attention8(0, True, DH ** -0.5, proj0)

        join0 = Join8(0, 0, w_o0[:, :])
        norm0b = adaptive_norm(1, 0, 1)
        mlp0 = Mlp(0, norm0b, "L0b1")

        att_ps, att_bias, att_exp = sem("att_ps"), sem("att_bias"), sem("att_exp")
        ratio, cum_ready = sem("ratio"), sem("cum_ready")
        val_ps, rep_ps, val_ready, scaled = sem("val_ps"), sem("rep_ps"), sem("val_ready"), sem("scaled")
        op_ps, op_ready, ff1_ps, ff1_ready = sem("op_ps"), sem("op_ready"), sem("ff1_ps"), sem("ff1_ready")
        ff2_ps, stream1, op_step = sem("ff2_ps"), sem("stream1"), sem("op_step")
        norm1 = LayerNorm(2, 1, lambda b: col("gamma"), lambda b: col("beta"), dst=xT)
        norm2a = adaptive_norm(3, 1, 0)
        proj2 = Projections(2, norm2a, w_qkv2[:, 0, :], w_qkv2[:, 1, :], w_qkv2[:, 2, :], col("bq"), col("bk"))
        RATIO_STEPS = 14

        cum = hid[:, :, 1, :]
        att1, den1, rat1, tmp1 = (hid[0:NB * VW, b, m, :] for b in range(NB) for m in (2, 3))
        part1 = [tile[0:NB * VW, 0, :].bitcast(BF16) for tile in (q_hi, q_lo, k_hi)]
        vals = big[:, 0, :, :].rearrange("p g (n t) -> p (g n) t", t=T)
        scaled1 = big[:, 1, 0:2, :].rearrange("p s (b t) -> p b s t", t=T)
        opT = big[:, 1, 2, :].rearrange("p (b t) -> p b t", t=T)
        resT = big[:, 1, 3, :].rearrange("p (b t) -> p b t", t=T)

        def additive_pe(pe):
            for b in range(NB):
                pe.wait_ge(mlp0.stream, b + 1)
                nc.tensor.matmul(ps[VW * b:VW * (b + 1), 1, :], w_att1[:, :], xT[:, b, :], start=True, stop=True).then_inc(att_ps, 1)
            for n in range(NB * NC):
                c, b = n // NB, n % NB
                if c == 0:
                    pe.wait_ge(cum_ready, b + 1)
                else:
                    pe.wait_ge(val_ready, n - 1)
                nc.tensor.matmul(ps[:, 4 * b, :], w_val1[:, c * P:(c + 1) * P], cum[:, b, :], start=True,
                                 stop=True).then_inc(val_ps, 1)
            pe.wait_ge(val_ready, NB * NC)
            pe.wait_ge(ratio, RATIO_STEPS)
            for n in range(2):
                repeat_pe(n)
            for n in range(NB * NC):
                pe.wait_ge(scaled, n + 1)
                if n + 2 < NB * NC:
                    repeat_pe(n + 2)
                else:
                    b = n % NB
                    nc.tensor.matmul(ps[:, 4 * b, :], w_ff1[:, 0, :], xT[:, b, :], start=True, stop=False)
                c, b = n // NB, n % NB
                last = nc.tensor.matmul(ps[:, 4 * b + 3, :], w_op1[:, c, :], scaled1[:, b, c % 2, :],
                                        start=(c == 0), stop=(c == NC - 1))
                last.then_inc(op_ps if c == NC - 1 else op_step, 1)
            for b in range(NB):
                pe.wait_ge(op_ready, b + 1)
                nc.tensor.matmul(ps[:, 4 * b, :], w_ff1[:, 1, :], opT[:, b, :], start=False, stop=True).then_inc(ff1_ps, 1)
            for b in range(NB):
                pe.wait_ge(ff1_ready, b + 1)
                nc.tensor.matmul(ps[:, 4 * b + 1, :], w_ff2[:, :], resT[:, b, :], start=True, stop=True).then_inc(ff2_ps, 1)

        def repeat_pe(n):
            c, b = n // NB, n % NB
            nc.tensor.matmul(ps[:, 4 * b + 1, :], pair_sel[:, c, :, :].rearrange("p a b -> p (a b)"), r_parts[:, b, :],
                             start=True, stop=True).then_inc(rep_ps, 1)

        def additive_act(act):
            act.wait_ge(att_bias, 2)
            nc.scalar.activation(att1, ps[0:NB * VW, 1, :], ACT.Exp, scale=temp[:, :], bias=amax[:, 1:2]).then_inc(att_exp, 1)
            for n in range(NB * NC):
                act.wait_ge(val_ps, n + 1)
                nc.scalar.copy(vals[:, n, :], ps[:, 4 * (n % NB), :]).then_inc(val_ready, 1)
            for b in range(NB):
                act.wait_ge(op_ps, b + 1)
                nc.scalar.activation(opT[:, b, :], ps[:, 4 * b + 3, :], ACT.Identity, bias=col("cond", b)).then_inc(op_ready, 1)
            for b in range(NB):
                act.wait_ge(ff1_ps, b + 1)
                nc.scalar.activation(resT[:, b, :], ps[:, 4 * b, :], ACT.Relu, bias=col("ff1b")).then_inc(ff1_ready, 1)

        def running_sum(dve, b):
            dve.wait_ge(mlp0.stream, b + 1)
            nc.vector.tensor_tensor_scan(cum[:, b, :], ones_row[:, :], xT[:, b, :], 0.0, ALU.mult, ALU.add).then_inc(cum_ready, 1)

        def additive_dve(dve):
            dve.wait_ge(att_ps, NB)
            nc.vector.tensor_reduce(amax[:, 0:1], ps[0:NB * VW, 1, :], AX_X, ALU.max, negate=True).then_inc(att_bias, 1)
            dve.wait_ge(att_bias, 1)
            nc.vector.tensor_tensor(out=amax[:, 1:2], in0=amax[:, 0:1], in1=temp[:, :], op=ALU.mult).then_inc(att_bias, 1)
            dve.wait_ge(att_exp, 1)
            done = 0

            def step(ins):
                nonlocal done
                done += 1
                ins.then_inc(ratio, 1)
                dve.wait_ge(ratio, done)

            step(nc.vector.tensor_tensor(out=den1, in0=att1, in1=counts[:, :], op=ALU.mult))
            step(nc.vector.tensor_scalar_add(den1, den1, 1e-30))
            step(nc.vector.reciprocal(rat1, den1))
            step(nc.vector.tensor_tensor(out=rat1, in0=rat1, in1=att1, op=ALU.mult))
            step(nc.vector.tensor_copy(part1[0], rat1))
            step(nc.vector.tensor_tensor(out=tmp1, in0=rat1, in1=part1[0], op=ALU.subtract))
            step(nc.vector.tensor_copy(part1[1], tmp1))
            step(nc.vector.tensor_tensor(out=part1[2], in0=tmp1, in1=part1[1], op=ALU.subtract))
            for b in range(NB):
                for i in range(3):
                    nc.vector.tensor_copy(r_parts[VW * i:VW * i + H, b, :], part1[i][VW * b:VW * b + H, :]).then_inc(ratio, 1)
            for n in range(NB * NC):
                c, b = n // NB, n % NB
                dve.wait_ge(rep_ps, n + 1)
                if n == 0:
                    dve.wait_ge(val_ready, NB * NC)
                if c >= 2:
                    dve.wait_ge(op_step, n - 3)
                nc.vector.tensor_tensor(out=scaled1[:, b, c % 2, :], in0=ps[:, 4 * b + 1, :], in1=vals[:, n, :],
                                        op=ALU.mult).then_inc(scaled, 1)
            for b in range(NB):
                dve.wait_ge(ff2_ps, b + 1)
                nc.vector.scalar_tensor_tensor(out=xT[:, b, :], in0=ps[:, 4 * b + 1, :], scalar=col("ff2b"), in1=xT[:, b, :],
                                               op0=ALU.add, op1=ALU.add).then_inc(stream1, 1)

        sp_att2, pool_att2, dve_att2, act_att2, pe_att2 = attention8(2, False, 1.0 / DH, proj2)

        join2 = Join8(2, 1, w_o2[:, :])
        norm2b = adaptive_norm(4, 1, 1)
        mlp2 = Mlp(1, norm2b, "L2b1")
        norm3a = adaptive_norm(5, 2, 0)
        xm_hi_ready, xm_lo_ready = sem("xm_hi_ready"), sem("xm_lo_ready")

        pair_loaded = sem("pair_loaded")
        w_hi_ready, w_lo_ready = sem("w_hi_ready"), sem("w_lo_ready")
        q3_ps, q3_hi, q3_lo = sem("q3_ps"), sem("q3_hi"), sem("q3_lo")
        k3_ps, k3_hi, k3_lo = sem("k3_ps"), sem("k3_hi"), sem("k3_lo")
        v3_ps, v3_ready = sem("v3_ps"), sem("v3_ready")
        placed_a = [[sem(f"placed_a{b}_{h}") for h in range(2)] for b in range(NB)]
        placed_b = [sem(f"placed_b{b}") for b in range(NB)]
        max3_ps, max3_taken = sem("max3_ps"), sem("max3_taken")
        max3_turned, max3_in = sem("max3_turned"), sem("max3_in")
        score3_ps, exp3_done = sem("score3_ps"), sem("exp3_done")
        pair3_sum, key3_sum = sem("pair3_sum"), sem("key3_sum")
        sum3_hi, sum3_lo = sem("sum3_hi"), sem("sum3_lo")
        pv3_ps, den3_ps = sem("pv3_ps"), sem("den3_ps")
        den3_log, den3_inv, pair3_out = sem("den3_log"), sem("den3_inv"), sem("pair3_out")
        inv3 = big[:, 0, 3, 2 * T:3 * T]
        half_sum = big[:, 0, 2, :].rearrange("p (h n) -> p h n", h=2)
        key_sum = big[:, 0, 3, 0:2 * T].rearrange("p (h n) -> p h n", h=2)
        sum_hi, sum_lo = k_head[:, 0, 0:2, :], q_exp
        w_qkv3 = a["L3_cond_W_qkv"].rearrange("d (s c n) -> c d s n", s=3, n=P)

        def pe3_project(pe, v, b, c, i):
            pe.wait_ge(w_lo_ready, c + 1)
            for n, (w, x) in enumerate(((w_hi, xm_hi), (w_lo, xm_hi), (w_hi, xm_lo))):
                last = nc.tensor.matmul(ps[:, i, :], w[:, i, :], x[:, b, :], start=(n == 0), stop=(n == 2))
            last.then_inc((q3_ps, k3_ps)[i], 1)

        def pe3_values(pe, b):
            for k in range(KT):
                for n, (w, x) in enumerate(((w_hi, xm_hi), (w_lo, xm_hi), (w_hi, xm_lo))):
                    last = nc.tensor.matmul(ps[:, 6, k * P:(k + 1) * P], x[:, b, k * P:(k + 1) * P], w[:, 2, :],
                                            start=(n == 0), stop=(n == 2))
            last.then_inc(v3_ps, 1)

        def pe3_maxima(pe, v, b, uses, n, projected=True, first=False):
            h, t = n // KT, n % KT
            if t == 0:
                pe.wait_ge(placed_a[b][h], uses * (4 * 16))
            if first and n >= 4:
                pe.wait_ge(max3_taken, n - 3)
            if n < 2 and projected:
                pe.wait_ge((q3_lo, k3_lo)[n], v + 2)
            if n >= 2 and not first:
                pe.wait_ge(max3_taken, v * 8 + n - 1)
            nc.tensor.matmul(ps[:, n % (4 if first else 2), :], q_a[:, b, h, t * P:(t + 1) * P], k_a[:, b, h, :],
                             start=True, stop=True).then_inc(max3_ps, 1)

        def pe3_turn(pe, u, b, h, first=False):
            pe.wait_ge(max3_taken, u * 8 + 4 * h + 4)
            if h == 1 and not first:
                pe.wait_ge(den3_log, u - 1)
            for t in range(KT):
                last = nc.tensor.transpose(ps[0:VW, 3 if h else 7, t * P:(t + 1) * P], neg_max3[:, b, h, t, :], ident[:, :])
            last.then_inc(max3_turned, 1)

        def pe3_scores(pe, u, b, uses, n, values=True, first=False):
            h, half = n // 2, n % 2
            if n == 0:
                pe.wait_ge(placed_b[b], uses * (4 * 16))
            if half == 0:
                pe.wait_ge(max3_in, u * 2 + h + 1)
            if n == 1 and values:
                pe.wait_ge(v3_ready, u + 2)
            if not (first and n < 2):
                pe.wait_ge(exp3_done, u * 4 + n - 1)
            for k in (2 * half, 2 * half + 1):
                dst = ps[:, 4 + k, :]
                nc.tensor.matmul(dst, k_a[:, b, h, k * P:(k + 1) * P], q_a[:, b, h, :], start=True, stop=False)
                last = nc.tensor.matmul(dst, k_b[:, b, h, k * P:(k + 1) * P], q_b[:, b, h, :], start=False, stop=True)
            last.then_inc(score3_ps, 1)

        def pe3_outputs(pe, u, b, k, first=False):
            if k == 0 and not first:
                pe.wait_ge(pair3_out, u)
            for h in range(2):
                if k % 2 == 0:
                    pe.wait_ge(exp3_done, u * 4 + 2 * h + k // 2 + 1)
                last = nc.tensor.matmul(ps[DW * h:DW * (h + 1), 2, :], v_pair[:, b, k, DW * h:DW * (h + 1)],
                                        probs[:, 0, h, k * T:(k + 1) * T], start=(k == 0), stop=(k == KT - 1))
            if k == KT - 1:
                last.then_inc(pv3_ps, 1)

        def pe3_denominators(pe, u, last=False):
            pe.wait_ge(sum3_lo, u + 1)
            if last:
                pe.wait_ge(den3_log, u)
            else:
                pe.wait_ge(max3_in, u * 2 + 4)
            for n, part in enumerate((sum_hi, sum_lo)):
                for h in range(2):
                    last_pass = nc.tensor.matmul(ps[DW * h:DW * (h + 1), 3, :], den_ones[:, :], part[:, h, :],
                                                 start=(n == 0), stop=(n == 1))
            last_pass.then_inc(den3_ps, 1)

        def pe3_body(pe, u, b, c_next, uses, index=2, last=False):
            if index == 0:
                pe.wait_ge(v3_ready, 1)
            if not last:
                pe3_values(pe, 1 - b)
            pe3_scores(pe, u, b, uses, 0, first=(index == 0))
            pe3_turn(pe, u, b, 1, first=(index < 2))
            pe3_scores(pe, u, b, uses, 1, values=not last, first=(index == 0))
            if last:
                pe3_join(pe, 0, 0)
            if c_next is not None:
                pe3_project(pe, u + 2, b, c_next, 0)
            if index > 0:
                pe3_denominators(pe, u - 1)
            if c_next is not None:
                pe3_project(pe, u + 2, b, c_next, 1)
            pe3_scores(pe, u, b, uses, 2)
            pe3_scores(pe, u, b, uses, 3)
            if last:
                for c in range(1, 4):
                    pe3_join(pe, 0, c)
            for n in range(2 * KT):
                if not last:
                    pe3_maxima(pe, u + 1, 1 - b, uses + b, n, projected=c_next is not None)
                if n == 5 and not last:
                    pe3_turn(pe, u + 1, 1 - b, 0)
                if n % 2 == 0:
                    pe3_outputs(pe, u, b, n // 2, first=(index == 0))
                if last and n < 3:
                    pe3_join(pe, 0, n + 4)

        def pe3_join(pe, b, c):
            if c == NC - 1:
                pe.wait_ge(pair3_out, NB * c + b + 1)
            last = nc.tensor.matmul(ps[:, 4 * b, :], w_o3[:, c, :], pair_out[:, NB * c + b, :], start=(c == 0), stop=(c == NC - 1))
            if c == NC - 1:
                last.then_inc(out3_ps, 1)

        def act3_weights(act, c, reuse=True):
            act.wait_ge(pair_loaded, c * 16 + 16)
            if reuse:
                act.wait_ge(v3_ps, c * 2)
            nc.scalar.mul(w_hi[:, :, :], w_pair[:, :, :], WSC).then_inc(w_hi_ready, 1)

        def act3_split(act, v, b, i):
            act.wait_ge((q3_ps, k3_ps)[i], v + 1)
            nc.scalar.mul((q_hi, k_hi)[i][:, b, :], ps[:, i, :], 1.0 / WSC).then_inc((q3_hi, k3_hi)[i], 1)

        def act3_max_in(act, u, b, h):
            act.wait_ge(max3_turned, u * 2 + h + 1)
            nc.scalar.mul(q_b[DW:96, b, h, :], ps[0:VW, 3 if h else 7, :], 1.0 / MAXC).then_inc(max3_in, 1)

        def act3_exp(act, u, b, n, first=False):
            h, half = n // 2, n % 2
            if n == 0 and not first:
                act.wait_ge(pv3_ps, u)
            if half == 0 and not first:
                act.wait_ge(pair3_sum, u * 2 + h - 1)
            act.wait_ge(score3_ps, u * 4 + n + 1)
            nc.scalar.activation(probs[:, 0, h, half * 2 * T:(half + 1) * 2 * T],
                                 ps[:, 4 + 2 * half:6 + 2 * half, :].rearrange("p n t -> p (n t)"), ACT.Exp,
                                 scale=DW ** -0.5).then_inc(exp3_done, 1)

        def act3_inverse(act, u, first=False):
            act.wait_ge(den3_ps, u + 1)
            if not first:
                act.wait_ge(pair3_out, u)
            nc.scalar.activation(inv3, ps[:, 3, :], ACT.Ln).then_inc(den3_log, 1)
            act.wait_ge(den3_log, u + 1)
            nc.scalar.activation(inv3, inv3, ACT.Exp, scale=-1.0).then_inc(den3_inv, 1)

        def act3_body(act, u, b, c_new=None, project=True, index=2, last=False):
            if c_new is not None:
                act3_weights(act, c_new)
            act3_exp(act, u, b, 0, index == 0)
            act3_max_in(act, u, b, 1)
            act3_exp(act, u, b, 1)
            if project:
                act3_split(act, u + 2, b, 0)
            if index > 0:
                act3_inverse(act, u - 1, index == 1)
            if project:
                act3_split(act, u + 2, b, 1)
            act3_exp(act, u, b, 2, index == 0)
            act3_exp(act, u, b, 3)
            if not last:
                act3_max_in(act, u + 1, 1 - b, 0)
            act.wait_ge(key3_sum, u * 2 + 2)
            if index > 0:
                act.wait_ge(den3_ps, u)
            nc.scalar.mul(sum_hi, key_sum, SUMC).then_inc(sum3_hi, 1)

        def dve3_weights(dve, c):
            dve.wait_ge(w_hi_ready, c + 1)
            nc.vector.scalar_tensor_tensor(out=w_lo[:, :, :], in0=w_pair[:, :, :], scalar=WSC, in1=w_hi[:, :, :],
                                           op0=ALU.mult, op1=ALU.subtract).then_inc(w_lo_ready, 1)

        def dve3_split(dve, v, b, i):
            hi, lo, hi_ready, lo_ready = ((q_hi, q_lo, q3_hi, q3_lo), (k_hi, k_lo, k3_hi, k3_lo))[i]
            dve.wait_ge(hi_ready, v + 1)
            nc.vector.scalar_tensor_tensor(out=lo[:, b, :], in0=ps[:, i, :], scalar=1.0 / WSC, in1=hi[:, b, :],
                                           op0=ALU.mult, op1=ALU.subtract).then_inc(lo_ready, 1)

        def dve3_values(dve, v, b, reuse):
            dve.wait_ge(v3_ps, v + 1)
            if reuse:
                dve.wait_ge(pv3_ps, v - 1)
            nc.vector.tensor_scalar(v_pair[:, b, :, :].rearrange("p k n -> p (k n)"), ps[:, 6, :], 1.0 / WSC, None,
                                    ALU.mult).then_inc(v3_ready, 1)

        def dve3_maxima(dve, v, b, n, reuse, first=False):
            h, t = n // KT, n % KT
            if t == 0 and reuse:
                dve.wait_ge(max3_turned, v * 2 - 3 + h)
            dve.wait_ge(max3_ps, v * 8 + n + 1)
            nc.vector.tensor_reduce(neg_max3[:, b, h, t, h:h + 1], ps[:, n % (4 if first else 2), :], AX_X, ALU.max,
                                    negate=True).then_inc(max3_taken, 1)

        def dve3_sum_lo(dve, u):
            dve.wait_ge(sum3_hi, u + 1)
            nc.vector.scalar_tensor_tensor(out=sum_lo[:, :, :], in0=key_sum, scalar=SUMC, in1=sum_hi,
                                           op0=ALU.mult, op1=ALU.subtract).then_inc(sum3_lo, 1)

        def dve3_divide(dve, u):
            dve.wait_ge(den3_inv, u + 1)
            nc.vector.tensor_tensor(out=pair_out[:, u, :], in0=ps[:, 2, :], in1=inv3, op=ALU.mult).then_inc(pair3_out, 1)

        def dve3_body(dve, u, b, c_new=None, project=True, index=2, last=False):
            if not last:
                dve3_values(dve, u + 1, 1 - b, index > 0)
            if c_new is not None:
                dve3_weights(dve, c_new)
            if index > 0:
                dve3_sum_lo(dve, u - 1)
            if project:
                dve3_split(dve, u + 2, b, 0)
            if index > 0:
                dve3_divide(dve, u - 1)
            if project:
                dve3_split(dve, u + 2, b, 1)
            if not last:
                for n in range(2 * KT):
                    dve3_maxima(dve, u + 1, 1 - b, n, index > 0)

        def pool3_body(pool, u, first=False):
            for h in range(2):
                pool.wait_ge(exp3_done, u * 4 + 2 * h + 2)
                nc.gpsimd.tensor_tensor(out=half_sum[:, h, :], in0=probs[:, 0, h, 0:2 * T], in1=probs[:, 0, h, 2 * T:4 * T],
                                        op=ALU.add).then_inc(pair3_sum, 1)
                pool.wait_ge(pair3_sum, u * 2 + h + 1)
                if h == 0 and not first:
                    pool.wait_ge(sum3_lo, u)
                nc.gpsimd.tensor_tensor(out=key_sum[:, h, :], in0=half_sum[:, h, 0:T], in1=half_sum[:, h, T:2 * T],
                                        op=ALU.add).then_inc(key3_sum, 1)

        def sp3_place(sp, v, b, reuse):
            sp.wait_ge(q3_lo, v + 1)
            if reuse:
                sp.wait_ge(score3_ps, v * 4 - 4)
            rows = [slice(DW * h, DW * (h + 1)) for h in range(2)]
            for h in range(2):
                sp.dma_start(q_a[0:DW, b, h, :], q_hi[rows[h], b, :]).then_inc(placed_a[b][h], 16)
                sp.dma_start(q_a[DW:P, b, h, :], q_lo[rows[h], b, :]).then_inc(placed_a[b][h], 16)
                if h == 0:
                    sp.wait_ge(k3_hi, v + 1)
                for half in (0, DW):
                    sp.dma_start(k_a[half:half + DW, b, h, :], k_hi[rows[h], b, :]).then_inc(placed_a[b][h], 16)
            sp.wait_ge(k3_lo, v + 1)
            for h in range(2):
                sp.dma_start(k_b[0:DW, b, h, :], k_lo[rows[h], b, :]).then_inc(placed_b[b], 16)
                sp.dma_start(q_b[0:DW, b, h, :], q_hi[rows[h], b, :]).then_inc(placed_b[b], 16)

        def attention3_sp(sp):
            def load_pair(c):
                sp.dma_start(w_pair[:, :, :], w_qkv3[c]).then_inc(pair_loaded, 16)

            load_pair(0)
            sp.wait_ge(w_lo_ready, 1)
            load_pair(1)
            sp3_place(sp, 0, 0, False)
            sp3_place(sp, 1, 1, False)
            with sp.Fori(1, NC - 1) as c:
                sp.wait_ge(w_lo_ready, c + 1)
                load_pair(c + 1)
                sp3_place(sp, c * 2, 0, True)
                sp3_place(sp, c * 2 + 1, 1, True)
            sp3_place(sp, 2 * NC - 2, 0, True)
            sp3_place(sp, 2 * NC - 1, 1, True)

        def attention3_pool(pool):
            for b in range(NB):
                pool.wait_ge(mlp2.stream, b + 1)
                nc.gpsimd.tensor_scalar(xb[:, b, :], xT[:, b, :], gate_b[:, 2, 0, b:b + 1], None, ALU.add).then_inc(biased3, 1)
            pool3_body(pool, 0, first=True)
            with pool.Fori(1, 2 * NC) as u:
                pool3_body(pool, u)

        def attention3_pe(pe):
            pe.wait_ge(const_made, N_CONST_MADE)
            pe.wait_ge(xm_lo_ready, 1)
            for i in range(2):
                pe3_project(pe, 0, 0, 0, i)
            pe.wait_ge(xm_lo_ready, 2)
            pe3_values(pe, 0)
            for i in range(2):
                pe.wait_ge((q3_lo, k3_lo)[i], 1)
                pe3_project(pe, 1, 1, 0, i)
            for n in range(2 * KT):
                pe3_maxima(pe, 0, 0, 1, n, first=True)
            pe3_turn(pe, 0, 0, 0)
            pe3_body(pe, 0, 0, 1, 1, index=0)
            pe3_body(pe, 1, 1, 1, 1, index=1)
            with pe.Fori(1, NC - 1) as c:
                pe3_body(pe, c * 2, 0, c + 1, c + 1)
                pe3_body(pe, c * 2 + 1, 1, c + 1, c + 1)
            pe3_body(pe, 2 * NC - 2, 0, None, NC)
            pe3_body(pe, 2 * NC - 1, 1, None, NC, last=True)
            pe3_join(pe, 0, NC - 1)
            for c in range(3):
                pe3_join(pe, 1, c)
            pe3_denominators(pe, 2 * NC - 1, last=True)
            norm3b.centre(pe, 0, stream3)
            pe3_join(pe, 1, 3)
            pe3_join(pe, 1, 4)
            norm3b.variance(pe, 0)
            for c in range(5, NC):
                pe3_join(pe, 1, c)
            mlp3.norm_up(pe, stream3)

        def attention3_act(act):
            for v in range(2):
                for i in range(2):
                    act3_split(act, v, v, i)
            act3_max_in(act, 0, 0, 0)
            act3_body(act, 0, 0, c_new=1, index=0)
            act3_body(act, 1, 1, index=1)
            with act.Fori(1, NC - 1) as c:
                act3_body(act, c * 2, 0, c_new=c + 1)
                act3_body(act, c * 2 + 1, 1)
            act3_body(act, 2 * NC - 2, 0, project=False)
            act3_body(act, 2 * NC - 1, 1, project=False, last=True)
            act3_inverse(act, 2 * NC - 1)
            norm3b.act_skewed(act)

        def attention3_dve(dve):
            for i in range(2):
                dve3_split(dve, 0, 0, i)
            dve3_values(dve, 0, 0, False)
            for i in range(2):
                dve3_split(dve, 1, 1, i)
            for n in range(2 * KT):
                dve3_maxima(dve, 0, 0, n, False, first=True)
            dve3_body(dve, 0, 0, c_new=1, index=0)
            dve3_body(dve, 1, 1, index=1)
            with dve.Fori(1, NC - 1) as c:
                dve3_body(dve, c * 2, 0, c_new=c + 1)
                dve3_body(dve, c * 2 + 1, 1)
            dve3_body(dve, 2 * NC - 2, 0, project=False)
            dve3_body(dve, 2 * NC - 1, 1, project=False, last=True)

            def join(b):
                dve.wait_ge(out3_ps, b + 1)
                dve.wait_ge(biased3, b + 1)
                nc.vector.scalar_tensor_tensor(out=xT[:, b, :], in0=ps[:, 4 * b, :], scalar=mods[:, 14, b:b + 1],
                                               in1=xb[:, b, :], op0=ALU.mult, op1=ALU.add).then_inc(stream3, 1)

            dve3_sum_lo(dve, 2 * NC - 1)
            join(0)
            dve3_divide(dve, 2 * NC - 1)
            norm3b.apply(dve, 0)
            join(1)
            norm3b.apply(dve, 1)

        out3_ps, biased3, stream3 = sem("out3_ps"), sem("biased3"), sem("stream3")
        norm3b = adaptive_norm(6, 2, 1)
        mlp3 = Mlp(2, norm3b, "L3b1")
        y_ps, y_ready, y_stored = sem("y_ps"), sem("y_ready"), sem("y_stored")

        def output_pe(pe, b):
            pe.wait_ge(mlp3.stream, b + 1)
            for k in range(KT):
                last = nc.tensor.transpose(ps[:, 4 * b + 1, k * P:(k + 1) * P], xT[:, b, k * P:(k + 1) * P], ident[:, :])
            last.then_inc(y_ps, 1)

        with nc.Block() as block:
            @block.sync
            def _(sp):
                setup_sp(sp)
                sp_att0(sp)
                sp_att2(sp)
                attention3_sp(sp)
                for b in range(NB):
                    sp.wait_ge(y_ready, b + 1)
                    sp.dma_start(out[b].rearrange("(k p) d -> p k d", p=P),
                                 xc[:, b, :].rearrange("p (k d) -> p k d", d=D)).then_inc(y_stored, 16)
                sp.wait_ge(y_stored, 16 * NB)

            @block.gpsimd
            def _(pool):
                setup_pool(pool)
                pool_att0(pool)
                pool.wait_ge(mods_done, N_MODS_DONE)
                join0.pool(pool)
                mlp0.pool(pool)
                pool_att2(pool)
                join2.pool(pool)
                mlp2.pool(pool)
                attention3_pool(pool)
                mlp3.pool(pool)

            @block.tensor
            def _(pe):
                setup_pe(pe)
                norm0a.pe(pe, xT_ready)
                mods0_pe(pe)
                proj0.pe(pe)
                mods_pe(pe)
                pe.wait_ge(mods_done, 3)
                pe_att0(pe, lambda pe: join0.pick(pe, 0))
                pe.wait_ge(w_bulk, 16 * len(weights))
                join0.pe(pe, mlp0)
                additive_pe(pe)
                norm1.pe(pe, stream1)
                for b in range(NB):
                    pe.wait_ge(ln_out, norm1.count(b))
                    norm2a.centre(pe, b)
                for b in range(NB):
                    norm2a.variance(pe, b)
                proj2.pe(pe)
                pe_att2(pe, lambda pe: join2.pick(pe, 0))
                join2.pe(pe, mlp2)
                norm3a.pe(pe, mlp2.stream)
                attention3_pe(pe)
                for b in range(NB):
                    for m in range(MLP):
                        mlp3.down(pe, b, m)
                        if (b, m) == (1, 1):
                            output_pe(pe, 0)
                output_pe(pe, 1)

            @block.scalar
            def _(act):
                setup_act(act)
                norm0a.act(act)
                proj0.act(act)
                act_att0(act, lambda act: join0.act(act, 0))
                join0.act(act, 1)
                norm0b.act_skewed(act)
                mlp0.act(act)
                additive_act(act)
                norm1.act(act)
                norm2a.act(act)
                proj2.act(act)
                act_att2(act, lambda act: join2.act(act, 0))
                act3_weights(act, 0, reuse=False)
                join2.act(act, 1)
                norm2b.act_skewed(act)
                mlp2.act(act)
                norm3a.act(act)
                for b in range(NB):
                    act.wait_ge(ln_out, norm3a.count(b))
                    nc.scalar.copy(xm_hi[:, b, :], xm[:, b, :]).then_inc(xm_hi_ready, 1)
                attention3_act(act)
                mlp3.act(act)
                for b in range(NB):
                    act.wait_ge(y_ps, b + 1)
                    nc.scalar.copy(xc[:, b, :], ps[:, 4 * b + 1, :]).then_inc(y_ready, 1)

            @block.vector
            def _(dve):
                setup_dve(dve)
                norm0a.dve(dve, beside=mods0_dve)
                proj0.dve(dve)
                mods_dve(dve)
                dve_att0(dve)
                vectors_dve(dve)
                join0.dve(dve)
                norm0b.dve(dve)
                mlp0.dve(dve, behind=running_sum)
                additive_dve(dve)
                norm1.dve(dve)
                norm2a.dve(dve)
                proj2.dve(dve)
                dve_att2(dve)
                dve3_weights(dve, 0)
                join2.dve(dve)
                norm2b.dve(dve)
                mlp2.dve(dve)
                norm3a.dve(dve)
                for b in range(NB):
                    dve.wait_ge(xm_hi_ready, b + 1)
                    dve.wait_ge(ln_out, norm3a.count(b))
                    nc.vector.tensor_tensor(out=xm_lo[:, b, :], in0=xm[:, b, :], in1=xm_hi[:, b, :],
                                            op=ALU.subtract).then_inc(xm_lo_ready, 1)
                attention3_dve(dve)
                mlp3.dve(dve)


def kernel(**inputs):
    import numpy as np
    import concourse.bacc as bacc
    from concourse.bass_utils import run_bass_kernel_spmd

    nc = bacc.Bacc("TRN2", target_bir_lowering=False, num_devices=1)
    arrays, aps = {}, {}
    for name, value in inputs.items():
        value = np.ascontiguousarray(value)
        arrays[f"in_{name}"] = value
        aps[name] = nc.dram_tensor(f"in_{name}", value.shape, mybir.dt.from_np(value.dtype), kind="ExternalInput").ap()
    out = nc.dram_tensor("out_0", (NB, T, D), F32, kind="ExternalOutput").ap()
    build_program(nc, aps, out)
    result = run_bass_kernel_spmd(nc, [arrays], core_ids=[0])
    return result.results[0]["out_0"]
```
